# Optimizing a Trainium2 kernel written in Bass

```python
import numpy as np
import jax
import jax.numpy as jnp

def _softmax(x, axis=-1):
    return jax.nn.softmax(x, axis=axis)

def _gelu(x):
    return jax.nn.gelu(x, approximate=True)

def _silu(x):
    return jax.nn.silu(x)

def _sigmoid(x):
    return jax.nn.sigmoid(x)

def _layernorm(x, axis=-1, eps=1e-05):
    m = jnp.mean(x, axis=axis, keepdims=True)
    v = jnp.var(x, axis=axis, keepdims=True)
    return (x - m) / jnp.sqrt(v + eps)

def _scatter_add(tgt, idx, src, axis=0):
    return tgt.at[idx].add(src)

def _segment_sum(src, seg, n):
    return jax.ops.segment_sum(src, seg, n)
kernel_name = 'mk_adj_preln_d2_adj_r2_7d0e90'

def setup_inputs(seed: int=0):
    np.random.seed(seed)
    _w = jnp.asarray

    def _rec_inputs():
        import jax
        import jax.numpy as jnp
        _gk = jax.random.key(seed)
        x = 7.22e-05 + 1 * jax.random.normal(jax.random.fold_in(_gk, 1), (16, 512, 128), jnp.float32)
        _a = jax.random.bernoulli(jax.random.fold_in(_gk, 2), 0.03125, (512, 512))
        _a = jnp.logical_or(_a, jnp.swapaxes(_a, -1, -2))
        _a = jnp.logical_or(_a, jnp.eye(512, dtype=bool))
        _af = _a.astype(jnp.float32)
        _af = _af * jax.random.uniform(jax.random.fold_in(_gk, 3), (512, 512), jnp.float32, 0.05, 0.000976562)
        adj = _af
        return (x, adj)
    x, adj = _rec_inputs()

    def _L0_gnn_setup():
        import jax, jax.numpy as jnp
        import numpy as np
        N_STEPS = 8
        SPATIAL_SCALE = 1.0
        key = jax.random.key(seed)
        ks = jax.random.split(key, 6)
        B, N, D = (32, 512, 128)
        x = jax.random.normal(ks[0], (B, N, D), dtype=jnp.float32)
        adj_mx = jax.random.uniform(ks[1], (N, N), dtype=jnp.float32) / N
        alpha_train = jnp.ones((N,), dtype=jnp.float32)
        w = jnp.eye(D, dtype=jnp.float32) + 0.01 * jax.random.normal(ks[2], (D, D), dtype=jnp.float32)
        d = jax.random.uniform(ks[3], (D,), dtype=jnp.float32)
        fc_in_w = jax.random.normal(ks[4], (D, D), dtype=jnp.float32) * (1.0 / np.sqrt(D))
        fc_in_b = jnp.zeros((D,), dtype=jnp.float32)
        return {'x': x, 'adj_mx': adj_mx, 'alpha_train': alpha_train, 'w': w, 'd': d, 'fc_in_w': fc_in_w, 'fc_in_b': fc_in_b, 'vt': 0}
    _L0_gnn_all = _L0_gnn_setup()
    _L0_gnn_in = {k: v for k, v in _L0_gnn_all.items() if k in ('alpha_train', 'w', 'd', 'fc_in_w', 'fc_in_b')}
    del _L0_gnn_all

    def _L1_gnn_setup():
        import jax, jax.numpy as jnp
        import numpy as np
        EPS_LN = 1e-05

        def _layernorm(x, g, b):
            mu = x.mean(-1, keepdims=True)
            var = ((x - mu) ** 2).mean(-1, keepdims=True)
            return (x - mu) / jnp.sqrt(var + EPS_LN) * g + b
        key = jax.random.key(seed)
        B, N, D, H = (4, 1024, 128, 4)
        hid = int(D * 2.0)
        ks = jax.random.split(key, 12)
        x = jax.random.normal(ks[0], (B, N, D), jnp.float32)
        Au = jax.random.uniform(ks[1], (N, N)) < 0.004
        A = jnp.logical_or(Au, Au.T)
        A = A.at[jnp.arange(N), jnp.arange(N)].set(False)
        Af = A.astype(jnp.float32)
        deg = Af.sum(axis=1)
        L = jnp.diag(deg) - Af
        adjacency = Af + jnp.eye(N, dtype=jnp.float32)
        s = lambda k, sh, f: jax.random.normal(k, sh, jnp.float32) * f
        sc = 1.0 / np.sqrt(D)
        Wc = s(ks[2], (D, D), sc)
        bc = jnp.zeros((D,), jnp.float32)
        Wq = s(ks[3], (D, D), sc)
        Wk = s(ks[4], (D, D), sc)
        Wv = s(ks[5], (D, D), sc)
        Wo = s(ks[6], (D, D), sc)
        bo = jnp.zeros((D,), jnp.float32)
        W1 = s(ks[7], (D, hid), sc)
        b1 = jnp.zeros((hid,), jnp.float32)
        W2 = s(ks[8], (hid, D), 1.0 / np.sqrt(hid))
        b2 = jnp.zeros((D,), jnp.float32)
        g1 = jnp.ones((D,), jnp.float32)
        be1 = jnp.zeros((D,), jnp.float32)
        g2 = jnp.ones((D,), jnp.float32)
        be2 = jnp.zeros((D,), jnp.float32)
        g3 = jnp.ones((D,), jnp.float32)
        be3 = jnp.zeros((D,), jnp.float32)
        return dict(x=x, L=L, adjacency=adjacency, Wc=Wc, bc=bc, g1=g1, be1=be1, Wq=Wq, Wk=Wk, Wv=Wv, Wo=Wo, bo=bo, g2=g2, be2=be2, W1=W1, b1=b1, W2=W2, b2=b2, g3=g3, be3=be3)
    _L1_gnn_all = _L1_gnn_setup()
    _L1_gnn_in = {k: v for k, v in _L1_gnn_all.items() if k in ('Wc', 'bc', 'g1', 'be1', 'Wq', 'Wk', 'Wv', 'Wo', 'bo', 'g2', 'be2', 'W1', 'b1', 'W2', 'b2', 'g3', 'be3')}
    del _L1_gnn_all
    return {'x': x, 'adj': adj, 'L0_gnn_alpha_train': _L0_gnn_in['alpha_train'], 'L0_gnn_w': _L0_gnn_in['w'], 'L0_gnn_d': _L0_gnn_in['d'], 'L0_gnn_fc_in_w': _L0_gnn_in['fc_in_w'], 'L0_gnn_fc_in_b': _L0_gnn_in['fc_in_b'], 'L1_gnn_Wc': _L1_gnn_in['Wc'], 'L1_gnn_bc': _L1_gnn_in['bc'], 'L1_gnn_g1': _L1_gnn_in['g1'], 'L1_gnn_be1': _L1_gnn_in['be1'], 'L1_gnn_Wq': _L1_gnn_in['Wq'], 'L1_gnn_Wk': _L1_gnn_in['Wk'], 'L1_gnn_Wv': _L1_gnn_in['Wv'], 'L1_gnn_Wo': _L1_gnn_in['Wo'], 'L1_gnn_bo': _L1_gnn_in['bo'], 'L1_gnn_g2': _L1_gnn_in['g2'], 'L1_gnn_be2': _L1_gnn_in['be2'], 'L1_gnn_W1': _L1_gnn_in['W1'], 'L1_gnn_b1': _L1_gnn_in['b1'], 'L1_gnn_W2': _L1_gnn_in['W2'], 'L1_gnn_b2': _L1_gnn_in['b2'], 'L1_gnn_g3': _L1_gnn_in['g3'], 'L1_gnn_be3': _L1_gnn_in['be3']}

def reference(x, adj, L0_gnn_alpha_train, L0_gnn_w, L0_gnn_d, L0_gnn_fc_in_w, L0_gnn_fc_in_b, L1_gnn_Wc, L1_gnn_bc, L1_gnn_g1, L1_gnn_be1, L1_gnn_Wq, L1_gnn_Wk, L1_gnn_Wv, L1_gnn_Wo, L1_gnn_bo, L1_gnn_g2, L1_gnn_be2, L1_gnn_W1, L1_gnn_b1, L1_gnn_W2, L1_gnn_b2, L1_gnn_g3, L1_gnn_be3):
    import jax
    import jax.numpy as jnp

    def _L0_gnn_ref(x, adj_mx, alpha_train, w, d, fc_in_w, fc_in_b, vt):
        import jax, jax.numpy as jnp
        import numpy as np
        N_STEPS = 8
        SPATIAL_SCALE = 1.0
        x0 = jax.lax.stop_gradient(x)
        h = jnp.einsum('bnd,ed->bne', x, fc_in_w) + fc_in_b
        alph = jax.nn.sigmoid(alpha_train)[:, None]
        d_clamped = jnp.clip(d, 0.0, 1.0)
        w_eff = w * d_clamped @ w.T
        dt = jnp.float32(SPATIAL_SCALE / N_STEPS)

        def euler_step(h, _):
            ax = jnp.einsum('nm,bmd->bnd', adj_mx, h)
            f = alph * 0.5 * (ax - h) + h @ w_eff - h + x0
            return (h + dt * f, None)
        h, _ = jax.lax.scan(euler_step, h, None, length=N_STEPS)
        return h

    def _L1_gnn_ref(x, L, adjacency, Wc, bc, g1, be1, Wq, Wk, Wv, Wo, bo, g2, be2, W1, b1, W2, b2, g3, be3):
        import jax, jax.numpy as jnp
        import numpy as np
        EPS_LN = 1e-05

        def _layernorm(x, g, b):
            mu = x.mean(-1, keepdims=True)
            var = ((x - mu) ** 2).mean(-1, keepdims=True)
            return (x - mu) / jnp.sqrt(var + EPS_LN) * g + b
        B, N, D = x.shape
        H = 4
        hd = D // H
        eig = jnp.linalg.eigvalsh(L)
        lam_max = eig[-1] + 1e-08
        L_norm = 2.0 * L / lam_max - jnp.eye(N, dtype=L.dtype)
        xp = jnp.einsum('mn,bnf->bmf', L_norm, x)
        h = xp @ Wc + bc
        h = _layernorm(h, g1, be1)
        h = jax.nn.relu(h)
        x1 = h + x
        q = (x1 @ Wq).reshape(B, N, H, hd).transpose(0, 2, 1, 3)
        k = (x1 @ Wk).reshape(B, N, H, hd).transpose(0, 2, 1, 3)
        v = (x1 @ Wv).reshape(B, N, H, hd).transpose(0, 2, 1, 3)
        scores = jnp.einsum('bhnd,bhmd->bhnm', q, k) / np.sqrt(hd).astype(np.float32)
        scores = jnp.where(adjacency[None, None] > 0, scores, jnp.float32(-1000000000.0))
        attn = jax.nn.softmax(scores, axis=-1)
        o = jnp.einsum('bhnm,bhmd->bhnd', attn, v)
        o = o.transpose(0, 2, 1, 3).reshape(B, N, D)
        o = o @ Wo + bo
        x2 = _layernorm(x1 + o, g2, be2)
        m = jax.nn.gelu(x2 @ W1 + b1, approximate=False) @ W2 + b2
        return _layernorm(x2 + m, g3, be3)
    h = jnp.maximum(_layernorm(x, axis=-1), 0.0)
    x = x + _L0_gnn_ref(h, adj, L0_gnn_alpha_train, L0_gnn_w, L0_gnn_d, L0_gnn_fc_in_w, L0_gnn_fc_in_b, 0)
    h = jnp.maximum(_layernorm(x, axis=-1), 0.0)
    x = x + _L1_gnn_ref(h, adj, adj, L1_gnn_Wc, L1_gnn_bc, L1_gnn_g1, L1_gnn_be1, L1_gnn_Wq, L1_gnn_Wk, L1_gnn_Wv, L1_gnn_Wo, L1_gnn_bo, L1_gnn_g2, L1_gnn_be2, L1_gnn_W1, L1_gnn_b1, L1_gnn_W2, L1_gnn_b2, L1_gnn_g3, L1_gnn_be3)
    return x

_drawn_inputs = setup_inputs


def setup_inputs(seed=0):
    import zlib

    import numpy as np

    out = dict(_drawn_inputs(seed))
    spreads = {'L0_gnn_alpha_train': (1.0, 0.6),
     'L0_gnn_fc_in_b': (0.0, 0.1),
     'L1_gnn_bc': (0.0, 0.1),
     'L1_gnn_g1': (1.0, 0.2),
     'L1_gnn_be1': (0.0, 0.1),
     'L1_gnn_bo': (0.0, 0.1),
     'L1_gnn_g2': (1.0, 0.2),
     'L1_gnn_be2': (0.0, 0.1),
     'L1_gnn_b1': (0.0, 0.318),
     'L1_gnn_b2': (0.0, 0.1),
     'L1_gnn_g3': (1.0, 0.2),
     'L1_gnn_be3': (0.0, 0.1)}
    factors = {}
    for name, (base, spread) in spreads.items():
        noise = np.random.default_rng([zlib.crc32(name.encode()), seed]).standard_normal(out[name].shape)
        drawn = base * np.exp(spread * noise) if base else spread * noise
        out[name] = jnp.asarray(drawn.astype(out[name].dtype))
    for name, factor in factors.items():
        out[name] = (out[name] * factor).astype(out[name].dtype)
    return out
```

```python
from contextlib import ExitStack
from math import comb

import concourse.bass as bass
from concourse import mybir

F32 = mybir.dt.float32
F32R = mybir.dt.float32r
BF16 = mybir.dt.bfloat16
ALU = mybir.AluOpType
ACT = mybir.ActivationFunctionType
AX = mybir.AxisListType

BATCH, N, D = 16, 512, 128
P = 128
NT = N // P
STEPS = 8
DT = 1.0 / STEPS
HEADS = 4
HD = D // HEADS
HID = 2 * D
HT = HID // P
EPS = 1e-5
GROUP = 3
MASKED = 1e30
TINY = 1e-15
UNITS = NT * HEADS
assert (STEPS + 1) == GROUP * GROUP and BATCH % 2 == 0


def at_least(eng, semaphore, value):
    if isinstance(value, int) and value <= 0:
        return
    eng.wait_ge(semaphore, value)


def rounds(eng, body, first_full, after_full, last):
    for r in range(first_full):
        body(r, r % 2, r // 2)
    with eng.Fori(first_full // 2, after_full // 2) as half:
        body(2 * half, 0, half)
        body(2 * half + 1, 1, half)
    for r in range(after_full, last):
        body(r, r % 2, r // 2)


def within(r, low, high):
    return low <= r <= high if isinstance(r, int) else True


def two_layers(nc, x, adj, alpha, w, d, fc_w, fc_b, Wc, bc, g1, be1, Wq, Wk, Wv, Wo, bo, g2, be2, W1, b1, W2, b2,
               g3, be3, out):
    x_dram = x.rearrange("b (t p) d -> p b t d", p=P)
    out_dram = out.rearrange("b (t p) d -> p b t d", p=P)

    with ExitStack() as whole:
        def tensor(ctx, name, shape, dt=F32):
            return ctx.enter_context(nc.sbuf_tensor(name, shape, dt))

        def sem(name):
            return whole.enter_context(nc.semaphore(name))

        psum = [whole.enter_context(nc.psum_tensor(f"bank{i}", [P, N], F32)) for i in range(8)]

        waited = (sem("dve_waited"), sem("pool_waited"))

        y = tensor(whole, "y", [P, BATCH * N])
        adjT = tensor(whole, "adjT", [P, NT, N])
        mask = tensor(whole, "mask", [P, NT, N], BF16)
        ident = tensor(whole, "ident", [P, P])
        ones = tensor(whole, "ones", [P, P])
        exponent = tensor(whole, "exponent", [P, NT])
        two_over_lam = tensor(whole, "two_over_lam", [P, 1])

        layer0(nc, whole, tensor, sem, psum, x_dram, adj, alpha, w, d, fc_w, fc_b,
               y, adjT, mask, ident, ones, exponent, two_over_lam, waited)
        layer1(nc, whole, tensor, sem, psum, Wc, bc, g1, be1, Wq, Wk, Wv, Wo, bo, g2, be2, W1, b1, W2, b2, g3, be3,
               out_dram, y, adjT, mask, ident, ones, exponent, two_over_lam, waited)


def layer0(nc, whole, tensor, sem, psum, x_dram, adj, alpha, w, d, fc_w, fc_b,
           y, adjT, mask, ident, ones, exponent, two_over_lam, waited):
    dve_waited, pool_waited = waited
    with ExitStack() as ctx:
        def sb(name, shape, dt=F32):
            return tensor(ctx, name, shape, dt)

        A = sb("A", [P, NT, N])
        alpha_in = sb("alpha_in", [P, NT])
        w_in = sb("w_in", [P, D])
        d_in = sb("d_in", [P, 1])
        fc_in = sb("fc_in", [P, D])
        b_in = sb("b_in", [P, 1])
        Pn = sb("Pn", [P, NT, N])
        PT = sb("PT", [P, NT, N])
        P2T = sb("P2T", [P, NT, N])
        P3T = sb("P3T", [P, NT, N])
        a_exp = sb("a_exp", [P, NT])
        a_one = sb("a_one", [P, NT])
        a_sig = sb("a_sig", [P, NT])
        edge_scale = sb("edge_scale", [P, NT])
        self_scale = sb("self_scale", [P, NT])
        wT = sb("wT", [P, D])
        d_clip = sb("d_clip", [P, 1])
        d_dt = sb("d_dt", [P, 1])
        dwT = sb("dwT", [P, D])
        powers = sb("powers", [P, STEPS + 1, D + 1])
        W = powers[:, 1, 0:D]
        B = sb("B", [P, GROUP, GROUP, D])
        U = sb("U", [P, NT, STEPS + 1])
        beta = sb("beta", [P, STEPS + 1])
        U_rows = sb("U_rows", [STEPS + 1, N])
        beta_rows = sb("beta_rows", [STEPS + 1, D])
        bias = sb("bias", [P, NT, D])
        S = sb("S", [P, NT, N])
        Sq = [sb(f"Sq{i}", [P, NT, N], F32R) for i in range(2)]
        row_sum = sb("row_sum", [P, 1])
        shift = sb("shift", [P, 1])
        diagonal = sb("diagonal", [P, NT, D], BF16)
        trace_part = sb("trace_part", [P, 1])
        trace = sb("trace", [P, 1])
        trace_inv = sb("trace_inv", [P, 1])
        trace_inv2 = sb("trace_inv2", [P, 1])
        v = sb("v", [P, NT])
        Sv = sb("Sv", [P, NT])
        scratch4 = sb("scratch4", [P, NT])
        quotient = sb("quotient", [P, 2])
        quotient_all = sb("quotient_all", [P, 2])
        den_inv = sb("den_inv", [P, 1])
        lam = sb("lam", [P, 1])
        lam_inv = sb("lam_inv", [P, 1])
        x_in = [sb(f"x_in{i}", [P, NT, D]) for i in range(2)]
        stats = sb("stats", [P, NT, 6])
        mv = [sb(f"mv{i}", [P, NT, 2]) for i in range(2)]
        var_eps = [sb(f"var_eps{i}", [P, NT]) for i in range(2)]
        rstd = [sb(f"rstd{i}", [P, NT]) for i in range(2)]
        mean_rstd = [sb(f"mean_rstd{i}", [P, NT]) for i in range(2)]
        shift_ln = [sb(f"shift_ln{i}", [P, NT]) for i in range(2)]
        x0 = [sb(f"x0_{i}", [P, NT, D]) for i in range(2)]
        x_bias = [sb(f"x_bias{i}", [P, NT, D]) for i in range(2)]
        T = [[sb(f"T{m}_{i}", [P, N]) for m in range(GROUP)] for i in range(2)]
        C2 = sb("C2", [P, NT, D])
        Y1 = sb("Y1", [P, NT, D])

        loaded = sem("adj_loaded")
        small_loaded = sem("small_loaded")
        x_loaded = [sem(f"x_loaded{i}") for i in range(2)]
        consts_set = sem("consts_set")
        alpha_exp = sem("alpha_exp")
        dve_setup = sem("dve_setup")
        ident_ready = sem("ident_ready")
        P_ready = sem("P_ready")
        PT_psum = sem("PT_psum")
        PT_ready = sem("PT_ready")
        adjT_psum = sem("adjT_psum")
        adjT_ready = sem("adjT_ready")
        wT_psum = sem("wT_psum")
        wT_ready = sem("wT_ready")
        weff_psum = sem("weff_psum")
        power_psum = sem("power_psum")
        power_ready = sem("power_ready")
        FW_psum = sem("FW_psum")
        B_step = sem("B_step")
        P2_psum = sem("P2_psum")
        P2_ready = sem("P2_ready")
        P3_psum = sem("P3_psum")
        P3_ready = sem("P3_ready")
        U_psum = sem("U_psum")
        U_ready = sem("U_ready")
        beta_ready = sem("beta_ready")
        rows_psum = sem("rows_psum")
        rows_ready = sem("rows_ready")
        bias_psum = sem("bias_psum")
        bias_ready = sem("bias_ready")
        S_ready = sem("S_ready")
        sum_psum = sem("sum_psum")
        S0_ready = sem("S0_ready")
        trace_part_ready = sem("trace_part_ready")
        trace_psum = sem("trace_psum")
        trace_step = sem("trace_step")
        square_psum = sem("square_psum")
        square_ready = sem("square_ready")
        v_ready = sem("v_ready")
        Sv_psum = sem("Sv_psum")
        Sv_step = sem("Sv_step")
        quotient_psum = sem("quotient_psum")
        lam_step = sem("lam_step")
        stats_ready = sem("stats_ready")
        mv_ready = sem("mv_ready")
        ln_pool = sem("ln_pool")
        x0_ready = sem("x0_ready")
        x_bias_ready = sem("x_bias_ready")
        T_psum = [sem(f"T{m}_psum") for m in range(GROUP)]
        T_ready = [sem(f"T{m}_ready") for m in range(GROUP)]
        C_psum = sem("C_psum")
        C2_ready = sem("C2_ready")
        Y1_psum = sem("Y1_psum")
        Y1_ready = sem("Y1_ready")
        Y0_psum = sem("Y0_psum")
        y_ready = sem("y_ready")

        SQ_BANK = psum[7]
        ident_tiles = ident[:, :].unsqueeze(1).broadcast_to([P, NT, D])
        n_B = sum(STEPS - j for j in range(STEPS))

        def diagonal_of(tile):
            a = tile[:, :, 0:D]
            step = list(map(list, a.ap))
            step[1][0] += D
            return bass.AP(tensor=a.tensor, offset=a.offset, ap=step)

        with nc.Block() as block:

            @block.sync
            def _(sp):
                adj_tiles = adj.rearrange("(t p) m -> p t m", p=P)
                for t in range(NT):
                    sp.dma_start(A[:, t, :], adj_tiles[:, t, :]).then_inc(loaded, 16)
                sp.dma_start(alpha_in[:, :], alpha.rearrange("(t p) -> p t", p=P),
                             allow_slow_non_contiguous=True).then_inc(small_loaded, 16)
                sp.dma_start(w_in[:, :], w).then_inc(small_loaded, 16)
                sp.dma_start(fc_in[:, :], fc_w).then_inc(small_loaded, 16)
                sp.dma_start(d_in[:, :], d.rearrange("(p o) -> p o", o=1)).then_inc(small_loaded, 16)
                sp.dma_start(b_in[:, :], fc_b.rearrange("(p o) -> p o", o=1)).then_inc(small_loaded, 16)

                def load_x(b, s, half):
                    at_least(sp, x0_ready, b - 1)
                    at_least(sp, x_bias_ready, b - 1)
                    sp.dma_start(x_in[s][:, :, :], x_dram[:, bass.ds(b, 1), :, :].rearrange("p b t d -> p (b t) d")
                                 ).then_inc(x_loaded[s], 16)
                rounds(sp, load_x, 2, BATCH, BATCH)

            @block.gpsimd
            def _(pool):
                pool.memset(ident[:, :], 0.0).then_inc(consts_set, 1)
                pool.memset(ones[:, :], 1.0).then_inc(consts_set, 1)
                pool.memset(exponent[:, :], -0.5).then_inc(consts_set, 1)
                pool.wait_ge(consts_set, 1)
                pool.affine_select(out=ident[:, :], in_=ident[:, :], compare_op=ALU.not_equal, fill=1.0, base=0,
                                   pattern=[[-1, P]], channel_multiplier=1).then_inc(ident_ready, 1)

                def ln_and_residual(b, s, half):
                    pool.wait_ge(mv_ready, b + 1)
                    at_least(pool, x0_ready, b - 1)
                    pool.sem_inc(pool_waited, 1)
                    pool.tensor_scalar(var_eps[s][:, :], mv[s][:, :, 1], EPS, None, ALU.add).then_inc(ln_pool, 1)
                    pool.wait_ge(consts_set, 3)
                    pool.wait_ge(ln_pool, 4 * b + 1)
                    pool.tensor_tensor(out=rstd[s][:, :], in0=var_eps[s][:, :], in1=exponent[:, :],
                                       op=ALU.pow).then_inc(ln_pool, 1)
                    pool.wait_ge(ln_pool, 4 * b + 2)
                    pool.tensor_tensor(out=mean_rstd[s][:, :], in0=mv[s][:, :, 0], in1=rstd[s][:, :],
                                       op=ALU.mult).then_inc(ln_pool, 1)
                    pool.wait_ge(ln_pool, 4 * b + 3)
                    pool.sem_inc(pool_waited, 1)
                    pool.tensor_scalar(shift_ln[s][:, :], mean_rstd[s][:, :], -1.0, None,
                                       ALU.mult).then_inc(ln_pool, 1)
                    pool.wait_ge(bias_ready, 1)
                    at_least(pool, y_ready, NT * (b - 1))
                    pool.tensor_tensor(out=x_bias[s][:, :, :], in0=x_in[s][:, :, :], in1=bias[:, :, :],
                                       op=ALU.add).then_inc(x_bias_ready, 1)
                rounds(pool, ln_and_residual, 2, BATCH, BATCH)

            @block.tensor
            def _(pe):
                pe.wait_ge(ident_ready, 1)
                pe.wait_ge(loaded, 16 * NT)
                for mt in range(NT):
                    for nt in range(NT):
                        last = pe.transpose(psum[mt][:, nt * P:(nt + 1) * P], A[:, nt, mt * P:(mt + 1) * P],
                                            ident[:, :])
                    last.then_inc(adjT_psum, 1)
                pe.wait_ge(small_loaded, 16 * 5)
                pe.transpose(psum[4][:, 0:D], w_in[:, :], ident[:, :]).then_inc(wT_psum, 1)
                pe.wait_ge(wT_ready, 2)
                pe.matmul(psum[5][:, 0:D], wT[:, :], dwT[:, :], start=True, stop=True).then_inc(weff_psum, 1)
                pe.wait_ge(P_ready, 2 * NT)
                for mt in range(NT):
                    pe.wait_ge(adjT_ready, mt + 1)
                    for nt in range(NT):
                        last = pe.transpose(psum[mt][:, nt * P:(nt + 1) * P], Pn[:, nt, mt * P:(mt + 1) * P],
                                            ident[:, :])
                    last.then_inc(PT_psum, 1)
                for k in range(1, STEPS + 1):
                    pe.wait_ge(power_ready, k)
                    pe.matmul(psum[5][:, 0:D + 1], W, powers[:, k - 1, :], start=True,
                              stop=True).then_inc(power_psum, 1)
                pe.wait_ge(PT_ready, NT)
                for mt in range(NT):
                    for k in range(NT):
                        last = pe.matmul(psum[mt][:, :], Pn[:, k, mt * P:(mt + 1) * P], PT[:, k, :],
                                         start=k == 0, stop=k == NT - 1)
                    last.then_inc(P2_psum, 1)
                pe.wait_ge(power_ready, STEPS + 1)
                for k in range(STEPS + 1):
                    last = pe.matmul(psum[4 + k // NT][:, k % NT * D:(k % NT + 1) * D], fc_in[:, :],
                                     powers[:, k, 0:D], start=True, stop=True)
                last.then_inc(FW_psum, 1)
                pe.wait_ge(P2_ready, NT)
                for mt in range(NT):
                    for k in range(NT):
                        last = pe.matmul(psum[mt][:, :], Pn[:, k, mt * P:(mt + 1) * P], P2T[:, k, :],
                                         start=k == 0, stop=k == NT - 1)
                    last.then_inc(P3_psum, 1)
                pe.wait_ge(S_ready, 2)
                pe.matmul(SQ_BANK[:, 0:1], ones[:, :], row_sum[:, :], start=True, stop=True).then_inc(sum_psum, 1)
                pe.wait_ge(P3_ready, NT)
                for g in range(GROUP):
                    pe.wait_ge(U_ready, g + 1)
                    for nt in range(NT):
                        if g == 0:
                            for j, op in enumerate((PT, P2T, P3T)):
                                for k in range(NT):
                                    last = pe.matmul(psum[0][:, 4 * nt + j:4 * nt + j + 1],
                                                     op[:, k, nt * P:(nt + 1) * P], U[:, k, 0:1],
                                                     start=k == 0, stop=k == NT - 1)
                        else:
                            n_cols = 3 if g == 1 else 2
                            for k in range(NT):
                                last = pe.matmul(psum[0][:, 4 * nt:4 * nt + n_cols],
                                                 P3T[:, k, nt * P:(nt + 1) * P],
                                                 U[:, k, 3 * g - 2:3 * g - 2 + n_cols],
                                                 start=k == 0, stop=k == NT - 1)
                    last.then_inc(U_psum, 1)
                pe.wait_ge(U_ready, GROUP + 1)
                pe.wait_ge(beta_ready, STEPS + 1)
                for nt in range(NT):
                    pe.transpose(psum[1][0:STEPS + 1, nt * P:(nt + 1) * P], U[:, nt, :], ident[:, :])
                pe.transpose(psum[2][0:STEPS + 1, 0:D], beta[:, :], ident[:, :]).then_inc(rows_psum, 1)
                pe.wait_ge(rows_ready, 2)
                for nt in range(NT):
                    last = pe.matmul(psum[3][:, nt * D:(nt + 1) * D], U_rows[:, nt * P:(nt + 1) * P],
                                     beta_rows[:, :], start=True, stop=True)
                last.then_inc(bias_psum, 1)
                pe.wait_ge(B_step, STEPS + 1 + n_B)
                pe.wait_ge(bias_ready, 1)

                def square(r, s, mt):
                    if mt == 0:
                        pe.wait_ge(trace_step, 3 * r + 1)
                    else:
                        pe.wait_ge(square_ready, NT * r + mt)
                    for k in range(NT):
                        last = pe.matmul(SQ_BANK[:, :], Sq[s][:, k, mt * P:(mt + 1) * P], Sq[s][:, k, :],
                                         start=k == 0, stop=k == NT - 1)
                    last.then_inc(square_psum, 1)

                def round_(r, s, half):
                    enters, leaves, squares = within(r, 0, BATCH - 1), within(r, 1, BATCH), within(r, 0, BATCH - 1)
                    if squares:
                        pe.wait_ge(trace_part_ready, r + 1)
                        pe.matmul(SQ_BANK[:, 0:1], ones[:, :], trace_part[:, :], start=True,
                                  stop=True).then_inc(trace_psum, 1)
                    if leaves:
                        for m in range(GROUP):
                            pe.wait_ge(T_ready[m], r)
                        for nt in range(NT):
                            at_least(pe, y_ready, NT * (r - 2) + nt + 1)
                            for m in range(GROUP):
                                last = pe.matmul(psum[nt][:, 0:GROUP * D], T[1 - s][m][:, nt * P:(nt + 1) * P],
                                                 B[:, m, :, :].rearrange("p i d -> p (i d)"),
                                                 start=m == 0, stop=m == GROUP - 1, skip_group_check=True)
                            last.then_inc(C_psum, 1)
                    if squares:
                        square(r, s, 0)
                    if enters:
                        pe.wait_ge(x0_ready, r + 1)
                        at_least(pe, T_ready[0], r)
                        for nt in range(NT):
                            last = pe.transpose(psum[4][:, nt * P:(nt + 1) * P], x0[s][:, nt, :], ident[:, :])
                        last.then_inc(T_psum[0], 1)
                    if squares:
                        square(r, s, 1)
                    if enters:
                        at_least(pe, T_ready[1], r)
                        for k in range(NT):
                            last = pe.matmul(psum[5][:, :], x0[s][:, k, :], PT[:, k, :],
                                             start=k == 0, stop=k == NT - 1)
                        last.then_inc(T_psum[1], 1)
                    if leaves:
                        pe.wait_ge(C2_ready, NT * r)
                        for nt in range(NT):
                            for k in range(NT):
                                last = pe.matmul(psum[nt][:, D:2 * D], P3T[:, k, nt * P:(nt + 1) * P], C2[:, k, :],
                                                 start=False, stop=k == NT - 1, skip_group_check=True)
                            last.then_inc(Y1_psum, 1)
                    if squares:
                        square(r, s, 2)
                    if enters:
                        at_least(pe, T_ready[2], r)
                        for k in range(NT):
                            last = pe.matmul(psum[6][:, :], x0[s][:, k, :], P2T[:, k, :],
                                             start=k == 0, stop=k == NT - 1)
                        last.then_inc(T_psum[2], 1)
                    if leaves:
                        pe.wait_ge(Y1_ready, NT * r)
                        for nt in range(NT):
                            for k in range(NT):
                                last = pe.matmul(psum[nt][:, 0:D], P3T[:, k, nt * P:(nt + 1) * P], Y1[:, k, :],
                                                 start=False, stop=k == NT - 1, skip_group_check=True)
                            last.then_inc(Y0_psum, 1)
                    if squares:
                        square(r, s, 3)
                rounds(pe, round_, 2, BATCH, BATCH + 1)

                pe.wait_ge(v_ready, 1)
                for nt in range(NT):
                    for k in range(NT):
                        last = pe.matmul(psum[4][:, nt:nt + 1], S[:, k, nt * P:(nt + 1) * P], v[:, k:k + 1],
                                         start=k == 0, stop=k == NT - 1)
                last.then_inc(Sv_psum, 1)
                pe.wait_ge(Sv_step, 3)
                pe.matmul(psum[5][:, 0:2], ones[:, :], quotient[:, :], start=True,
                          stop=True).then_inc(quotient_psum, 1)

            @block.scalar
            def _(act):
                act.wait_ge(small_loaded, 16 * 5)
                act.activation(a_exp[:, :], alpha_in[:, :], ACT.Exp, scale=-1.0).then_inc(alpha_exp, 1)
                for mt in range(NT):
                    act.wait_ge(adjT_psum, mt + 1)
                    act.activation(adjT[:, mt, :], psum[mt][:, :], ACT.Copy).then_inc(adjT_ready, 1)
                for mt in range(NT):
                    act.wait_ge(PT_psum, mt + 1)
                    act.activation(PT[:, mt, :], psum[mt][:, :], ACT.Copy).then_inc(PT_ready, 1)
                for mt in range(NT):
                    act.wait_ge(P2_psum, mt + 1)
                    act.activation(P2T[:, mt, :], psum[mt][:, :], ACT.Copy).then_inc(P2_ready, 1)
                for mt in range(NT):
                    act.wait_ge(P3_psum, mt + 1)
                    act.activation(P3T[:, mt, :], psum[mt][:, :], ACT.Copy).then_inc(P3_ready, 1)

                def square_out(r, s, mt):
                    act.wait_ge(square_psum, NT * r + mt + 1)
                    if mt == 0:
                        act.wait_ge(trace_step, 3 * r + 3)
                    act.activation(Sq[1 - s][:, mt, :], SQ_BANK[:, :], ACT.Copy,
                                   scale=trace_inv2[:, 0:1]).then_inc(square_ready, 1)

                def round_(r, s, half):
                    enters, leaves, squares = within(r, 0, BATCH - 1), within(r, 1, BATCH), within(r, 0, BATCH - 1)
                    if enters:
                        act.wait_ge(ln_pool, 4 * r + 4)
                        at_least(act, T_psum[2], r - 1)
                        for t in range(NT):
                            last = act.activation(x0[s][:, t, :], x_in[s][:, t, :], ACT.Relu,
                                                  scale=rstd[s][:, t:t + 1], bias=shift_ln[s][:, t:t + 1])
                        last.then_inc(x0_ready, 1)
                    if leaves:
                        for nt in range(NT):
                            act.wait_ge(C_psum, NT * (r - 1) + nt + 1)
                            act.activation(C2[:, nt, :], psum[nt][:, 2 * D:3 * D], ACT.Copy).then_inc(C2_ready, 1)
                    if squares:
                        square_out(r, s, 0)
                        square_out(r, s, 1)
                    if enters:
                        act.wait_ge(T_psum[1], r + 1)
                        act.activation(T[s][1][:, :], psum[5][:, :], ACT.Copy).then_inc(T_ready[1], 1)
                    if leaves:
                        for nt in range(NT):
                            act.wait_ge(Y1_psum, NT * (r - 1) + nt + 1)
                            act.activation(Y1[:, nt, :], psum[nt][:, D:2 * D], ACT.Copy).then_inc(Y1_ready, 1)
                    if squares:
                        square_out(r, s, 2)
                        square_out(r, s, 3)
                rounds(act, round_, 2, BATCH, BATCH + 1)

            @block.vector
            def _(dve):
                dve.wait_ge(alpha_exp, 1)
                dve.tensor_scalar(a_one[:, :], a_exp[:, :], 1.0, None, ALU.add).then_inc(dve_setup, 1)
                dve.wait_ge(dve_setup, 1)
                dve.reciprocal(a_sig[:, :], a_one[:, :]).then_inc(dve_setup, 1)
                dve.wait_ge(dve_setup, 2)
                dve.tensor_scalar(edge_scale[:, :], a_sig[:, :], 0.5 * DT, None, ALU.mult).then_inc(dve_setup, 1)
                dve.tensor_scalar(self_scale[:, :], a_sig[:, :], -0.5 * DT, 1.0 - DT, ALU.mult,
                                  ALU.add).then_inc(dve_setup, 1)
                dve.wait_ge(dve_setup, 4)
                dve.wait_ge(ident_ready, 1)
                dve.wait_ge(loaded, 16 * NT)
                for t in range(NT):
                    dve.tensor_scalar(Pn[:, t, :], A[:, t, :], edge_scale[:, t:t + 1], None,
                                      ALU.mult).then_inc(P_ready, 1)
                for t in range(NT):
                    block_t = Pn[:, t, t * P:(t + 1) * P]
                    dve.wait_ge(P_ready, NT)
                    dve.scalar_tensor_tensor(out=block_t, in0=ident[:, :], scalar=self_scale[:, t:t + 1],
                                             in1=block_t, op0=ALU.mult, op1=ALU.add).then_inc(P_ready, 1)
                dve.tensor_scalar(d_clip[:, :], d_in[:, :], 0.0, 1.0, ALU.max, ALU.min).then_inc(dve_setup, 1)
                dve.wait_ge(dve_setup, 5)
                dve.tensor_scalar(d_dt[:, :], d_clip[:, :], DT, None, ALU.mult).then_inc(dve_setup, 1)
                dve.wait_ge(dve_setup, 6)
                dve.wait_ge(wT_psum, 1)
                dve.tensor_copy(wT[:, :], psum[4][:, 0:D]).then_inc(wT_ready, 1)
                dve.tensor_scalar(dwT[:, :], psum[4][:, 0:D], d_dt[:, 0:1], None, ALU.mult).then_inc(wT_ready, 1)
                dve.tensor_copy(powers[:, 0, 0:D], ident[:, :])
                dve.tensor_copy(powers[:, 0, D:D + 1], b_in[:, :])
                dve.wait_ge(weff_psum, 1)
                dve.tensor_copy(W, psum[5][:, 0:D]).then_inc(power_ready, 1)
                dve.wait_ge(power_psum, 1)
                dve.tensor_copy(powers[:, 1, D:D + 1], psum[5][:, D:D + 1]).then_inc(power_ready, 1)
                for k in range(2, STEPS + 1):
                    dve.wait_ge(power_psum, k)
                    dve.tensor_copy(powers[:, k, :], psum[5][:, 0:D + 1]).then_inc(power_ready, 1)
                dve.memset(U[:, :, 0:1], 1.0).then_inc(U_ready, 1)
                dve.wait_ge(power_ready, STEPS + 1)
                for j in range(STEPS + 1):
                    dve.tensor_scalar(beta[:, j:j + 1], powers[:, STEPS - j, D:D + 1], float(comb(STEPS, j)), None,
                                      ALU.mult).then_inc(beta_ready, 1)
                dve.wait_ge(adjT_ready, NT)
                dve.tensor_tensor(out=S[:, :, :], in0=A[:, :, :], in1=adjT[:, :, :], op=ALU.add).then_inc(S_ready, 1)
                dve.wait_ge(S_ready, 1)
                dve.tensor_reduce(row_sum[:, :], S[:, :, :].rearrange("p t n -> p (t n)"), AX.X,
                                  ALU.add).then_inc(S_ready, 1)
                dve.tensor_scalar(mask[:, :, :], A[:, :, :], 0.0, MASKED, ALU.is_le, ALU.mult).then_inc(S_ready, 1)
                dve.wait_ge(FW_psum, 1)
                at = {}
                count = 0
                for j in range(STEPS + 1):
                    k = STEPS - j
                    count += 1
                    at[j] = count
                    dve.tensor_scalar(B[:, j % GROUP, j // GROUP, :], psum[4 + k // NT][:, k % NT * D:(k % NT + 1) * D],
                                      float(comb(STEPS, j)), None, ALU.mult).then_inc(B_step, 1)
                for i in range(STEPS):
                    for j in range(STEPS - i):
                        dve.wait_ge(B_step, at[j])
                        count += 1
                        at[j] = count
                        Bj = B[:, j % GROUP, j // GROUP, :]
                        dve.scalar_tensor_tensor(out=Bj, in0=powers[:, i, 0:D], scalar=DT * comb(i + j, j), in1=Bj,
                                                 op0=ALU.mult, op1=ALU.add).then_inc(B_step, 1)
                dve.wait_ge(sum_psum, 1)
                dve.tensor_scalar(shift[:, :], SQ_BANK[:, 0:1], 0.5 / N, TINY, ALU.mult,
                                  ALU.add).then_inc(S0_ready, 1)
                dve.tensor_scalar(S[:, :, :], S[:, :, :], 0.5, None, ALU.mult).then_inc(S0_ready, 1)
                dve.wait_ge(S0_ready, 2)
                dve.tensor_copy(Sq[0][:, :, :], S[:, :, :]).then_inc(S0_ready, 1)
                dve.wait_ge(S0_ready, 3)
                for t in range(NT):
                    dve.scalar_tensor_tensor(out=Sq[0][:, t, t * P:(t + 1) * P], in0=ident[:, :],
                                             scalar=shift[:, 0:1], in1=S[:, t, t * P:(t + 1) * P],
                                             op0=ALU.mult, op1=ALU.add).then_inc(S0_ready, 1)
                dve.wait_ge(S0_ready, 3 + NT)
                dve.tensor_tensor_reduce(diagonal[:, :, :], diagonal_of(Sq[0]).bitcast(F32), ident_tiles, 1.0, 0.0, ALU.mult,
                                         ALU.add, trace_part[:, :]).then_inc(trace_part_ready, 1)
                for g in range(GROUP):
                    n_cols = 2 if g == 2 else 3
                    dve.wait_ge(U_psum, g + 1)
                    dve.tensor_copy(U[:, :, 3 * g + 1:3 * g + 1 + n_cols],
                                    psum[0][:, 0:4 * NT].rearrange("p (t c) -> p t c", c=4)[:, :, 0:n_cols]
                                    ).then_inc(U_ready, 1)
                dve.wait_ge(rows_psum, 1)
                dve.tensor_copy(U_rows[:, :], psum[1][0:STEPS + 1, :]).then_inc(rows_ready, 1)
                dve.tensor_copy(beta_rows[:, :], psum[2][0:STEPS + 1, 0:D]).then_inc(rows_ready, 1)
                dve.wait_ge(bias_psum, 1)
                dve.tensor_copy(bias[:, :, :].rearrange("p t d -> p (t d)"), psum[3][:, :]).then_inc(bias_ready, 1)

                def round_(r, s, half):
                    enters, leaves, squares = within(r, 0, BATCH - 1), within(r, 1, BATCH), within(r, 0, BATCH - 1)
                    if enters:
                        dve.wait_ge(x_loaded[s], 16 * (half + 1))
                        at_least(dve, mv_ready, r)
                        for t in range(NT):
                            last = dve.bn_stats(stats[:, t, :], x_in[s][:, t, :])
                        last.then_inc(stats_ready, 1)
                        dve.wait_ge(stats_ready, r + 1)
                        at_least(dve, ln_pool, 4 * (r - 1))
                        dve.sem_inc(dve_waited, 1)
                        for t in range(NT):
                            last = dve.bn_aggr(mv[s][:, t, :], stats[:, t, :])
                        last.then_inc(mv_ready, 1)
                    if squares:
                        dve.wait_ge(trace_psum, r + 1)
                        dve.tensor_scalar(trace[:, :], SQ_BANK[:, 0:1], TINY, None, ALU.max).then_inc(trace_step, 1)
                        dve.wait_ge(trace_step, 3 * r + 1)
                        dve.reciprocal(trace_inv[:, :], trace[:, :]).then_inc(trace_step, 1)
                        dve.wait_ge(trace_step, 3 * r + 2)
                        at_least(dve, square_ready, NT * r)
                        dve.tensor_tensor(out=trace_inv2[:, :], in0=trace_inv[:, :], in1=trace_inv[:, :],
                                          op=ALU.mult).then_inc(trace_step, 1)
                    if enters:
                        dve.wait_ge(T_psum[0], r + 1)
                        dve.tensor_copy(T[s][0][:, :], psum[4][:, :]).then_inc(T_ready[0], 1)
                        dve.wait_ge(T_psum[2], r + 1)
                        dve.tensor_copy(T[s][2][:, :], psum[6][:, :]).then_inc(T_ready[2], 1)
                    if leaves:
                        dve.wait_ge(x_bias_ready, r)
                        for nt in range(NT):
                            dve.wait_ge(Y0_psum, NT * (r - 1) + nt + 1)
                            dve.tensor_tensor(out=y[:, bass.ds((r - 1) * N + nt * D, D)], in0=psum[nt][:, 0:D],
                                              in1=x_bias[1 - s][:, nt, :], op=ALU.add).then_inc(y_ready, 1)
                    if squares:
                        dve.wait_ge(square_ready, NT * (r + 1))
                        dve.tensor_tensor_reduce(diagonal[:, :, :], diagonal_of(Sq[1 - s]).bitcast(F32), ident_tiles, 1.0, 0.0,
                                                 ALU.mult, ALU.add, trace_part[:, :]).then_inc(trace_part_ready, 1)
                rounds(dve, round_, 2, BATCH, BATCH + 1)

                dve.tensor_reduce(v[:, :], Sq[0][:, :, :].bitcast(F32), AX.X, ALU.add).then_inc(v_ready, 1)
                dve.wait_ge(Sv_psum, 1)
                dve.tensor_copy(Sv[:, :], psum[4][:, 0:NT]).then_inc(Sv_step, 1)
                dve.wait_ge(Sv_step, 1)
                dve.tensor_tensor_reduce(scratch4[:, :], v[:, :], Sv[:, :], 1.0, 0.0, ALU.mult, ALU.add,
                                         quotient[:, 0:1]).then_inc(Sv_step, 1)
                dve.wait_ge(Sv_step, 2)
                dve.tensor_tensor_reduce(scratch4[:, :], v[:, :], v[:, :], 1.0, 0.0, ALU.mult, ALU.add,
                                         quotient[:, 1:2]).then_inc(Sv_step, 1)
                dve.wait_ge(quotient_psum, 1)
                dve.tensor_scalar(quotient_all[:, :], psum[5][:, 0:2], TINY, None, ALU.max).then_inc(lam_step, 1)
                dve.wait_ge(lam_step, 1)
                dve.reciprocal(den_inv[:, :], quotient_all[:, 1:2]).then_inc(lam_step, 1)
                dve.wait_ge(lam_step, 2)
                dve.tensor_scalar(lam[:, :], quotient_all[:, 0:1], den_inv[:, 0:1], 1e-8, ALU.mult,
                                  ALU.add).then_inc(lam_step, 1)
                dve.wait_ge(lam_step, 3)
                dve.reciprocal(lam_inv[:, :], lam[:, :]).then_inc(lam_step, 1)
                dve.wait_ge(lam_step, 4)
                dve.tensor_scalar(two_over_lam[:, :], lam_inv[:, :], 2.0, None, ALU.mult).then_inc(lam_step, 1)
                dve.wait_ge(lam_step, 5)
                dve.tensor_scalar(adjT[:, :, :], adjT[:, :, :], two_over_lam[:, 0:1], None,
                                  ALU.mult).then_inc(lam_step, 1)
                dve.wait_ge(lam_step, 6)
                for t in range(NT):
                    own = adjT[:, t, t * P:(t + 1) * P]
                    last = dve.tensor_tensor(out=own, in0=own, in1=ident[:, :], op=ALU.subtract)
                last.then_inc(lam_step, 1)


AT_MOMENTS, AT_CONV, AT_Z, AT_Z_OUT, AT_X1, AT_X1T, AT_Q, AT_K, AT_V = 0, 4, 5, 5, 7, 9, 10, 11, 12
AT_RINV, AT_SPREAD, AT_O, AT_PROJ, AT_Z2, AT_X2 = 2, 4, 4, 6, 6, 8
TURN_LAG = 2
DVE_COPIES = (3, 7, 11, 15)
RING = 4
TURNED = 8
STACKS = 4
ROWS = 9


def copied(by_dve, batch, unit):
    mine = [u for u in range(UNITS) if (u in DVE_COPIES) == by_dve]
    return len(mine) * batch + sum(u <= unit for u in mine)


def layer1(nc, whole, tensor, sem, psum, Wc, bc, g1, be1, Wq, Wk, Wv, Wo, bo, g2, be2, W1, b1, W2, b2, g3, be3,
           out_dram, y, adjT, mask, ident, ones, exponent, two_over_lam, waited):
    dve_waited, pool_waited = waited
    Lnorm = adjT
    x2 = tensor(whole, "x2", [P, BATCH * N])
    bc_all = tensor(whole, "bc_all", [P, ROWS, D])
    BC, G1, BE1, BO, G2, BE2, B2, G3, BE3 = range(ROWS)
    W1s = tensor(whole, "W1s", [P, HID])
    W2s = tensor(whole, "W2s", [P, HT, D])
    b1s = tensor(whole, "b1s", [P, HT])
    mlp_loaded = sem("mlp_loaded")

    def all_tiles(row):
        return bc_all[:, row:row + 1, :].broadcast_to([P, NT, D])

    def flat(t):
        return t[:, :, :].rearrange("p t d -> p (t d)")

    with ExitStack() as ctx:
        def sb(name, shape, dt=F32):
            return tensor(ctx, name, shape, dt)

        row_in = sb("row_in", [1, ROWS, D])
        Wcs, Wqs, Wks, Wvs, Wos = (sb(f"W_{n}", [P, D]) for n in "cqkvo")
        stats_a, stats_b, stats_c = (sb(f"stats_{n}", [P, NT, 6]) for n in "abc")
        mv_a, mv_b, mv_c = (sb(f"mv_{n}", [P, NT, 2]) for n in "abc")
        ve_a, ve_b, ve_c = (sb(f"ve_{n}", [P, NT]) for n in "abc")
        rstd_a, rstd_b, rstd_c = (sb(f"rstd_{n}", [P, NT]) for n in "abc")
        y_now = sb("y_now", [P, NT, D])
        h_norm = sb("h_norm", [P, NT, D])
        h = [sb(f"h{i}", [P, NT, D]) for i in range(2)]
        convT = sb("convT", [P, N])
        z = sb("z", [P, NT, D])
        z_gain = sb("z_gain", [P, NT, D])
        z_norm = sb("z_norm", [P, NT, D])
        x1 = sb("x1", [P, NT, D])
        x1_bo = [sb(f"x1_bo{i}", [P, NT, D]) for i in range(2)]
        x1T = sb("x1T", [P, N])
        q_hi, q_lo, k_hi, k_lo = (sb(n, [P, N], F32R) for n in ("q_hi", "q_lo", "k_hi", "k_lo"))
        q_stack = [sb(f"q_stack{i}", [P, HEADS, N], F32R) for i in range(2)]
        k_stack = [sb(f"k_stack{i}", [P, HEADS, N], F32R) for i in range(2)]
        v = [sb(f"v_{i}", [P, NT, D]) for i in range(2)]
        prob = [sb(f"prob{i}", [P, N]) for i in range(RING)]
        low = sb("low", [P, TURNED])
        probT = [sb(f"probT{i}", [P, NT, P]) for i in range(TURNED)]
        row_sums = [sb(f"row_sums{i}", [P, UNITS]) for i in range(2)]
        rinv = sb("rinv", [P, UNITS * HD])
        spread = sb("spread", [P, N])
        oT = sb("oT", [P, N])
        z2 = sb("z2", [P, NT, D])
        z2_gain = sb("z2_gain", [P, NT, D])

        rows_loaded = sem("rows_loaded")
        weights_loaded = sem("weights_loaded")
        rows_spread = sem("rows_spread")
        rows_copied = sem("rows_copied")
        a_stats, a_mv, a_pool, h_part, h_ready = (sem(n) for n in ("a_stats", "a_mv", "a_pool", "h_part", "h_ready"))
        y_copied = sem("y_copied")
        conv_psum, conv_ready = sem("conv_psum"), sem("conv_ready")
        z_psum, z_ready, b_stats, b_mv, b_pool, z_step, x1_ready, x1_bo_ready = (
            sem(n) for n in ("z_psum", "z_ready", "b_stats", "b_mv", "b_pool", "z_step", "x1_ready", "x1_bo_ready"))
        x1T_psum, x1T_ready = sem("x1T_psum"), sem("x1T_ready")
        q_psum, q_hi_ready, q_lo_ready = sem("q_psum"), sem("q_hi_ready"), sem("q_lo_ready")
        k_psum, k_hi_ready, k_lo_ready = sem("k_psum"), sem("k_hi_ready"), sem("k_lo_ready")
        v_psum, v_copied = sem("v_psum"), sem("v_copied")
        stacked = [sem(f"stacked{i}") for i in range(2)]
        scores_psum, masked, exp_done, turned_psum = (
            sem(n) for n in ("scores_psum", "masked", "exp_done", "turned_psum"))
        copied_act, copied_dve = sem("copied_act"), sem("copied_dve")
        o_psum, rinv_ready, spread_psum, spread_ready, oT_ready = (
            sem(n) for n in ("o_psum", "rinv_ready", "spread_psum", "spread_ready", "oT_ready"))
        proj_psum, z2_ready, c_stats, c_mv, c_pool, z2_step, x2_ready = (
            sem(n) for n in ("proj_psum", "z2_ready", "c_stats", "c_mv", "c_pool", "z2_step", "x2_ready"))

        A_BANK, B_BANK = psum[4], psum[5]
        STACK_DMAS = 2 * STACKS * HEADS * 16

        def parts(r):
            return within(r, 0, BATCH - 1), within(r, 1, BATCH), within(r, 2, BATCH + 1)

        def copy_wait(eng, batch, unit):
            by_dve = unit in DVE_COPIES
            at_least(eng, copied_dve if by_dve else copied_act, copied(by_dve, batch, unit))

        with nc.Block() as block:

            @block.sync
            def _(sp):
                for n, row in enumerate((bc, g1, be1, bo, g2, be2, b2, g3, be3)):
                    sp.dma_start(row_in[:, n, :], row.rearrange("(o d) -> o d", o=1)).then_inc(rows_loaded, 16)
                for tile, source in ((Wcs, Wc), (Wqs, Wq), (Wks, Wk), (Wvs, Wv), (Wos, Wo)):
                    sp.dma_start(tile[:, :], source).then_inc(weights_loaded, 16)
                sp.dma_start(W1s[:, :], W1).then_inc(mlp_loaded, 16)
                sp.dma_start(W2s[:, :, :], W2.rearrange("(j p) d -> p j d", p=P)).then_inc(mlp_loaded, 16)
                sp.dma_start(b1s[:, :], b1.rearrange("(j p) -> p j", p=P),
                             allow_slow_non_contiguous=True).then_inc(mlp_loaded, 16)

                def stack(p, s, half):
                    for tile, ready, hi, lo, order in ((q_stack, q_lo_ready, q_hi, q_lo, (0, 0, 1, 1)),
                                                       (k_stack, k_lo_ready, k_hi, k_lo, (0, 1, 0, 1))):
                        sp.wait_ge(ready, p + 1)
                        for j, part in enumerate(order):
                            for head in range(HEADS):
                                sp.dma_start(tile[s][j * HD:(j + 1) * HD, head, :].bitcast(F32),
                                             (hi, lo)[part][head * HD:(head + 1) * HD, :].bitcast(F32)
                                             ).then_inc(stacked[s], 16)
                rounds(sp, stack, 2, BATCH, BATCH)

            @block.gpsimd
            def _(pool):
                def inverse_root(b, mv, mv_sem, ve, rstd, pool_sem, used_sem, used):
                    pool.wait_ge(mv_sem, b + 1)
                    at_least(pool, used_sem, used)
                    pool.sem_inc(pool_waited, 1)
                    pool.tensor_scalar(ve[:, :], mv[:, :, 1], EPS, None, ALU.add).then_inc(pool_sem, 1)
                    pool.wait_ge(pool_sem, 2 * b + 1)
                    pool.tensor_tensor(out=rstd[:, :], in0=ve[:, :], in1=exponent[:, :],
                                       op=ALU.pow).then_inc(pool_sem, 1)

                def round_(r, s, half):
                    enters, attends, leaves = parts(r)
                    if enters:
                        inverse_root(r, mv_a, a_mv, ve_a, rstd_a, a_pool, h_ready, r)
                        pool.tensor_copy(flat(y_now), y[:, bass.ds(r * N, N)]).then_inc(y_copied, 1)
                        pool.wait_ge(y_copied, r + 1)
                        pool.wait_ge(a_pool, 2 * r + 2)
                        pool.sem_inc(pool_waited, 1)
                        for t in range(NT):
                            last = pool.tensor_scalar(h_norm[:, t, :], y_now[:, t, :],
                                                      mv_a[:, t, 0:1], rstd_a[:, t:t + 1], ALU.subtract, ALU.mult)
                        last.then_inc(h_part, 1)
                        pool.wait_ge(h_part, r + 1)
                        at_least(pool, x1_ready, r - 1)
                        pool.sem_inc(pool_waited, 1)
                        pool.tensor_scalar(h[s][:, :, :], h_norm[:, :, :], 0.0, None, ALU.max).then_inc(h_ready, 1)
                    if enters:
                        inverse_root(r, mv_b, b_mv, ve_b, rstd_b, b_pool, x1_ready, r)
                    if leaves:
                        e = r - 2
                        inverse_root(e, mv_c, c_mv, ve_c, rstd_c, c_pool, x2_ready, e)
                    if enters:
                        pool.wait_ge(x1_ready, r + 1)
                        at_least(pool, z2_ready, r - 1)
                        pool.tensor_tensor(out=x1_bo[s][:, :, :], in0=x1[:, :, :], in1=all_tiles(BO),
                                           op=ALU.add).then_inc(x1_bo_ready, 1)
                pool.wait_ge(rows_copied, 3)
                rounds(pool, round_, 2, BATCH, BATCH + 2)

            @block.tensor
            def _(pe):
                pe.wait_ge(rows_loaded, 16 * ROWS)
                row_flat = row_in[:, :, :].rearrange("o r d -> o (r d)")
                for c in range(3):
                    cols = min(N, ROWS * D - c * N)
                    pe.matmul(psum[c][:, 0:cols], ones[0:1, :], row_flat[:, c * N:c * N + cols], start=True,
                              stop=True).then_inc(rows_spread, 1)
                pe.wait_ge(weights_loaded, 16 * 5)
                pe.wait_ge(rows_copied, 3)

                def scores(a, s, u, half):
                    if u == 0:
                        pe.wait_ge(stacked[s], STACK_DMAS * half)
                    at_least(pe, masked, UNITS * a + u - 1)
                    t, head = divmod(u, HEADS)
                    pe.matmul(psum[u % 2][:, :], q_stack[s][:, head, t * P:(t + 1) * P], k_stack[s][:, head, :],
                              start=True, stop=True).then_inc(scores_psum, 1)

                def turn(batch, u):
                    pe.wait_ge(exp_done, UNITS * batch + u + 1)
                    if isinstance(batch, int) and batch == 0 and u < 2:
                        pass
                    elif u < 2:
                        copy_wait(pe, batch - 1, u - 2 + UNITS)
                    else:
                        copy_wait(pe, batch, u - 2)
                    for mt in range(NT):
                        last = pe.transpose(psum[2 + u % 2][:, mt * P:(mt + 1) * P],
                                            prob[u % RING][:, mt * P:(mt + 1) * P], ident[:, :])
                    last.then_inc(turned_psum, 1)

                def values(batch, s, t):
                    for u in range(HEADS * t, HEADS * (t + 1)):
                        copy_wait(pe, batch, u)
                    if t == 0:
                        pe.wait_ge(v_copied, batch + 1)
                        at_least(pe, oT_ready, batch - 1)
                    for mt in range(NT):
                        for head in range(HEADS):
                            rows = slice(head * HD, (head + 1) * HD)
                            last = pe.matmul(psum[6 + s][rows, t * P:(t + 1) * P], v[s][:, mt, rows],
                                             probT[(HEADS * t + head) % TURNED][:, mt, :],
                                             start=mt == 0, stop=mt == NT - 1, skip_group_check=True)
                    last.then_inc(o_psum, 1)

                def round_(r, s, half):
                    enters, attends, leaves = parts(r)
                    a, e = r - 1, r - 2
                    for u in range(UNITS):
                        if attends:
                            scores(a, 1 - s, u, half + s)
                        if u >= TURN_LAG and attends:
                            turn(a, u - TURN_LAG)
                        if u < TURN_LAG and leaves:
                            turn(e, u - TURN_LAG + UNITS)
                        if u == 3 and leaves:
                            values(e, s, NT - 1)
                        if u > 3 and u % HEADS == 3 and attends:
                            values(a, 1 - s, u // HEADS - 1)
                        if u == AT_SPREAD and leaves:
                            pe.wait_ge(rinv_ready, e + 1)
                            at_least(pe, k_lo_ready, min(e + 2, BATCH) if isinstance(e, int) else e + 2)
                            for t in range(NT):
                                last = pe.transpose(
                                    A_BANK[:, t * P:(t + 1) * P],
                                    rinv[:, t * P:(t + 1) * P],
                                    ident[:, :])
                            last.then_inc(spread_psum, 1)
                        if u == AT_CONV and enters:
                            pe.wait_ge(h_ready, r + 1)
                            at_least(pe, v_copied, r)
                            for k in range(NT):
                                last = pe.matmul(B_BANK[:, :], h[s][:, k, :], Lnorm[:, k, :],
                                                 start=k == 0, stop=k == NT - 1)
                            last.then_inc(conv_psum, 1)
                        if u == AT_Z and enters:
                            pe.wait_ge(conv_ready, r + 1)
                            for t in range(NT):
                                last = pe.matmul(B_BANK[:, t * D:(t + 1) * D], convT[:, t * P:(t + 1) * P],
                                                 Wcs[:, :], start=True, stop=True)
                            last.then_inc(z_psum, 1)
                        if u == AT_PROJ and leaves:
                            pe.wait_ge(oT_ready, e + 1)
                            for t in range(NT):
                                last = pe.matmul(A_BANK[:, t * D:(t + 1) * D], oT[:, t * P:(t + 1) * P],
                                                 Wos[:, :], start=True, stop=True)
                            last.then_inc(proj_psum, 1)
                        if u == AT_X1T and enters:
                            pe.wait_ge(x1_ready, r + 1)
                            at_least(pe, z2_ready, r - 1)
                            for t in range(NT):
                                last = pe.transpose(A_BANK[:, t * P:(t + 1) * P], x1[:, t, :], ident[:, :])
                            last.then_inc(x1T_psum, 1)
                        if u == AT_Q and enters:
                            pe.wait_ge(x1T_ready, r + 1)
                            pe.matmul(B_BANK[:, :], Wqs[:, :], x1T[:, :], start=True, stop=True).then_inc(q_psum, 1)
                        if u == AT_K and enters:
                            pe.matmul(A_BANK[:, :], Wks[:, :], x1T[:, :], start=True, stop=True).then_inc(k_psum, 1)
                        if u == AT_V and enters:
                            pe.wait_ge(q_lo_ready, r + 1)
                            for t in range(NT):
                                last = pe.matmul(B_BANK[:, t * D:(t + 1) * D], x1T[:, t * P:(t + 1) * P],
                                                 Wvs[:, :], start=True, stop=True)
                            last.then_inc(v_psum, 1)
                rounds(pe, round_, 2, BATCH, BATCH + 2)

            @block.scalar
            def _(act):
                def copy_turned(batch, u):
                    act.wait_ge(turned_psum, UNITS * batch + u + 1)
                    act.activation(probT[u % TURNED][:, :, :].rearrange("p t n -> p (t n)"), psum[2 + u % 2][:, :],
                                   ACT.Copy).then_inc(copied_act, 1)

                def round_(r, s, half):
                    enters, attends, leaves = parts(r)
                    a, e = r - 1, r - 2
                    for u in range(UNITS):
                        if attends:
                            if u == 0:
                                at_least(act, rinv_ready, a - 1)
                            act.wait_ge(masked, UNITS * a + u + 1)
                            act.activation(prob[u % RING][:, :], prob[u % RING][:, :], ACT.Exp,
                                           bias=low[:, u % TURNED:u % TURNED + 1], scale=-1.0,
                                           accum_out=row_sums[1 - s][:, u:u + 1]).then_inc(exp_done, 1)
                        x = (u - TURN_LAG) % UNITS
                        if x not in DVE_COPIES:
                            if u < TURN_LAG and leaves:
                                copy_turned(e, x)
                            if u >= TURN_LAG and attends:
                                copy_turned(a, x)
                        if u == AT_SPREAD and leaves:
                            act.wait_ge(spread_psum, e + 1)
                            at_least(act, oT_ready, e)
                            act.activation(spread[:, :], A_BANK[:, :], ACT.Copy).then_inc(spread_ready, 1)
                        if u == AT_CONV and enters:
                            act.wait_ge(conv_psum, r + 1)
                            act.activation(convT[:, :], B_BANK[:, :], ACT.Copy).then_inc(conv_ready, 1)
                        if u == AT_X1T and enters:
                            act.wait_ge(x1T_psum, r + 1)
                            act.activation(x1T[:, :], A_BANK[:, :], ACT.Copy).then_inc(x1T_ready, 1)
                        if u == AT_Q and enters:
                            act.wait_ge(q_psum, r + 1)
                            if not (isinstance(r, int) and r == 0):
                                act.wait_ge(stacked[1 - s], STACK_DMAS * (half + s))
                            act.activation(q_hi[:, :], B_BANK[:, :], ACT.Copy,
                                           scale=-float(HD) ** -0.5).then_inc(q_hi_ready, 1)
                        if u == AT_K and enters:
                            act.wait_ge(k_psum, r + 1)
                            act.activation(k_hi[:, :], A_BANK[:, :], ACT.Copy).then_inc(k_hi_ready, 1)
                        if u == AT_V and enters:
                            act.wait_ge(v_psum, r + 1)
                            act.activation(flat(v[s]), B_BANK[:, :], ACT.Copy).then_inc(v_copied, 1)
                rounds(act, round_, 2, BATCH, BATCH + 2)

            @block.vector
            def _(dve):
                for c in range(3):
                    cols = min(N, ROWS * D - c * N)
                    dve.wait_ge(rows_spread, c + 1)
                    dve.tensor_copy(bc_all[:, :, :].rearrange("p r d -> p (r d)")[:, c * N:c * N + cols],
                                    psum[c][:, 0:cols]).then_inc(rows_copied, 1)
                dve.wait_ge(rows_copied, 3)

                def moments(b, source, stats, stats_sem, mv, mv_sem, used_sem):
                    at_least(dve, mv_sem, b)
                    for t in range(NT):
                        last = dve.bn_stats(stats[:, t, :], source(t))
                    last.then_inc(stats_sem, 1)
                    dve.wait_ge(stats_sem, b + 1)
                    at_least(dve, used_sem, b)
                    dve.sem_inc(dve_waited, 1)
                    for t in range(NT):
                        last = dve.bn_aggr(mv[:, t, :], stats[:, t, :])
                    last.then_inc(mv_sem, 1)

                def copy_turned(batch, u):
                    dve.wait_ge(turned_psum, UNITS * batch + u + 1)
                    dve.tensor_copy(probT[u % TURNED][:, :, :].rearrange("p t n -> p (t n)"),
                                    psum[2 + u % 2][:, :]).then_inc(copied_dve, 1)

                def round_(r, s, half):
                    enters, attends, leaves = parts(r)
                    a, e = r - 1, r - 2
                    for u in range(UNITS):
                        if attends:
                            dve.wait_ge(scores_psum, UNITS * a + u + 1)
                            at_least(dve, turned_psum, UNITS * a + u + 1 - RING)
                            dve.sem_inc(dve_waited, 1)
                            dve.tensor_tensor_reduce(prob[u % RING][:, :], psum[u % 2][:, :],
                                                     mask[:, u // HEADS, :], 1.0, 3e38, ALU.add, ALU.min,
                                                     low[:, u % TURNED:u % TURNED + 1]).then_inc(masked, 1)
                        x = (u - TURN_LAG) % UNITS
                        if x in DVE_COPIES:
                            if u < TURN_LAG and leaves:
                                copy_turned(e, x)
                            if u >= TURN_LAG and attends:
                                copy_turned(a, x)
                        if u == AT_MOMENTS and enters:
                            moments(r, lambda t: y[:, bass.ds(r * N + t * D, D)], stats_a, a_stats, mv_a, a_mv,
                                    h_part)
                        if u == AT_RINV and leaves:
                            dve.wait_ge(exp_done, UNITS * (e + 1))
                            at_least(dve, spread_psum, e)
                            dve.reciprocal(rinv[:, :].rearrange("p (u d) -> p u d", d=HD),
                                           row_sums[s][:, :].unsqueeze(2).broadcast_to([P, UNITS, HD])
                                           ).then_inc(rinv_ready, 1)
                        if u == AT_O and leaves:
                            dve.wait_ge(o_psum, NT * (e + 1))
                            dve.wait_ge(spread_ready, e + 1)
                            at_least(dve, proj_psum, e)
                            dve.tensor_tensor(out=oT[:, :], in0=psum[6 + s][:, :], in1=spread[:, :],
                                              op=ALU.mult).then_inc(oT_ready, 1)
                        if u == AT_Z_OUT and enters:
                            dve.wait_ge(z_psum, r + 1)
                            at_least(dve, x1_ready, r)
                            dve.tensor_tensor(out=z[:, :, :], in0=B_BANK[:, :].rearrange("p (t d) -> p t d", d=D),
                                              in1=all_tiles(BC), op=ALU.add).then_inc(z_ready, 1)
                            dve.wait_ge(z_ready, r + 1)
                            moments(r, lambda t: z[:, t, :], stats_b, b_stats, mv_b, b_mv, x1_ready)
                        if u == AT_Z2 and leaves:
                            dve.wait_ge(proj_psum, e + 1)
                            dve.wait_ge(x1_bo_ready, e + 1)
                            at_least(dve, x2_ready, e)
                            dve.tensor_tensor(out=flat(z2), in0=A_BANK[:, :], in1=flat(x1_bo[s]),
                                              op=ALU.add).then_inc(z2_ready, 1)
                            dve.wait_ge(z2_ready, e + 1)
                            moments(e, lambda t: z2[:, t, :], stats_c, c_stats, mv_c, c_mv, x2_ready)
                        if u == AT_X1 and enters:
                            dve.wait_ge(b_pool, 2 * r + 2)
                            for t in range(NT):
                                last = dve.scalar_tensor_tensor(out=z_gain[:, t, :], in0=z[:, t, :],
                                                                scalar=mv_b[:, t, 0:1], in1=bc_all[:, G1, :],
                                                                op0=ALU.subtract, op1=ALU.mult)
                            last.then_inc(z_step, 1)
                            dve.wait_ge(z_step, 2 * r + 1)
                            for t in range(NT):
                                last = dve.scalar_tensor_tensor(out=z_norm[:, t, :], in0=z_gain[:, t, :],
                                                                scalar=rstd_b[:, t:t + 1], in1=bc_all[:, BE1, :],
                                                                op0=ALU.mult, op1=ALU.add)
                            last.then_inc(z_step, 1)
                            dve.wait_ge(z_step, 2 * r + 2)
                            at_least(dve, x1T_psum, r)
                            at_least(dve, x1_bo_ready, r)
                            dve.scalar_tensor_tensor(out=flat(x1), in0=flat(z_norm), scalar=0.0, in1=flat(h[s]),
                                                     op0=ALU.max, op1=ALU.add).then_inc(x1_ready, 1)
                        if u == AT_X2 and leaves:
                            dve.wait_ge(c_pool, 2 * e + 2)
                            for t in range(NT):
                                last = dve.scalar_tensor_tensor(out=z2_gain[:, t, :], in0=z2[:, t, :],
                                                                scalar=mv_c[:, t, 0:1], in1=bc_all[:, G2, :],
                                                                op0=ALU.subtract, op1=ALU.mult)
                            last.then_inc(z2_step, 1)
                            dve.wait_ge(z2_step, e + 1)
                            for t in range(NT):
                                last = dve.scalar_tensor_tensor(out=x2[:, bass.ds(e * N + t * D, D)],
                                                                in0=z2_gain[:, t, :], scalar=rstd_c[:, t:t + 1],
                                                                in1=bc_all[:, BE2, :], op0=ALU.mult, op1=ALU.add)
                            last.then_inc(x2_ready, 1)
                        if u == AT_Q and enters:
                            dve.wait_ge(q_hi_ready, r + 1)
                            if not (isinstance(r, int) and r == 0):
                                dve.wait_ge(stacked[1 - s], STACK_DMAS * (half + s))
                            dve.scalar_tensor_tensor(out=q_lo[:, :], in0=B_BANK[:, :], scalar=-float(HD) ** -0.5,
                                                     in1=q_hi[:, :].bitcast(F32), op0=ALU.mult,
                                                     op1=ALU.subtract).then_inc(q_lo_ready, 1)
                        if u == AT_K and enters:
                            dve.wait_ge(k_hi_ready, r + 1)
                            dve.tensor_tensor(out=k_lo[:, :], in0=A_BANK[:, :], in1=k_hi[:, :].bitcast(F32),
                                              op=ALU.subtract).then_inc(k_lo_ready, 1)
                rounds(dve, round_, 2, BATCH, BATCH + 2)

    with ExitStack() as ctx:
        def sb(name, shape, dt=F32):
            return tensor(ctx, name, shape, dt)

        x2_now = [sb(f"x2_now{i}", [P, NT, D]) for i in range(2)]
        x2T = [sb(f"x2T{i}", [P, N]) for i in range(2)]
        x2_b2 = [sb(f"x2_b2{i}", [P, NT, D]) for i in range(2)]
        y_be3 = [sb(f"y_be3{i}", [P, NT, D]) for i in range(2)]
        gelu = [sb(f"gelu{i}", [P, HT, N]) for i in range(2)]
        z3 = [sb(f"z3_{i}", [P, NT, D]) for i in range(2)]
        z3_gain = sb("z3_gain", [P, NT, D])
        result = [sb(f"result{i}", [P, NT, D]) for i in range(2)]
        b2_tiles = sb("b2_tiles", [P, NT, D])
        be3_tiles = sb("be3_tiles", [P, NT, D])
        stats3 = sb("stats3", [P, NT, 6])
        mv3 = [sb(f"mv3{i}", [P, NT, 2]) for i in range(2)]
        ve3 = sb("ve3", [P, NT])
        rstd3 = [sb(f"rstd3{i}", [P, NT]) for i in range(2)]

        x2_now_ready, x2T_psum, x2T_ready, hid_psum, gelu_ready, mlp_psum, z3_ready = (
            sem(n) for n in ("x2_now_ready", "x2T_psum", "x2T_ready", "hid_psum", "gelu_ready", "mlp_psum", "z3_ready"))
        x2_b2_ready, y_be3_ready, stats3_ready, mv3_ready, pool3, z3_step, result_ready = (
            sem(n) for n in ("x2_b2_ready", "y_be3_ready", "stats3_ready", "mv3_ready", "pool3", "z3_step",
                             "result_ready"))
        tiles_ready = sem("tiles_ready")
        stored = [sem(f"stored{i}") for i in range(2)]

        with nc.Block() as block:

            @block.sync
            def _(sp):
                def store(b, s, half):
                    sp.wait_ge(result_ready, b + 1)
                    sp.dma_start(out_dram[:, bass.ds(b, 1), :, :].rearrange("p b t d -> p (b t) d"),
                                 result[s][:, :, :]).then_inc(stored[s], 16)
                rounds(sp, store, 2, BATCH, BATCH)
                for s in range(2):
                    sp.wait_ge(stored[s], 16 * (BATCH // 2))

            @block.gpsimd
            def _(pool):
                def round_(r, s, half):
                    if within(r, 0, BATCH - 1):
                        at_least(pool, z3_ready, r - 1)
                        pool.tensor_tensor(out=flat(x2_b2[s]), in0=x2[:, bass.ds(r * N, N)], in1=flat(b2_tiles),
                                           op=ALU.add).then_inc(x2_b2_ready, 1)
                        at_least(pool, result_ready, r - 1)
                        pool.tensor_tensor(out=flat(y_be3[s]), in0=y[:, bass.ds(r * N, N)], in1=flat(be3_tiles),
                                           op=ALU.add).then_inc(y_be3_ready, 1)
                    if within(r, 1, BATCH):
                        b = r - 1
                        pool.wait_ge(mv3_ready, b + 1)
                        at_least(pool, result_ready, b - 1)
                        pool.sem_inc(pool_waited, 1)
                        pool.tensor_scalar(ve3[:, :], mv3[1 - s][:, :, 1], EPS, None, ALU.add).then_inc(pool3, 1)
                        pool.wait_ge(pool3, 2 * b + 1)
                        pool.tensor_tensor(out=rstd3[1 - s][:, :], in0=ve3[:, :], in1=exponent[:, :],
                                           op=ALU.pow).then_inc(pool3, 1)
                for t in range(NT):
                    pool.tensor_copy(b2_tiles[:, t, :], bc_all[:, B2, :])
                    last = pool.tensor_copy(be3_tiles[:, t, :], bc_all[:, BE3, :])
                last.then_inc(tiles_ready, 1)
                pool.wait_ge(tiles_ready, 1)
                rounds(pool, round_, 2, BATCH, BATCH + 1)

            @block.tensor
            def _(pe):
                pe.wait_ge(mlp_loaded, 16 * 3)

                def round_(r, s, half):
                    if within(r, 0, BATCH - 1):
                        pe.wait_ge(x2_now_ready, r + 1)
                        at_least(pe, x2T_ready, r - 1)
                        for t in range(NT):
                            last = pe.transpose(psum[s][:, t * P:(t + 1) * P], x2_now[s][:, t, :], ident[:, :])
                        last.then_inc(x2T_psum, 1)
                    if within(r, 1, BATCH):
                        pe.wait_ge(gelu_ready, HT * r)
                        at_least(pe, z3_ready, r - 2)
                        for t in range(NT):
                            for j in range(HT):
                                last = pe.matmul(psum[7 - s][:, t * D:(t + 1) * D],
                                                 gelu[1 - s][:, j, t * P:(t + 1) * P], W2s[:, j, :],
                                                 start=j == 0, stop=j == HT - 1)
                        last.then_inc(mlp_psum, 1)
                    if within(r, 0, BATCH - 1):
                        pe.wait_ge(x2T_ready, r + 1)
                        for j in range(HT):
                            at_least(pe, gelu_ready, HT * (r - 2) + j + 1)
                            pe.matmul(psum[2 + HT * s + j][:, :], W1s[:, j * P:(j + 1) * P], x2T[s][:, :],
                                      start=True, stop=True).then_inc(hid_psum, 1)
                rounds(pe, round_, 2, BATCH, BATCH + 1)

            @block.scalar
            def _(act):
                def fetch(r, s):
                    at_least(act, x2T_psum, r - 1)
                    act.activation(flat(x2_now[s]), x2[:, bass.ds(r * N, N)], ACT.Copy).then_inc(x2_now_ready, 1)

                def round_(r, s, half):
                    if within(r, 0, BATCH - 1):
                        if isinstance(r, int) and r == 0:
                            fetch(0, 0)
                        act.wait_ge(x2T_psum, r + 1)
                        act.activation(x2T[s][:, :], psum[s][:, :], ACT.Copy).then_inc(x2T_ready, 1)
                        if within(r, 0, BATCH - 2):
                            fetch(r + 1, 1 - s)
                        for j in range(HT):
                            act.wait_ge(hid_psum, HT * r + j + 1)
                            act.activation(gelu[s][:, j, :], psum[2 + HT * s + j][:, :], ACT.Gelu,
                                           bias=b1s[:, j:j + 1]).then_inc(gelu_ready, 1)
                rounds(act, round_, 2, BATCH - 2, BATCH)

            @block.vector
            def _(dve):
                def round_(r, s, half):
                    if within(r, 2, BATCH + 1):
                        b = r - 2
                        dve.wait_ge(pool3, 2 * b + 2)
                        dve.wait_ge(y_be3_ready, b + 1)
                        for t in range(NT):
                            last = dve.scalar_tensor_tensor(out=z3_gain[:, t, :], in0=z3[s][:, t, :],
                                                            scalar=mv3[s][:, t, 0:1], in1=bc_all[:, G3, :],
                                                            op0=ALU.subtract, op1=ALU.mult)
                        last.then_inc(z3_step, 1)
                        dve.wait_ge(z3_step, b + 1)
                        if isinstance(r, int):
                            if b >= 2:
                                dve.wait_ge(stored[s], 16 * (b // 2))
                        else:
                            at_least(dve, stored[s], 16 * (half - 1))
                        for t in range(NT):
                            last = dve.scalar_tensor_tensor(out=result[s][:, t, :], in0=z3_gain[:, t, :],
                                                            scalar=rstd3[s][:, t:t + 1], in1=y_be3[s][:, t, :],
                                                            op0=ALU.mult, op1=ALU.add)
                        last.then_inc(result_ready, 1)
                    if within(r, 1, BATCH):
                        b = r - 1
                        dve.wait_ge(mlp_psum, b + 1)
                        dve.wait_ge(x2_b2_ready, b + 1)
                        dve.tensor_tensor(out=flat(z3[1 - s]), in0=psum[7 - s][:, :], in1=flat(x2_b2[1 - s]),
                                          op=ALU.add).then_inc(z3_ready, 1)
                        dve.wait_ge(z3_ready, b + 1)
                        at_least(dve, mv3_ready, b)
                        for t in range(NT):
                            last = dve.bn_stats(stats3[:, t, :], z3[1 - s][:, t, :])
                        last.then_inc(stats3_ready, 1)
                        dve.wait_ge(stats3_ready, b + 1)
                        at_least(dve, result_ready, b - 1)
                        dve.sem_inc(dve_waited, 1)
                        for t in range(NT):
                            last = dve.bn_aggr(mv3[1 - s][:, t, :], stats3[:, t, :])
                        last.then_inc(mv3_ready, 1)
                rounds(dve, round_, 2, BATCH, BATCH + 2)


_INS = ["x", "adj", "L0_gnn_alpha_train", "L0_gnn_w", "L0_gnn_d", "L0_gnn_fc_in_w", "L0_gnn_fc_in_b",
        "L1_gnn_Wc", "L1_gnn_bc", "L1_gnn_g1", "L1_gnn_be1", "L1_gnn_Wq", "L1_gnn_Wk", "L1_gnn_Wv", "L1_gnn_Wo",
        "L1_gnn_bo", "L1_gnn_g2", "L1_gnn_be2", "L1_gnn_W1", "L1_gnn_b1", "L1_gnn_W2", "L1_gnn_b2", "L1_gnn_g3",
        "L1_gnn_be3"]


def kernel(**inputs):
    import numpy as _np
    import concourse.bacc as _bacc
    from concourse import mybir as _mybir
    from concourse.bass_utils import run_bass_kernel_spmd as _run

    nc = _bacc.Bacc("TRN2", target_bir_lowering=False, num_devices=1)
    arrays, args = {}, []
    for name in _INS:
        a = _np.ascontiguousarray(inputs[name])
        arrays[f"in_{name}_dram"] = a
        args.append(nc.dram_tensor(f"in_{name}_dram", a.shape, _mybir.dt.from_np(a.dtype), kind="ExternalInput").ap())
    args.append(nc.dram_tensor("out_dram", (BATCH, N, D), _mybir.dt.float32, kind="ExternalOutput").ap())
    two_layers(nc, *args)
    return _run(nc, [arrays], core_ids=[0]).results[0]["out_dram"]
```

```python
from contextlib import ExitStack
from math import comb

import concourse.bass as bass
from concourse import mybir

F32 = mybir.dt.float32
F32R = mybir.dt.float32r
BF16 = mybir.dt.bfloat16
ALU = mybir.AluOpType
ACT = mybir.ActivationFunctionType
AX = mybir.AxisListType

BATCH, N, D = 16, 512, 128
P = 128
NT = N // P
STEPS = 8
DT = 1.0 / STEPS
HEADS = 4
HD = D // HEADS
HID = 2 * D
HT = HID // P
EPS = 1e-5
GROUP = 3
MASKED = 1e30
TINY = 1e-15
UNITS = NT * HEADS
assert (STEPS + 1) == GROUP * GROUP and BATCH % 2 == 0


def at_least(eng, semaphore, value):
    if isinstance(value, int) and value <= 0:
        return
    eng.wait_ge(semaphore, value)


def rounds(eng, body, first_full, after_full, last):
    for r in range(first_full):
        body(r, r % 2, r // 2)
    with eng.Fori(first_full // 2, after_full // 2) as half:
        body(2 * half, 0, half)
        body(2 * half + 1, 1, half)
    for r in range(after_full, last):
        body(r, r % 2, r // 2)


def within(r, low, high):
    return low <= r <= high if isinstance(r, int) else True


def two_layers(nc, x, adj, alpha, w, d, fc_w, fc_b, Wc, bc, g1, be1, Wq, Wk, Wv, Wo, bo, g2, be2, W1, b1, W2, b2,
               g3, be3, out):
    x_dram = x.rearrange("b (t p) d -> p b t d", p=P)
    out_dram = out.rearrange("b (t p) d -> p b t d", p=P)

    with ExitStack() as whole:
        def tensor(ctx, name, shape, dt=F32):
            return ctx.enter_context(nc.sbuf_tensor(name, shape, dt))

        def sem(name):
            return whole.enter_context(nc.semaphore(name))

        psum = [whole.enter_context(nc.psum_tensor(f"bank{i}", [P, N], F32)) for i in range(8)]

        waited = (sem("dve_waited"), sem("pool_waited"))

        y = tensor(whole, "y", [P, BATCH * N])
        adjT = tensor(whole, "adjT", [P, NT, N])
        mask = tensor(whole, "mask", [P, NT, N], BF16)
        ident = tensor(whole, "ident", [P, P])
        ones = tensor(whole, "ones", [P, P])
        exponent = tensor(whole, "exponent", [P, NT])
        two_over_lam = tensor(whole, "two_over_lam", [P, 1])

        layer0(nc, whole, tensor, sem, psum, x_dram, adj, alpha, w, d, fc_w, fc_b,
               y, adjT, mask, ident, ones, exponent, two_over_lam, waited)
        layer1(nc, whole, tensor, sem, psum, Wc, bc, g1, be1, Wq, Wk, Wv, Wo, bo, g2, be2, W1, b1, W2, b2, g3, be3,
               out_dram, y, adjT, mask, ident, ones, exponent, two_over_lam, waited)


def layer0(nc, whole, tensor, sem, psum, x_dram, adj, alpha, w, d, fc_w, fc_b,
           y, adjT, mask, ident, ones, exponent, two_over_lam, waited):
    dve_waited, pool_waited = waited
    with ExitStack() as ctx:
        def sb(name, shape, dt=F32):
            return tensor(ctx, name, shape, dt)

        A = sb("A", [P, NT, N])
        alpha_in = sb("alpha_in", [P, NT])
        w_in = sb("w_in", [P, D])
        d_in = sb("d_in", [P, 1])
        fc_in = sb("fc_in", [P, D])
        b_in = sb("b_in", [P, 1])
        Pn = sb("Pn", [P, NT, N])
        PT = sb("PT", [P, NT, N])
        P2T = sb("P2T", [P, NT, N])
        P3T = sb("P3T", [P, NT, N])
        a_exp = sb("a_exp", [P, NT])
        a_one = sb("a_one", [P, NT])
        a_sig = sb("a_sig", [P, NT])
        edge_scale = sb("edge_scale", [P, NT])
        self_scale = sb("self_scale", [P, NT])
        wT = sb("wT", [P, D])
        d_clip = sb("d_clip", [P, 1])
        d_dt = sb("d_dt", [P, 1])
        dwT = sb("dwT", [P, D])
        powers = sb("powers", [P, STEPS + 1, D + 1])
        W = powers[:, 1, 0:D]
        B = sb("B", [P, GROUP, GROUP, D])
        U = sb("U", [P, NT, STEPS + 1])
        beta = sb("beta", [P, STEPS + 1])
        U_rows = sb("U_rows", [STEPS + 1, N])
        beta_rows = sb("beta_rows", [STEPS + 1, D])
        bias = sb("bias", [P, NT, D])
        S = sb("S", [P, NT, N])
        Sq = [sb(f"Sq{i}", [P, NT, N], F32R) for i in range(2)]
        row_sum = sb("row_sum", [P, 1])
        shift = sb("shift", [P, 1])
        diagonal = sb("diagonal", [P, NT, D], BF16)
        trace_part = sb("trace_part", [P, 1])
        trace = sb("trace", [P, 1])
        trace_inv = sb("trace_inv", [P, 1])
        trace_inv2 = sb("trace_inv2", [P, 1])
        v = sb("v", [P, NT])
        Sv = sb("Sv", [P, NT])
        scratch4 = sb("scratch4", [P, NT])
        quotient = sb("quotient", [P, 2])
        quotient_all = sb("quotient_all", [P, 2])
        den_inv = sb("den_inv", [P, 1])
        lam = sb("lam", [P, 1])
        lam_inv = sb("lam_inv", [P, 1])
        x_in = [sb(f"x_in{i}", [P, NT, D]) for i in range(2)]
        stats = sb("stats", [P, NT, 6])
        mv = [sb(f"mv{i}", [P, NT, 2]) for i in range(2)]
        var_eps = [sb(f"var_eps{i}", [P, NT]) for i in range(2)]
        rstd = [sb(f"rstd{i}", [P, NT]) for i in range(2)]
        mean_rstd = [sb(f"mean_rstd{i}", [P, NT]) for i in range(2)]
        shift_ln = [sb(f"shift_ln{i}", [P, NT]) for i in range(2)]
        x0 = [sb(f"x0_{i}", [P, NT, D]) for i in range(2)]
        x_bias = [sb(f"x_bias{i}", [P, NT, D]) for i in range(2)]
        T = [[sb(f"T{m}_{i}", [P, N]) for m in range(GROUP)] for i in range(2)]
        C2 = sb("C2", [P, NT, D])
        Y1 = sb("Y1", [P, NT, D])

        loaded = sem("adj_loaded")
        small_loaded = sem("small_loaded")
        x_loaded = [sem(f"x_loaded{i}") for i in range(2)]
        consts_set = sem("consts_set")
        alpha_exp = sem("alpha_exp")
        dve_setup = sem("dve_setup")
        ident_ready = sem("ident_ready")
        P_ready = sem("P_ready")
        PT_psum = sem("PT_psum")
        PT_ready = sem("PT_ready")
        adjT_psum = sem("adjT_psum")
        adjT_ready = sem("adjT_ready")
        wT_psum = sem("wT_psum")
        wT_ready = sem("wT_ready")
        weff_psum = sem("weff_psum")
        power_psum = sem("power_psum")
        power_ready = sem("power_ready")
        FW_psum = sem("FW_psum")
        B_step = sem("B_step")
        P2_psum = sem("P2_psum")
        P2_ready = sem("P2_ready")
        P3_psum = sem("P3_psum")
        P3_ready = sem("P3_ready")
        U_psum = sem("U_psum")
        U_ready = sem("U_ready")
        beta_ready = sem("beta_ready")
        rows_psum = sem("rows_psum")
        rows_ready = sem("rows_ready")
        bias_psum = sem("bias_psum")
        bias_ready = sem("bias_ready")
        S_ready = sem("S_ready")
        sum_psum = sem("sum_psum")
        S0_ready = sem("S0_ready")
        trace_part_ready = sem("trace_part_ready")
        trace_psum = sem("trace_psum")
        trace_step = sem("trace_step")
        square_psum = sem("square_psum")
        square_ready = sem("square_ready")
        v_ready = sem("v_ready")
        Sv_psum = sem("Sv_psum")
        Sv_step = sem("Sv_step")
        quotient_psum = sem("quotient_psum")
        lam_step = sem("lam_step")
        stats_ready = sem("stats_ready")
        mv_ready = sem("mv_ready")
        ln_pool = sem("ln_pool")
        x0_ready = sem("x0_ready")
        x_bias_ready = sem("x_bias_ready")
        T_psum = [sem(f"T{m}_psum") for m in range(GROUP)]
        T_ready = [sem(f"T{m}_ready") for m in range(GROUP)]
        C_psum = sem("C_psum")
        C2_ready = sem("C2_ready")
        Y1_psum = sem("Y1_psum")
        Y1_ready = sem("Y1_ready")
        Y0_psum = sem("Y0_psum")
        y_ready = sem("y_ready")

        SQ_BANK = psum[7]
        ident_tiles = ident[:, :].unsqueeze(1).broadcast_to([P, NT, D])
        n_B = sum(STEPS - j for j in range(STEPS))

        def diagonal_of(tile):
            a = tile[:, :, 0:D]
            step = list(map(list, a.ap))
            step[1][0] += D
            return bass.AP(tensor=a.tensor, offset=a.offset, ap=step)

        with nc.Block() as block:

            @block.sync
            def _(sp):
                adj_tiles = adj.rearrange("(t p) m -> p t m", p=P)
                for t in range(NT):
                    sp.dma_start(A[:, t, :], adj_tiles[:, t, :]).then_inc(loaded, 16)
                sp.dma_start(alpha_in[:, :], alpha.rearrange("(t p) -> p t", p=P),
                             allow_slow_non_contiguous=True).then_inc(small_loaded, 16)
                sp.dma_start(w_in[:, :], w).then_inc(small_loaded, 16)
                sp.dma_start(fc_in[:, :], fc_w).then_inc(small_loaded, 16)
                sp.dma_start(d_in[:, :], d.rearrange("(p o) -> p o", o=1)).then_inc(small_loaded, 16)
                sp.dma_start(b_in[:, :], fc_b.rearrange("(p o) -> p o", o=1)).then_inc(small_loaded, 16)

                def load_x(b, s, half):
                    at_least(sp, x0_ready, b - 1)
                    at_least(sp, x_bias_ready, b - 1)
                    sp.dma_start(x_in[s][:, :, :], x_dram[:, bass.ds(b, 1), :, :].rearrange("p b t d -> p (b t) d")
                                 ).then_inc(x_loaded[s], 16)
                rounds(sp, load_x, 2, BATCH, BATCH)

            @block.gpsimd
            def _(pool):
                pool.memset(ident[:, :], 0.0).then_inc(consts_set, 1)
                pool.memset(ones[:, :], 1.0).then_inc(consts_set, 1)
                pool.memset(exponent[:, :], -0.5).then_inc(consts_set, 1)
                pool.wait_ge(consts_set, 1)
                pool.affine_select(out=ident[:, :], in_=ident[:, :], compare_op=ALU.not_equal, fill=1.0, base=0,
                                   pattern=[[-1, P]], channel_multiplier=1).then_inc(ident_ready, 1)

                def ln_and_residual(b, s, half):
                    pool.wait_ge(mv_ready, b + 1)
                    at_least(pool, x0_ready, b - 1)
                    pool.sem_inc(pool_waited, 1)
                    pool.tensor_scalar(var_eps[s][:, :], mv[s][:, :, 1], EPS, None, ALU.add).then_inc(ln_pool, 1)
                    pool.wait_ge(consts_set, 3)
                    pool.wait_ge(ln_pool, 4 * b + 1)
                    pool.tensor_tensor(out=rstd[s][:, :], in0=var_eps[s][:, :], in1=exponent[:, :],
                                       op=ALU.pow).then_inc(ln_pool, 1)
                    pool.wait_ge(ln_pool, 4 * b + 2)
                    pool.tensor_tensor(out=mean_rstd[s][:, :], in0=mv[s][:, :, 0], in1=rstd[s][:, :],
                                       op=ALU.mult).then_inc(ln_pool, 1)
                    pool.wait_ge(ln_pool, 4 * b + 3)
                    pool.sem_inc(pool_waited, 1)
                    pool.tensor_scalar(shift_ln[s][:, :], mean_rstd[s][:, :], -1.0, None,
                                       ALU.mult).then_inc(ln_pool, 1)
                    pool.wait_ge(bias_ready, 1)
                    at_least(pool, y_ready, NT * (b - 1))
                    pool.tensor_tensor(out=x_bias[s][:, :, :], in0=x_in[s][:, :, :], in1=bias[:, :, :],
                                       op=ALU.add).then_inc(x_bias_ready, 1)
                rounds(pool, ln_and_residual, 2, BATCH, BATCH)

            @block.tensor
            def _(pe):
                pe.wait_ge(ident_ready, 1)
                pe.wait_ge(loaded, 16 * NT)
                for mt in range(NT):
                    for nt in range(NT):
                        last = pe.transpose(psum[mt][:, nt * P:(nt + 1) * P], A[:, nt, mt * P:(mt + 1) * P],
                                            ident[:, :])
                    last.then_inc(adjT_psum, 1)
                pe.wait_ge(small_loaded, 16 * 5)
                pe.transpose(psum[4][:, 0:D], w_in[:, :], ident[:, :]).then_inc(wT_psum, 1)
                pe.wait_ge(wT_ready, 2)
                pe.matmul(psum[5][:, 0:D], wT[:, :], dwT[:, :], start=True, stop=True).then_inc(weff_psum, 1)
                pe.wait_ge(P_ready, 2 * NT)
                for mt in range(NT):
                    pe.wait_ge(adjT_ready, mt + 1)
                    for nt in range(NT):
                        last = pe.transpose(psum[mt][:, nt * P:(nt + 1) * P], Pn[:, nt, mt * P:(mt + 1) * P],
                                            ident[:, :])
                    last.then_inc(PT_psum, 1)
                for k in range(1, STEPS + 1):
                    pe.wait_ge(power_ready, k)
                    pe.matmul(psum[5][:, 0:D + 1], W, powers[:, k - 1, :], start=True,
                              stop=True).then_inc(power_psum, 1)
                pe.wait_ge(PT_ready, NT)
                for mt in range(NT):
                    for k in range(NT):
                        last = pe.matmul(psum[mt][:, :], Pn[:, k, mt * P:(mt + 1) * P], PT[:, k, :],
                                         start=k == 0, stop=k == NT - 1)
                    last.then_inc(P2_psum, 1)
                pe.wait_ge(power_ready, STEPS + 1)
                for k in range(STEPS + 1):
                    last = pe.matmul(psum[4 + k // NT][:, k % NT * D:(k % NT + 1) * D], fc_in[:, :],
                                     powers[:, k, 0:D], start=True, stop=True)
                last.then_inc(FW_psum, 1)
                pe.wait_ge(P2_ready, NT)
                for mt in range(NT):
                    for k in range(NT):
                        last = pe.matmul(psum[mt][:, :], Pn[:, k, mt * P:(mt + 1) * P], P2T[:, k, :],
                                         start=k == 0, stop=k == NT - 1)
                    last.then_inc(P3_psum, 1)
                pe.wait_ge(S_ready, 2)
                pe.matmul(SQ_BANK[:, 0:1], ones[:, :], row_sum[:, :], start=True, stop=True).then_inc(sum_psum, 1)
                pe.wait_ge(P3_ready, NT)
                for g in range(GROUP):
                    pe.wait_ge(U_ready, g + 1)
                    for nt in range(NT):
                        if g == 0:
                            for j, op in enumerate((PT, P2T, P3T)):
                                for k in range(NT):
                                    last = pe.matmul(psum[0][:, 4 * nt + j:4 * nt + j + 1],
                                                     op[:, k, nt * P:(nt + 1) * P], U[:, k, 0:1],
                                                     start=k == 0, stop=k == NT - 1)
                        else:
                            n_cols = 3 if g == 1 else 2
                            for k in range(NT):
                                last = pe.matmul(psum[0][:, 4 * nt:4 * nt + n_cols],
                                                 P3T[:, k, nt * P:(nt + 1) * P],
                                                 U[:, k, 3 * g - 2:3 * g - 2 + n_cols],
                                                 start=k == 0, stop=k == NT - 1)
                    last.then_inc(U_psum, 1)
                pe.wait_ge(U_ready, GROUP + 1)
                pe.wait_ge(beta_ready, STEPS + 1)
                for nt in range(NT):
                    pe.transpose(psum[1][0:STEPS + 1, nt * P:(nt + 1) * P], U[:, nt, :], ident[:, :])
                pe.transpose(psum[2][0:STEPS + 1, 0:D], beta[:, :], ident[:, :]).then_inc(rows_psum, 1)
                pe.wait_ge(rows_ready, 2)
                for nt in range(NT):
                    last = pe.matmul(psum[3][:, nt * D:(nt + 1) * D], U_rows[:, nt * P:(nt + 1) * P],
                                     beta_rows[:, :], start=True, stop=True)
                last.then_inc(bias_psum, 1)
                pe.wait_ge(B_step, STEPS + 1 + n_B)
                pe.wait_ge(bias_ready, 1)

                def square(r, s, mt):
                    if mt == 0:
                        pe.wait_ge(trace_step, 3 * r + 1)
                    else:
                        pe.wait_ge(square_ready, NT * r + mt)
                    for k in range(NT):
                        last = pe.matmul(SQ_BANK[:, :], Sq[s][:, k, mt * P:(mt + 1) * P], Sq[s][:, k, :],
                                         start=k == 0, stop=k == NT - 1)
                    last.then_inc(square_psum, 1)

                def round_(r, s, half):
                    enters, leaves, squares = within(r, 0, BATCH - 1), within(r, 1, BATCH), within(r, 0, BATCH - 1)
                    if leaves:
                        for m in range(GROUP):
                            pe.wait_ge(T_ready[m], r)
                        for nt in range(NT):
                            at_least(pe, y_ready, NT * (r - 2) + nt + 1)
                            for m in range(GROUP):
                                last = pe.matmul(psum[nt][:, 0:GROUP * D], T[1 - s][m][:, nt * P:(nt + 1) * P],
                                                 B[:, m, :, :].rearrange("p i d -> p (i d)"),
                                                 start=m == 0, stop=m == GROUP - 1, skip_group_check=True)
                            last.then_inc(C_psum, 1)
                    if squares:
                        pe.wait_ge(trace_part_ready, r + 1)
                        pe.matmul(SQ_BANK[:, 0:1], ones[:, :], trace_part[:, :], start=True,
                                  stop=True).then_inc(trace_psum, 1)
                    if enters:
                        pe.wait_ge(x0_ready, r + 1)
                        at_least(pe, T_ready[0], r)
                        for nt in range(NT):
                            last = pe.transpose(psum[4][:, nt * P:(nt + 1) * P], x0[s][:, nt, :], ident[:, :])
                        last.then_inc(T_psum[0], 1)
                        at_least(pe, T_ready[1], r)
                        for k in range(NT):
                            last = pe.matmul(psum[5][:, :], x0[s][:, k, :], PT[:, k, :],
                                             start=k == 0, stop=k == NT - 1)
                        last.then_inc(T_psum[1], 1)
                    if squares:
                        square(r, s, 0)
                    if leaves:
                        pe.wait_ge(C2_ready, NT * r)
                        for nt in range(NT):
                            for k in range(NT):
                                last = pe.matmul(psum[nt][:, D:2 * D], P3T[:, k, nt * P:(nt + 1) * P], C2[:, k, :],
                                                 start=False, stop=k == NT - 1, skip_group_check=True)
                            last.then_inc(Y1_psum, 1)
                    if squares:
                        square(r, s, 1)
                    if enters:
                        at_least(pe, T_ready[2], r)
                        for k in range(NT):
                            last = pe.matmul(psum[6][:, :], x0[s][:, k, :], P2T[:, k, :],
                                             start=k == 0, stop=k == NT - 1)
                        last.then_inc(T_psum[2], 1)
                    if squares:
                        square(r, s, 2)
                    if leaves:
                        pe.wait_ge(Y1_ready, NT * r)
                        for nt in range(NT):
                            for k in range(NT):
                                last = pe.matmul(psum[nt][:, 0:D], P3T[:, k, nt * P:(nt + 1) * P], Y1[:, k, :],
                                                 start=False, stop=k == NT - 1, skip_group_check=True)
                            last.then_inc(Y0_psum, 1)
                    if squares:
                        square(r, s, 3)
                rounds(pe, round_, 2, BATCH, BATCH + 1)

                pe.wait_ge(v_ready, 1)
                for nt in range(NT):
                    for k in range(NT):
                        last = pe.matmul(psum[4][:, nt:nt + 1], S[:, k, nt * P:(nt + 1) * P], v[:, k:k + 1],
                                         start=k == 0, stop=k == NT - 1)
                last.then_inc(Sv_psum, 1)
                pe.wait_ge(Sv_step, 3)
                pe.matmul(psum[5][:, 0:2], ones[:, :], quotient[:, :], start=True,
                          stop=True).then_inc(quotient_psum, 1)

            @block.scalar
            def _(act):
                act.wait_ge(small_loaded, 16 * 5)
                act.activation(a_exp[:, :], alpha_in[:, :], ACT.Exp, scale=-1.0).then_inc(alpha_exp, 1)
                for mt in range(NT):
                    act.wait_ge(adjT_psum, mt + 1)
                    act.activation(adjT[:, mt, :], psum[mt][:, :], ACT.Copy).then_inc(adjT_ready, 1)
                for mt in range(NT):
                    act.wait_ge(PT_psum, mt + 1)
                    act.activation(PT[:, mt, :], psum[mt][:, :], ACT.Copy).then_inc(PT_ready, 1)
                for mt in range(NT):
                    act.wait_ge(P2_psum, mt + 1)
                    act.activation(P2T[:, mt, :], psum[mt][:, :], ACT.Copy).then_inc(P2_ready, 1)
                for mt in range(NT):
                    act.wait_ge(P3_psum, mt + 1)
                    act.activation(P3T[:, mt, :], psum[mt][:, :], ACT.Copy).then_inc(P3_ready, 1)

                def square_out(r, s, mt):
                    act.wait_ge(square_psum, NT * r + mt + 1)
                    if mt == 0:
                        act.wait_ge(trace_step, 3 * r + 3)
                    act.activation(Sq[1 - s][:, mt, :], SQ_BANK[:, :], ACT.Copy,
                                   scale=trace_inv2[:, 0:1]).then_inc(square_ready, 1)

                def round_(r, s, half):
                    enters, leaves, squares = within(r, 0, BATCH - 1), within(r, 1, BATCH), within(r, 0, BATCH - 1)
                    if enters:
                        act.wait_ge(ln_pool, 4 * r + 4)
                        at_least(act, T_psum[2], r - 1)
                        for t in range(NT):
                            last = act.activation(x0[s][:, t, :], x_in[s][:, t, :], ACT.Relu,
                                                  scale=rstd[s][:, t:t + 1], bias=shift_ln[s][:, t:t + 1])
                        last.then_inc(x0_ready, 1)
                    if leaves:
                        for nt in range(NT):
                            act.wait_ge(C_psum, NT * (r - 1) + nt + 1)
                            act.activation(C2[:, nt, :], psum[nt][:, 2 * D:3 * D], ACT.Copy).then_inc(C2_ready, 1)
                    if enters:
                        act.wait_ge(T_psum[1], r + 1)
                        act.activation(T[s][1][:, :], psum[5][:, :], ACT.Copy).then_inc(T_ready[1], 1)
                    if squares:
                        square_out(r, s, 0)
                    if leaves:
                        for nt in range(NT):
                            act.wait_ge(Y1_psum, NT * (r - 1) + nt + 1)
                            act.activation(Y1[:, nt, :], psum[nt][:, D:2 * D], ACT.Copy).then_inc(Y1_ready, 1)
                    if squares:
                        for mt in range(1, NT):
                            square_out(r, s, mt)
                rounds(act, round_, 2, BATCH, BATCH + 1)

            @block.vector
            def _(dve):
                dve.wait_ge(alpha_exp, 1)
                dve.tensor_scalar(a_one[:, :], a_exp[:, :], 1.0, None, ALU.add).then_inc(dve_setup, 1)
                dve.wait_ge(dve_setup, 1)
                dve.reciprocal(a_sig[:, :], a_one[:, :]).then_inc(dve_setup, 1)
                dve.wait_ge(dve_setup, 2)
                dve.tensor_scalar(edge_scale[:, :], a_sig[:, :], 0.5 * DT, None, ALU.mult).then_inc(dve_setup, 1)
                dve.tensor_scalar(self_scale[:, :], a_sig[:, :], -0.5 * DT, 1.0 - DT, ALU.mult,
                                  ALU.add).then_inc(dve_setup, 1)
                dve.wait_ge(dve_setup, 4)
                dve.wait_ge(ident_ready, 1)
                dve.wait_ge(loaded, 16 * NT)
                for t in range(NT):
                    dve.tensor_scalar(Pn[:, t, :], A[:, t, :], edge_scale[:, t:t + 1], None,
                                      ALU.mult).then_inc(P_ready, 1)
                for t in range(NT):
                    block_t = Pn[:, t, t * P:(t + 1) * P]
                    dve.wait_ge(P_ready, NT)
                    dve.scalar_tensor_tensor(out=block_t, in0=ident[:, :], scalar=self_scale[:, t:t + 1],
                                             in1=block_t, op0=ALU.mult, op1=ALU.add).then_inc(P_ready, 1)
                dve.tensor_scalar(d_clip[:, :], d_in[:, :], 0.0, 1.0, ALU.max, ALU.min).then_inc(dve_setup, 1)
                dve.wait_ge(dve_setup, 5)
                dve.tensor_scalar(d_dt[:, :], d_clip[:, :], DT, None, ALU.mult).then_inc(dve_setup, 1)
                dve.wait_ge(dve_setup, 6)
                dve.wait_ge(wT_psum, 1)
                dve.tensor_copy(wT[:, :], psum[4][:, 0:D]).then_inc(wT_ready, 1)
                dve.tensor_scalar(dwT[:, :], psum[4][:, 0:D], d_dt[:, 0:1], None, ALU.mult).then_inc(wT_ready, 1)
                dve.tensor_copy(powers[:, 0, 0:D], ident[:, :])
                dve.tensor_copy(powers[:, 0, D:D + 1], b_in[:, :])
                dve.wait_ge(weff_psum, 1)
                dve.tensor_copy(W, psum[5][:, 0:D]).then_inc(power_ready, 1)
                dve.wait_ge(power_psum, 1)
                dve.tensor_copy(powers[:, 1, D:D + 1], psum[5][:, D:D + 1]).then_inc(power_ready, 1)
                for k in range(2, STEPS + 1):
                    dve.wait_ge(power_psum, k)
                    dve.tensor_copy(powers[:, k, :], psum[5][:, 0:D + 1]).then_inc(power_ready, 1)
                dve.memset(U[:, :, 0:1], 1.0).then_inc(U_ready, 1)
                dve.wait_ge(power_ready, STEPS + 1)
                for j in range(STEPS + 1):
                    dve.tensor_scalar(beta[:, j:j + 1], powers[:, STEPS - j, D:D + 1], float(comb(STEPS, j)), None,
                                      ALU.mult).then_inc(beta_ready, 1)
                dve.wait_ge(adjT_ready, NT)
                dve.tensor_tensor(out=S[:, :, :], in0=A[:, :, :], in1=adjT[:, :, :], op=ALU.add).then_inc(S_ready, 1)
                dve.wait_ge(S_ready, 1)
                dve.tensor_reduce(row_sum[:, :], S[:, :, :].rearrange("p t n -> p (t n)"), AX.X,
                                  ALU.add).then_inc(S_ready, 1)
                dve.tensor_scalar(mask[:, :, :], A[:, :, :], 0.0, MASKED, ALU.is_le, ALU.mult).then_inc(S_ready, 1)
                dve.wait_ge(FW_psum, 1)
                at = {}
                count = 0
                for j in range(STEPS + 1):
                    k = STEPS - j
                    count += 1
                    at[j] = count
                    dve.tensor_scalar(B[:, j % GROUP, j // GROUP, :], psum[4 + k // NT][:, k % NT * D:(k % NT + 1) * D],
                                      float(comb(STEPS, j)), None, ALU.mult).then_inc(B_step, 1)
                for i in range(STEPS):
                    for j in range(STEPS - i):
                        dve.wait_ge(B_step, at[j])
                        count += 1
                        at[j] = count
                        Bj = B[:, j % GROUP, j // GROUP, :]
                        dve.scalar_tensor_tensor(out=Bj, in0=powers[:, i, 0:D], scalar=DT * comb(i + j, j), in1=Bj,
                                                 op0=ALU.mult, op1=ALU.add).then_inc(B_step, 1)
                dve.wait_ge(sum_psum, 1)
                dve.tensor_scalar(shift[:, :], SQ_BANK[:, 0:1], 0.5 / N, TINY, ALU.mult,
                                  ALU.add).then_inc(S0_ready, 1)
                dve.tensor_scalar(S[:, :, :], S[:, :, :], 0.5, None, ALU.mult).then_inc(S0_ready, 1)
                dve.wait_ge(S0_ready, 2)
                dve.tensor_copy(Sq[0][:, :, :], S[:, :, :]).then_inc(S0_ready, 1)
                dve.wait_ge(S0_ready, 3)
                for t in range(NT):
                    dve.scalar_tensor_tensor(out=Sq[0][:, t, t * P:(t + 1) * P], in0=ident[:, :],
                                             scalar=shift[:, 0:1], in1=S[:, t, t * P:(t + 1) * P],
                                             op0=ALU.mult, op1=ALU.add).then_inc(S0_ready, 1)
                dve.wait_ge(S0_ready, 3 + NT)
                dve.tensor_tensor_reduce(diagonal[:, :, :], diagonal_of(Sq[0]).bitcast(F32), ident_tiles, 1.0, 0.0, ALU.mult,
                                         ALU.add, trace_part[:, :]).then_inc(trace_part_ready, 1)
                for g in range(GROUP):
                    n_cols = 2 if g == 2 else 3
                    dve.wait_ge(U_psum, g + 1)
                    dve.tensor_copy(U[:, :, 3 * g + 1:3 * g + 1 + n_cols],
                                    psum[0][:, 0:4 * NT].rearrange("p (t c) -> p t c", c=4)[:, :, 0:n_cols]
                                    ).then_inc(U_ready, 1)
                dve.wait_ge(rows_psum, 1)
                dve.tensor_copy(U_rows[:, :], psum[1][0:STEPS + 1, :]).then_inc(rows_ready, 1)
                dve.tensor_copy(beta_rows[:, :], psum[2][0:STEPS + 1, 0:D]).then_inc(rows_ready, 1)
                dve.wait_ge(bias_psum, 1)
                dve.tensor_copy(bias[:, :, :].rearrange("p t d -> p (t d)"), psum[3][:, :]).then_inc(bias_ready, 1)

                def round_(r, s, half):
                    enters, leaves, squares = within(r, 0, BATCH - 1), within(r, 1, BATCH), within(r, 0, BATCH - 1)
                    if enters:
                        dve.wait_ge(x_loaded[s], 16 * (half + 1))
                        at_least(dve, mv_ready, r)
                        for t in range(NT):
                            last = dve.bn_stats(stats[:, t, :], x_in[s][:, t, :])
                        last.then_inc(stats_ready, 1)
                        dve.wait_ge(stats_ready, r + 1)
                        at_least(dve, ln_pool, 4 * (r - 1))
                        dve.sem_inc(dve_waited, 1)
                        for t in range(NT):
                            last = dve.bn_aggr(mv[s][:, t, :], stats[:, t, :])
                        last.then_inc(mv_ready, 1)
                    if squares:
                        dve.wait_ge(trace_psum, r + 1)
                        dve.tensor_scalar(trace[:, :], SQ_BANK[:, 0:1], TINY, None, ALU.max).then_inc(trace_step, 1)
                        dve.wait_ge(trace_step, 3 * r + 1)
                        dve.reciprocal(trace_inv[:, :], trace[:, :]).then_inc(trace_step, 1)
                        dve.wait_ge(trace_step, 3 * r + 2)
                        at_least(dve, square_ready, NT * r)
                        dve.tensor_tensor(out=trace_inv2[:, :], in0=trace_inv[:, :], in1=trace_inv[:, :],
                                          op=ALU.mult).then_inc(trace_step, 1)
                    if enters:
                        dve.wait_ge(T_psum[0], r + 1)
                        dve.tensor_copy(T[s][0][:, :], psum[4][:, :]).then_inc(T_ready[0], 1)
                        dve.wait_ge(T_psum[2], r + 1)
                        dve.tensor_copy(T[s][2][:, :], psum[6][:, :]).then_inc(T_ready[2], 1)
                    if leaves:
                        dve.wait_ge(x_bias_ready, r)
                        for nt in range(NT):
                            dve.wait_ge(Y0_psum, NT * (r - 1) + nt + 1)
                            dve.tensor_tensor(out=y[:, bass.ds((r - 1) * N + nt * D, D)], in0=psum[nt][:, 0:D],
                                              in1=x_bias[1 - s][:, nt, :], op=ALU.add).then_inc(y_ready, 1)
                    if squares:
                        dve.wait_ge(square_ready, NT * (r + 1))
                        dve.tensor_tensor_reduce(diagonal[:, :, :], diagonal_of(Sq[1 - s]).bitcast(F32), ident_tiles, 1.0, 0.0,
                                                 ALU.mult, ALU.add, trace_part[:, :]).then_inc(trace_part_ready, 1)
                rounds(dve, round_, 2, BATCH, BATCH + 1)

                dve.tensor_reduce(v[:, :], Sq[0][:, :, :].bitcast(F32), AX.X, ALU.add).then_inc(v_ready, 1)
                dve.wait_ge(Sv_psum, 1)
                dve.tensor_copy(Sv[:, :], psum[4][:, 0:NT]).then_inc(Sv_step, 1)
                dve.wait_ge(Sv_step, 1)
                dve.tensor_tensor_reduce(scratch4[:, :], v[:, :], Sv[:, :], 1.0, 0.0, ALU.mult, ALU.add,
                                         quotient[:, 0:1]).then_inc(Sv_step, 1)
                dve.wait_ge(Sv_step, 2)
                dve.tensor_tensor_reduce(scratch4[:, :], v[:, :], v[:, :], 1.0, 0.0, ALU.mult, ALU.add,
                                         quotient[:, 1:2]).then_inc(Sv_step, 1)
                dve.wait_ge(quotient_psum, 1)
                dve.tensor_scalar(quotient_all[:, :], psum[5][:, 0:2], TINY, None, ALU.max).then_inc(lam_step, 1)
                dve.wait_ge(lam_step, 1)
                dve.reciprocal(den_inv[:, :], quotient_all[:, 1:2]).then_inc(lam_step, 1)
                dve.wait_ge(lam_step, 2)
                dve.tensor_scalar(lam[:, :], quotient_all[:, 0:1], den_inv[:, 0:1], 1e-8, ALU.mult,
                                  ALU.add).then_inc(lam_step, 1)
                dve.wait_ge(lam_step, 3)
                dve.reciprocal(lam_inv[:, :], lam[:, :]).then_inc(lam_step, 1)
                dve.wait_ge(lam_step, 4)
                dve.tensor_scalar(two_over_lam[:, :], lam_inv[:, :], 2.0, None, ALU.mult).then_inc(lam_step, 1)
                dve.wait_ge(lam_step, 5)
                dve.tensor_scalar(adjT[:, :, :], adjT[:, :, :], two_over_lam[:, 0:1], None,
                                  ALU.mult).then_inc(lam_step, 1)
                dve.wait_ge(lam_step, 6)
                for t in range(NT):
                    own = adjT[:, t, t * P:(t + 1) * P]
                    last = dve.tensor_tensor(out=own, in0=own, in1=ident[:, :], op=ALU.subtract)
                last.then_inc(lam_step, 1)


AT_X1, AT_X1T, AT_X1T_OUT, AT_K, AT_Q, AT_K_HI, AT_Q_HI, AT_K_LO, AT_Q_LO = 1, 2, 3, 4, 5, 5, 6, 6, 7
AT_V, AT_V_OUT = 13, 14
AT_CONV, AT_CONV_OUT, AT_Z, AT_Z_OUT, AT_Z_MOMENTS, AT_Z_STD = 5, 9, 10, 11, 12, 14
AT_Y_MOMENTS, AT_H = 9, 12
AT_RINV, AT_SPREAD, AT_SPREAD_OUT, AT_O, AT_PROJ, AT_Z2, AT_Z2_MOMENTS, AT_Z2_STD = 0, 2, 2, 8, 10, 11, 13, 15
TURN_LAG = 3
VALUES_LAG = 8
DVE_COPIES = (0, 1, 2, 7, 15)
RING = 8
TURNED = 8
STACKS = 4
ROWS = 9


def copied(by_dve, batch, unit):
    mine = [u for u in range(UNITS) if (u in DVE_COPIES) == by_dve]
    return len(mine) * batch + sum(u <= unit for u in mine)


def layer1(nc, whole, tensor, sem, psum, Wc, bc, g1, be1, Wq, Wk, Wv, Wo, bo, g2, be2, W1, b1, W2, b2, g3, be3,
           out_dram, y, adjT, mask, ident, ones, exponent, two_over_lam, waited):
    dve_waited, pool_waited = waited
    Lnorm = adjT
    x2 = tensor(whole, "x2", [P, BATCH * N])
    bc_all = tensor(whole, "bc_all", [P, ROWS, D])
    BC, G1, BE1, BO, G2, BE2, B2, G3, BE3 = range(ROWS)
    W1s = tensor(whole, "W1s", [P, HID])
    W2s = tensor(whole, "W2s", [P, HT, D])
    b1s = tensor(whole, "b1s", [P, HT])
    mlp_loaded = sem("mlp_loaded")

    def all_tiles(row):
        return bc_all[:, row:row + 1, :].broadcast_to([P, NT, D])

    def flat(t):
        return t[:, :, :].rearrange("p t d -> p (t d)")

    with ExitStack() as ctx:
        def sb(name, shape, dt=F32):
            return tensor(ctx, name, shape, dt)

        row_in = sb("row_in", [1, ROWS, D])
        Wcs, Wqs, Wks, Wvs, Wos = (sb(f"W_{n}", [P, D]) for n in "cqkvo")
        stats_a, stats_b, stats_c = (sb(f"stats_{n}", [P, NT, 6]) for n in "abc")
        mv_a, mv_b, mv_c = (sb(f"mv_{n}", [P, NT, 2]) for n in "abc")
        ve_a, ve_b, ve_c = (sb(f"ve_{n}", [P, NT]) for n in "abc")
        rstd_a = [sb(f"rstd_a{i}", [P, NT]) for i in range(2)]
        rstd_b, rstd_c = (sb(f"rstd_{n}", [P, NT]) for n in "bc")
        minus_one = sb("minus_one", [P, NT])
        mean_rstd = sb("mean_rstd_a", [P, NT])
        shift_a = [sb(f"shift_a{i}", [P, NT]) for i in range(2)]
        h = [sb(f"h{i}", [P, NT, D]) for i in range(2)]
        convT = sb("convT", [P, N])
        z = sb("z", [P, NT, D])
        z_std = sb("z_std", [P, NT, D])
        z2_std = sb("z2_std", [P, NT, D])
        z_gain = sb("z_gain", [P, NT, D])
        z_norm = sb("z_norm", [P, NT, D])
        x1 = [sb(f"x1_{i}", [P, NT, D]) for i in range(2)]
        x1_bo = [sb(f"x1_bo{i}", [P, NT, D]) for i in range(2)]
        x1T = sb("x1T", [P, N])
        q_parts, k_parts = (sb(n, [P, 2, N], F32R) for n in ("q_parts", "k_parts"))
        q_hi, q_lo, k_hi, k_lo = q_parts[:, 0, :], q_parts[:, 1, :], k_parts[:, 0, :], k_parts[:, 1, :]
        bounce = [[nc.dram_tensor(f"bounce_{n}{i}", (2, P, N), F32, kind="Internal").ap() for i in range(2)]
                  for n in "qk"]
        q_stack = [sb(f"q_stack{i}", [P, HEADS, N], F32R) for i in range(2)]
        k_stack = [sb(f"k_stack{i}", [P, HEADS, N], F32R) for i in range(2)]
        v = [sb(f"v_{i}", [P, NT, D]) for i in range(2)]
        prob = [sb(f"prob{i}", [P, N]) for i in range(RING)]
        low = sb("low", [P, TURNED])
        probT = [sb(f"probT{i}", [P, NT, P]) for i in range(TURNED)]
        row_sums = [sb(f"row_sums{i}", [P, UNITS]) for i in range(2)]
        sums_inv = sb("sums_inv", [P, UNITS])
        rinv = sb("rinv", [P, UNITS * HD])
        spread = sb("spread", [P, N])
        oT = sb("oT", [P, N])
        z2 = sb("z2", [P, NT, D])
        z2_gain = sb("z2_gain", [P, NT, D])

        rows_loaded = sem("rows_loaded")
        weights_loaded = sem("weights_loaded")
        rows_spread = sem("rows_spread")
        rows_copied = sem("rows_copied")
        a_stats, a_mv, a_pool, h_ready = (sem(n) for n in ("a_stats", "a_mv", "a_pool", "h_ready"))
        minus_set, a_scales, z_std_ready, z_gain_ready, z_norm_ready, z2_std_ready, z2_gain_ready, sums_inv_ready = (
            sem(n) for n in ("minus_set", "a_scales", "z_std_ready", "z_gain_ready", "z_norm_ready", "z2_std_ready",
                             "z2_gain_ready", "sums_inv_ready"))
        conv_psum, conv_ready = sem("conv_psum"), sem("conv_ready")
        z_psum, z_ready, b_stats, b_mv, b_pool, x1_ready, x1_bo_ready = (
            sem(n) for n in ("z_psum", "z_ready", "b_stats", "b_mv", "b_pool", "x1_ready", "x1_bo_ready"))
        x1T_psum, x1T_ready = sem("x1T_psum"), sem("x1T_ready")
        q_psum, q_hi_ready, q_lo_ready = sem("q_psum"), sem("q_hi_ready"), sem("q_lo_ready")
        k_psum, k_hi_ready, k_lo_ready = sem("k_psum"), sem("k_hi_ready"), sem("k_lo_ready")
        v_psum, v_copied = sem("v_psum"), sem("v_copied")
        q_written, k_written = ([sem(f"{n}_written{i}") for i in range(2)] for n in "qk")
        stacked = [sem(f"stacked{i}") for i in range(2)]
        scores_psum, masked, exp_done, turned_psum = (
            sem(n) for n in ("scores_psum", "masked", "exp_done", "turned_psum"))
        copied_act, copied_dve = sem("copied_act"), sem("copied_dve")
        o_psum, rinv_ready, spread_psum, spread_ready, oT_ready = (
            sem(n) for n in ("o_psum", "rinv_ready", "spread_psum", "spread_ready", "oT_ready"))
        proj_psum, z2_ready, c_stats, c_mv, c_pool, x2_ready = (
            sem(n) for n in ("proj_psum", "z2_ready", "c_stats", "c_mv", "c_pool", "x2_ready"))

        A_BANK, B_BANK = psum[4], psum[5]
        STACK_DMAS = 2 * STACKS * 16

        def parts(r):
            return within(r, 0, BATCH - 1), within(r, 1, BATCH), within(r, 2, BATCH + 1)

        def copy_wait(eng, batch, unit):
            by_dve = unit in DVE_COPIES
            at_least(eng, copied_dve if by_dve else copied_act, copied(by_dve, batch, unit))

        with nc.Block() as block:

            @block.sync
            def _(sp):
                for n, row in enumerate((bc, g1, be1, bo, g2, be2, b2, g3, be3)):
                    sp.dma_start(row_in[:, n, :], row.rearrange("(o d) -> o d", o=1)).then_inc(rows_loaded, 16)
                for tile, source in ((Wcs, Wc), (Wqs, Wq), (Wks, Wk), (Wvs, Wv), (Wos, Wo)):
                    sp.dma_start(tile[:, :], source).then_inc(weights_loaded, 16)
                sp.dma_start(W1s[:, :], W1).then_inc(mlp_loaded, 16)
                sp.dma_start(W2s[:, :, :], W2.rearrange("(j p) d -> p j d", p=P)).then_inc(mlp_loaded, 16)
                sp.dma_start(b1s[:, :], b1.rearrange("(j p) -> p j", p=P),
                             allow_slow_non_contiguous=True).then_inc(mlp_loaded, 16)

                def stack(p, s, half):
                    for n, (tile, ready, parts_of, written) in enumerate((
                            (k_stack, k_lo_ready, k_parts, k_written), (q_stack, q_lo_ready, q_parts, q_written))):
                        sp.wait_ge(ready, p + 1)
                        sp.dma_start(bounce[n][s].rearrange("a p n -> p a n"), parts_of[:, :, :].bitcast(F32)
                                     ).then_inc(written[s], 16)
                        sp.wait_ge(written[s], 16 * (half + 1))
                        for j, part in enumerate(((0, 1, 0, 1), (0, 0, 1, 1))[n]):
                            sp.dma_start(tile[s][j * HD:(j + 1) * HD, :, :].bitcast(F32),
                                         bounce[n][s][part, :, :].rearrange("(h d) n -> d h n", h=HEADS)
                                         ).then_inc(stacked[s], 16)
                rounds(sp, stack, 2, BATCH, BATCH)

            @block.gpsimd
            def _(pool):
                def inverse_root(b, mv, mv_sem, ve, rstd, pool_sem, used_sem, used):
                    pool.wait_ge(mv_sem, b + 1)
                    at_least(pool, used_sem, used)
                    pool.sem_inc(pool_waited, 1)
                    pool.tensor_scalar(ve[:, :], mv[:, :, 1], EPS, None, ALU.add).then_inc(pool_sem, 1)
                    pool.wait_ge(pool_sem, 2 * b + 1)
                    pool.tensor_tensor(out=rstd[:, :], in0=ve[:, :], in1=exponent[:, :],
                                       op=ALU.pow).then_inc(pool_sem, 1)

                def h_scales(b, s):
                    inverse_root(b, mv_a, a_mv, ve_a, rstd_a[s], a_pool, h_ready, NT * (b - 1))
                    pool.wait_ge(a_pool, 2 * b + 2)
                    pool.tensor_tensor(out=mean_rstd[:, :], in0=mv_a[:, :, 0], in1=rstd_a[s][:, :],
                                       op=ALU.mult).then_inc(a_scales, 1)
                    pool.wait_ge(a_scales, 2 * b + 1)
                    pool.tensor_tensor(out=shift_a[s][:, :], in0=mean_rstd[:, :], in1=minus_one[:, :],
                                       op=ALU.mult).then_inc(a_scales, 1)

                def norm_z(b):
                    pool.wait_ge(z_std_ready, b + 1)
                    pool.tensor_tensor(out=z_gain[:, :, :], in0=z_std[:, :, :], in1=all_tiles(G1),
                                       op=ALU.mult).then_inc(z_gain_ready, 1)
                    pool.wait_ge(z_gain_ready, b + 1)
                    at_least(pool, x1_ready, b)
                    pool.tensor_tensor(out=z_norm[:, :, :], in0=z_gain[:, :, :], in1=all_tiles(BE1),
                                       op=ALU.add).then_inc(z_norm_ready, 1)

                def z_root(b):
                    inverse_root(b, mv_b, b_mv, ve_b, rstd_b, b_pool, z_std_ready, b)

                def round_(r, s, half):
                    enters, attends, leaves = parts(r)
                    e = r - 2
                    if within(r, 0, BATCH - 3):
                        h_scales(r + 2, s)
                    if enters:
                        pool.wait_ge(x1_ready, r + 1)
                        at_least(pool, z2_ready, r - 1)
                        pool.tensor_tensor(out=x1_bo[s][:, :, :], in0=x1[s][:, :, :], in1=all_tiles(BO),
                                           op=ALU.add).then_inc(x1_bo_ready, 1)
                    if within(r, 0, BATCH - 2):
                        z_root(r + 1)
                    if leaves:
                        inverse_root(e, mv_c, c_mv, ve_c, rstd_c, c_pool, z2_std_ready, e)
                    if within(r, 0, BATCH - 2):
                        norm_z(r + 1)
                    if leaves:
                        pool.wait_ge(z2_std_ready, e + 1)
                        pool.tensor_tensor(out=z2_gain[:, :, :], in0=z2_std[:, :, :], in1=all_tiles(G2),
                                           op=ALU.mult).then_inc(z2_gain_ready, 1)
                        pool.wait_ge(z2_gain_ready, e + 1)
                        pool.tensor_tensor(out=x2[:, bass.ds(e * N, N)].rearrange("p (t d) -> p t d", d=D),
                                           in0=z2_gain[:, :, :], in1=all_tiles(BE2), op=ALU.add
                                           ).then_inc(x2_ready, 1)
                pool.memset(minus_one[:, :], -1.0).then_inc(minus_set, 1)
                pool.wait_ge(minus_set, 1)
                h_scales(0, 0)
                h_scales(1, 1)
                z_root(0)
                norm_z(0)
                pool.wait_ge(rows_copied, 3)
                rounds(pool, round_, 2, BATCH - 2, BATCH + 2)

            @block.tensor
            def _(pe):
                pe.wait_ge(rows_loaded, 16 * ROWS)
                row_flat = row_in[:, :, :].rearrange("o r d -> o (r d)")
                for c in range(3):
                    cols = min(N, ROWS * D - c * N)
                    pe.matmul(psum[c][:, 0:cols], ones[0:1, :], row_flat[:, c * N:c * N + cols], start=True,
                              stop=True).then_inc(rows_spread, 1)
                pe.wait_ge(weights_loaded, 16 * 5)
                pe.wait_ge(rows_copied, 3)

                def scores(a, s, u, half):
                    if u == 0:
                        pe.wait_ge(stacked[s], STACK_DMAS * half)
                    at_least(pe, masked, UNITS * a + u - 1)
                    t, head = divmod(u, HEADS)
                    pe.matmul(psum[u % 2][:, :], q_stack[s][:, head, t * P:(t + 1) * P], k_stack[s][:, head, :],
                              start=True, stop=True).then_inc(scores_psum, 1)

                def turn(batch, u):
                    pe.wait_ge(exp_done, UNITS * batch + u + 1)
                    if isinstance(batch, int) and batch == 0 and u < 2:
                        pass
                    elif u < 2:
                        copy_wait(pe, batch - 1, u - 2 + UNITS)
                    else:
                        copy_wait(pe, batch, u - 2)
                    for mt in range(NT):
                        last = pe.transpose(psum[2 + u % 2][:, mt * P:(mt + 1) * P],
                                            prob[u % RING][:, mt * P:(mt + 1) * P], ident[:, :])
                    last.then_inc(turned_psum, 1)

                def values(batch, s, t, mt):
                    if mt == 0:
                        tile_units = range(HEADS * t, HEADS * (t + 1))
                        for by_dve in (False, True):
                            mine = [u for u in tile_units if (u in DVE_COPIES) == by_dve]
                            if mine:
                                copy_wait(pe, batch, mine[-1])
                        if t == 0:
                            pe.wait_ge(v_copied, batch + 1)
                            at_least(pe, oT_ready, batch - 1)
                            pe.wait_ge(k_lo_ready, min(batch + 2, BATCH) if isinstance(batch, int) else batch + 2)
                    for head in range(HEADS):
                        rows = slice(head * HD, (head + 1) * HD)
                        last = pe.matmul(psum[6 + s][rows, t * P:(t + 1) * P], v[s][:, mt, rows],
                                         probT[(HEADS * t + head) % TURNED][:, mt, :],
                                         start=mt == 0, stop=mt == NT - 1, skip_group_check=True)
                    if mt == NT - 1:
                        last.then_inc(o_psum, 1)

                def conv(b, s, k):
                    pe.wait_ge(h_ready, NT * b + k + 1)
                    if k == 0:
                        at_least(pe, x1T_ready, b)
                    last = pe.matmul(A_BANK[:, :], h[s][:, k, :], Lnorm[:, k, :], start=k == 0, stop=k == NT - 1)
                    if k == NT - 1:
                        last.then_inc(conv_psum, 1)

                def conv_weights(b):
                    pe.wait_ge(conv_ready, b + 1)
                    for t in range(NT):
                        last = pe.matmul(A_BANK[:, t * D:(t + 1) * D], convT[:, t * P:(t + 1) * P], Wcs[:, :],
                                         start=True, stop=True)
                    last.then_inc(z_psum, 1)

                def round_(r, s, half):
                    enters, attends, leaves = parts(r)
                    a, e = r - 1, r - 2
                    for u in range(UNITS):
                        if attends:
                            scores(a, 1 - s, u, half + s)
                        if u < VALUES_LAG and leaves:
                            values(e, s, (u + UNITS - VALUES_LAG) // HEADS, u % HEADS)
                        if u >= VALUES_LAG and attends:
                            values(a, 1 - s, (u - VALUES_LAG) // HEADS, u % HEADS)
                        if u >= TURN_LAG and attends:
                            turn(a, u - TURN_LAG)
                        if u < TURN_LAG and leaves:
                            turn(e, u - TURN_LAG + UNITS)
                        if u == AT_SPREAD and leaves:
                            pe.wait_ge(rinv_ready, e + 1)
                            pe.wait_ge(v_copied, min(r, BATCH) if isinstance(r, int) else r)
                            for t in range(NT):
                                last = pe.transpose(B_BANK[:, t * P:(t + 1) * P], rinv[:, t * P:(t + 1) * P],
                                                    ident[:, :])
                            last.then_inc(spread_psum, 1)
                        if u == AT_X1T and enters:
                            pe.wait_ge(x1_ready, r + 1)
                            for t in range(NT):
                                last = pe.transpose(A_BANK[:, t * P:(t + 1) * P], x1[s][:, t, :], ident[:, :])
                            last.then_inc(x1T_psum, 1)
                        if u == AT_K and enters:
                            pe.wait_ge(x1T_ready, r + 1)
                            at_least(pe, oT_ready, r - 2)
                            pe.matmul(psum[7 - s][:, :], Wks[:, :], x1T[:, :], start=True, stop=True
                                      ).then_inc(k_psum, 1)
                        if u == AT_Q and enters:
                            at_least(pe, v_copied, r)
                            at_least(pe, spread_ready, r - 1)
                            pe.matmul(B_BANK[:, :], Wqs[:, :], x1T[:, :], start=True, stop=True).then_inc(q_psum, 1)
                        if AT_CONV <= u < AT_CONV + NT and within(r, 0, BATCH - 2):
                            conv(r + 1, 1 - s, u - AT_CONV)
                        if u == AT_Z and within(r, 0, BATCH - 2):
                            conv_weights(r + 1)
                        if u == AT_PROJ and leaves:
                            pe.wait_ge(oT_ready, e + 1)
                            pe.wait_ge(q_lo_ready,
                                       min(r + 1, BATCH) if isinstance(r, int) else r + 1)
                            for t in range(NT):
                                last = pe.matmul(B_BANK[:, t * D:(t + 1) * D], oT[:, t * P:(t + 1) * P],
                                                 Wos[:, :], start=True, stop=True)
                            last.then_inc(proj_psum, 1)
                        if u == AT_V and enters:
                            pe.wait_ge(q_lo_ready, r + 1)
                            at_least(pe, z2_ready, r - 1)
                            for t in range(NT):
                                last = pe.matmul(B_BANK[:, t * D:(t + 1) * D], x1T[:, t * P:(t + 1) * P],
                                                 Wvs[:, :], start=True, stop=True)
                            last.then_inc(v_psum, 1)
                for k in range(NT):
                    conv(0, 0, k)
                conv_weights(0)
                rounds(pe, round_, 2, BATCH - 2, BATCH + 2)

            @block.scalar
            def _(act):
                def normalise(b, s, t):
                    if t == 0:
                        act.wait_ge(a_scales, 2 * b + 2)
                        at_least(act, x1_ready, b - 1)
                    act.activation(h[s][:, t, :], y[:, bass.ds(b * N + t * D, D)], ACT.Relu,
                                   scale=rstd_a[s][:, t:t + 1], bias=shift_a[s][:, t:t + 1]).then_inc(h_ready, 1)

                def copy_turned(batch, u):
                    act.wait_ge(turned_psum, UNITS * batch + u + 1)
                    act.activation(probT[u % TURNED][:, :, :].rearrange("p t n -> p (t n)"), psum[2 + u % 2][:, :],
                                   ACT.Copy).then_inc(copied_act, 1)

                def conv_out(b):
                    act.wait_ge(conv_psum, b + 1)
                    act.activation(convT[:, :], A_BANK[:, :], ACT.Copy).then_inc(conv_ready, 1)

                def round_(r, s, half):
                    enters, attends, leaves = parts(r)
                    a, e = r - 1, r - 2
                    for u in range(UNITS):
                        if attends:
                            if u == 0:
                                at_least(act, rinv_ready, a - 1)
                            act.wait_ge(masked, UNITS * a + u + 1)
                            act.activation(prob[u % RING][:, :], prob[u % RING][:, :], ACT.Exp,
                                           bias=low[:, u % TURNED:u % TURNED + 1], scale=-1.0,
                                           accum_out=row_sums[1 - s][:, u:u + 1]).then_inc(exp_done, 1)
                        x = (u - TURN_LAG) % UNITS
                        if x not in DVE_COPIES:
                            if u < TURN_LAG and leaves:
                                copy_turned(e, x)
                            if u >= TURN_LAG and attends:
                                copy_turned(a, x)
                        if u == AT_X1T_OUT and enters:
                            act.wait_ge(x1T_psum, r + 1)
                            at_least(act, v_psum, r)
                            act.activation(x1T[:, :], A_BANK[:, :], ACT.Copy).then_inc(x1T_ready, 1)
                        if u == AT_K_HI and enters:
                            act.wait_ge(k_psum, r + 1)
                            if not (isinstance(r, int) and r == 0):
                                act.wait_ge(k_written[1 - s], 16 * (half + s))
                            act.activation(k_hi, psum[7 - s][:, :], ACT.Copy).then_inc(k_hi_ready, 1)
                        if u == AT_Q_HI and enters:
                            act.wait_ge(q_psum, r + 1)
                            if not (isinstance(r, int) and r == 0):
                                act.wait_ge(q_written[1 - s], 16 * (half + s))
                            act.activation(q_hi, B_BANK[:, :], ACT.Copy,
                                           scale=-float(HD) ** -0.5).then_inc(q_hi_ready, 1)
                        if AT_H <= u < AT_H + NT and within(r, 0, BATCH - 3):
                            normalise(r + 2, s, u - AT_H)
                        if u == AT_V_OUT and enters:
                            act.wait_ge(v_psum, r + 1)
                            act.activation(flat(v[s]), B_BANK[:, :], ACT.Copy).then_inc(v_copied, 1)
                        if u == AT_SPREAD_OUT and leaves:
                            act.wait_ge(spread_psum, e + 1)
                            at_least(act, oT_ready, e)
                            act.activation(spread[:, :], B_BANK[:, :], ACT.Copy).then_inc(spread_ready, 1)
                        if u == AT_CONV_OUT and within(r, 0, BATCH - 2):
                            conv_out(r + 1)
                for b in range(2):
                    for t in range(NT):
                        normalise(b, b, t)
                conv_out(0)
                rounds(act, round_, 2, BATCH - 2, BATCH + 2)

            @block.vector
            def _(dve):
                for c in range(3):
                    cols = min(N, ROWS * D - c * N)
                    dve.wait_ge(rows_spread, c + 1)
                    dve.tensor_copy(bc_all[:, :, :].rearrange("p r d -> p (r d)")[:, c * N:c * N + cols],
                                    psum[c][:, 0:cols]).then_inc(rows_copied, 1)
                dve.wait_ge(rows_copied, 3)

                def moments(b, source, stats, stats_sem, mv, mv_sem, used_sem, steps=1):
                    at_least(dve, mv_sem, b)
                    for t in range(NT):
                        last = dve.bn_stats(stats[:, t, :], source(t))
                    last.then_inc(stats_sem, 1)
                    dve.wait_ge(stats_sem, b + 1)
                    at_least(dve, used_sem, steps * b)
                    dve.sem_inc(dve_waited, 1)
                    for t in range(NT):
                        last = dve.bn_aggr(mv[:, t, :], stats[:, t, :])
                    last.then_inc(mv_sem, 1)

                def y_moments(b):
                    moments(b, lambda t: y[:, bass.ds(b * N + t * D, D)], stats_a, a_stats, mv_a, a_mv, a_scales, 2)

                def standardise(out, src, mv, rstd, done):
                    for t in range(NT):
                        last = dve.tensor_scalar(out[:, t, :], src[:, t, :], mv[:, t, 0:1], rstd[:, t:t + 1],
                                                 ALU.subtract, ALU.mult)
                    last.then_inc(done, 1)

                def z_out(b):
                    dve.wait_ge(z_psum, b + 1)
                    at_least(dve, z_std_ready, b)
                    dve.tensor_tensor(out=z[:, :, :], in0=A_BANK[:, :].rearrange("p (t d) -> p t d", d=D),
                                      in1=all_tiles(BC), op=ALU.add).then_inc(z_ready, 1)

                def z_moments(b):
                    dve.wait_ge(z_ready, b + 1)
                    moments(b, lambda t: z[:, t, :], stats_b, b_stats, mv_b, b_mv, z_std_ready)

                def z_standard(b):
                    dve.wait_ge(b_pool, 2 * b + 2)
                    at_least(dve, z_gain_ready, b)
                    standardise(z_std, z, mv_b, rstd_b, z_std_ready)

                def copy_turned(batch, u):
                    dve.wait_ge(turned_psum, UNITS * batch + u + 1)
                    dve.tensor_copy(probT[u % TURNED][:, :, :].rearrange("p t n -> p (t n)"),
                                    psum[2 + u % 2][:, :]).then_inc(copied_dve, 1)

                def round_(r, s, half):
                    enters, attends, leaves = parts(r)
                    a, e = r - 1, r - 2
                    for u in range(UNITS):
                        if attends:
                            dve.wait_ge(scores_psum, UNITS * a + u + 1)
                            at_least(dve, turned_psum, UNITS * a + u + 1 - RING)
                            dve.sem_inc(dve_waited, 1)
                            dve.tensor_tensor_reduce(prob[u % RING][:, :], psum[u % 2][:, :],
                                                     mask[:, u // HEADS, :], 1.0, 3e38, ALU.add, ALU.min,
                                                     low[:, u % TURNED:u % TURNED + 1]).then_inc(masked, 1)
                        x = (u - TURN_LAG) % UNITS
                        if x in DVE_COPIES:
                            if u < TURN_LAG and leaves:
                                copy_turned(e, x)
                            if u >= TURN_LAG and attends:
                                copy_turned(a, x)
                        if u == AT_X1 and enters:
                            dve.wait_ge(z_norm_ready, r + 1)
                            at_least(dve, x1T_psum, r - 1)
                            at_least(dve, x1_bo_ready, r - 1)
                            dve.scalar_tensor_tensor(out=flat(x1[s]), in0=flat(z_norm), scalar=0.0, in1=flat(h[s]),
                                                     op0=ALU.max, op1=ALU.add).then_inc(x1_ready, 1)
                        if u == AT_Y_MOMENTS and within(r, 0, BATCH - 3):
                            y_moments(r + 2)
                        if u == AT_RINV and leaves:
                            dve.wait_ge(exp_done, UNITS * (e + 1))
                            at_least(dve, spread_psum, e)
                            dve.reciprocal(sums_inv[:, :], row_sums[s][:, :]).then_inc(sums_inv_ready, 1)
                            dve.wait_ge(sums_inv_ready, e + 1)
                            dve.tensor_copy(rinv[:, :].rearrange("p (u d) -> p u d", d=HD),
                                            sums_inv[:, :].unsqueeze(2).broadcast_to([P, UNITS, HD])
                                            ).then_inc(rinv_ready, 1)
                        if u == AT_K_LO and enters:
                            dve.wait_ge(k_hi_ready, r + 1)
                            dve.tensor_tensor(out=k_lo, in0=psum[7 - s][:, :], in1=k_hi.bitcast(F32),
                                              op=ALU.subtract).then_inc(k_lo_ready, 1)
                        if u == AT_Q_LO and enters:
                            dve.wait_ge(q_hi_ready, r + 1)
                            dve.scalar_tensor_tensor(out=q_lo, in0=B_BANK[:, :], scalar=-float(HD) ** -0.5,
                                                     in1=q_hi.bitcast(F32), op0=ALU.mult,
                                                     op1=ALU.subtract).then_inc(q_lo_ready, 1)
                        if u == AT_O and leaves:
                            dve.wait_ge(o_psum, NT * (e + 1))
                            dve.wait_ge(spread_ready, e + 1)
                            at_least(dve, proj_psum, e)
                            dve.tensor_tensor(out=oT[:, :], in0=psum[6 + s][:, :], in1=spread[:, :],
                                              op=ALU.mult).then_inc(oT_ready, 1)
                        if u == AT_Z_OUT and within(r, 0, BATCH - 2):
                            z_out(r + 1)
                        if u == AT_Z2 and leaves:
                            dve.wait_ge(proj_psum, e + 1)
                            dve.wait_ge(x1_bo_ready, e + 1)
                            at_least(dve, z2_std_ready, e)
                            dve.tensor_tensor(out=flat(z2), in0=B_BANK[:, :], in1=flat(x1_bo[s]),
                                              op=ALU.add).then_inc(z2_ready, 1)
                        if u == AT_Z_MOMENTS and within(r, 0, BATCH - 2):
                            z_moments(r + 1)
                        if u == AT_Z2_MOMENTS and leaves:
                            dve.wait_ge(z2_ready, e + 1)
                            moments(e, lambda t: z2[:, t, :], stats_c, c_stats, mv_c, c_mv, z2_std_ready)
                        if u == AT_Z_STD and within(r, 0, BATCH - 2):
                            z_standard(r + 1)
                        if u == AT_Z2_STD and leaves:
                            dve.wait_ge(c_pool, 2 * e + 2)
                            at_least(dve, z2_gain_ready, e)
                            standardise(z2_std, z2, mv_c, rstd_c, z2_std_ready)
                y_moments(0)
                y_moments(1)
                z_out(0)
                z_moments(0)
                z_standard(0)
                rounds(dve, round_, 2, BATCH - 2, BATCH + 2)

    with ExitStack() as ctx:
        def sb(name, shape, dt=F32):
            return tensor(ctx, name, shape, dt)

        x2_now = [sb(f"x2_now{i}", [P, NT, D]) for i in range(2)]
        x2T = [sb(f"x2T{i}", [P, N]) for i in range(2)]
        x2_b2 = [sb(f"x2_b2{i}", [P, NT, D]) for i in range(2)]
        y_be3 = [sb(f"y_be3{i}", [P, NT, D]) for i in range(2)]
        gelu = [sb(f"gelu{i}", [P, HT, N]) for i in range(2)]
        z3 = [sb(f"z3_{i}", [P, NT, D]) for i in range(2)]
        z3_gain = sb("z3_gain", [P, NT, D])
        result = [sb(f"result{i}", [P, NT, D]) for i in range(2)]
        b2_tiles = sb("b2_tiles", [P, NT, D])
        be3_tiles = sb("be3_tiles", [P, NT, D])
        stats3 = sb("stats3", [P, NT, 6])
        mv3 = [sb(f"mv3{i}", [P, NT, 2]) for i in range(2)]
        ve3 = sb("ve3", [P, NT])
        rstd3 = [sb(f"rstd3{i}", [P, NT]) for i in range(2)]

        x2_now_ready, x2T_psum, x2T_ready, hid_psum, gelu_ready, mlp_psum, z3_ready = (
            sem(n) for n in ("x2_now_ready", "x2T_psum", "x2T_ready", "hid_psum", "gelu_ready", "mlp_psum", "z3_ready"))
        x2_b2_ready, y_be3_ready, stats3_ready, mv3_ready, pool3, z3_step, result_ready = (
            sem(n) for n in ("x2_b2_ready", "y_be3_ready", "stats3_ready", "mv3_ready", "pool3", "z3_step",
                             "result_ready"))
        tiles_ready = sem("tiles_ready")
        stored = [sem(f"stored{i}") for i in range(2)]

        with nc.Block() as block:

            @block.sync
            def _(sp):
                def store(b, s, half):
                    sp.wait_ge(result_ready, b + 1)
                    sp.dma_start(out_dram[:, bass.ds(b, 1), :, :].rearrange("p b t d -> p (b t) d"),
                                 result[s][:, :, :]).then_inc(stored[s], 16)
                rounds(sp, store, 2, BATCH, BATCH)
                for s in range(2):
                    sp.wait_ge(stored[s], 16 * (BATCH // 2))

            @block.gpsimd
            def _(pool):
                def round_(r, s, half):
                    if within(r, 0, BATCH - 1):
                        at_least(pool, z3_ready, r - 1)
                        pool.tensor_tensor(out=flat(x2_b2[s]), in0=x2[:, bass.ds(r * N, N)], in1=flat(b2_tiles),
                                           op=ALU.add).then_inc(x2_b2_ready, 1)
                        at_least(pool, result_ready, r - 1)
                        pool.tensor_tensor(out=flat(y_be3[s]), in0=y[:, bass.ds(r * N, N)], in1=flat(be3_tiles),
                                           op=ALU.add).then_inc(y_be3_ready, 1)
                    if within(r, 1, BATCH):
                        b = r - 1
                        pool.wait_ge(mv3_ready, b + 1)
                        at_least(pool, result_ready, b - 1)
                        pool.sem_inc(pool_waited, 1)
                        pool.tensor_scalar(ve3[:, :], mv3[1 - s][:, :, 1], EPS, None, ALU.add).then_inc(pool3, 1)
                        pool.wait_ge(pool3, 2 * b + 1)
                        pool.tensor_tensor(out=rstd3[1 - s][:, :], in0=ve3[:, :], in1=exponent[:, :],
                                           op=ALU.pow).then_inc(pool3, 1)
                for t in range(NT):
                    pool.tensor_copy(b2_tiles[:, t, :], bc_all[:, B2, :])
                    last = pool.tensor_copy(be3_tiles[:, t, :], bc_all[:, BE3, :])
                last.then_inc(tiles_ready, 1)
                pool.wait_ge(tiles_ready, 1)
                rounds(pool, round_, 2, BATCH, BATCH + 1)

            @block.tensor
            def _(pe):
                pe.wait_ge(mlp_loaded, 16 * 3)

                def round_(r, s, half):
                    if within(r, 0, BATCH - 1):
                        pe.wait_ge(x2_now_ready, r + 1)
                        at_least(pe, x2T_ready, r - 1)
                        for t in range(NT):
                            last = pe.transpose(psum[s][:, t * P:(t + 1) * P], x2_now[s][:, t, :], ident[:, :])
                        last.then_inc(x2T_psum, 1)
                    if within(r, 1, BATCH):
                        pe.wait_ge(gelu_ready, HT * r)
                        at_least(pe, z3_ready, r - 2)
                        for t in range(NT):
                            for j in range(HT):
                                last = pe.matmul(psum[7 - s][:, t * D:(t + 1) * D],
                                                 gelu[1 - s][:, j, t * P:(t + 1) * P], W2s[:, j, :],
                                                 start=j == 0, stop=j == HT - 1)
                        last.then_inc(mlp_psum, 1)
                    if within(r, 0, BATCH - 1):
                        pe.wait_ge(x2T_ready, r + 1)
                        for j in range(HT):
                            at_least(pe, gelu_ready, HT * (r - 2) + j + 1)
                            pe.matmul(psum[2 + HT * s + j][:, :], W1s[:, j * P:(j + 1) * P], x2T[s][:, :],
                                      start=True, stop=True).then_inc(hid_psum, 1)
                rounds(pe, round_, 2, BATCH, BATCH + 1)

            @block.scalar
            def _(act):
                def fetch(r, s):
                    at_least(act, x2T_psum, r - 1)
                    act.activation(flat(x2_now[s]), x2[:, bass.ds(r * N, N)], ACT.Copy).then_inc(x2_now_ready, 1)

                def round_(r, s, half):
                    if within(r, 0, BATCH - 1):
                        if isinstance(r, int) and r == 0:
                            fetch(0, 0)
                        act.wait_ge(x2T_psum, r + 1)
                        act.activation(x2T[s][:, :], psum[s][:, :], ACT.Copy).then_inc(x2T_ready, 1)
                        if within(r, 0, BATCH - 2):
                            fetch(r + 1, 1 - s)
                        for j in range(HT):
                            act.wait_ge(hid_psum, HT * r + j + 1)
                            act.activation(gelu[s][:, j, :], psum[2 + HT * s + j][:, :], ACT.Gelu,
                                           bias=b1s[:, j:j + 1]).then_inc(gelu_ready, 1)
                rounds(act, round_, 2, BATCH - 2, BATCH)

            @block.vector
            def _(dve):
                def round_(r, s, half):
                    if within(r, 2, BATCH + 1):
                        b = r - 2
                        dve.wait_ge(pool3, 2 * b + 2)
                        dve.wait_ge(y_be3_ready, b + 1)
                        for t in range(NT):
                            last = dve.scalar_tensor_tensor(out=z3_gain[:, t, :], in0=z3[s][:, t, :],
                                                            scalar=mv3[s][:, t, 0:1], in1=bc_all[:, G3, :],
                                                            op0=ALU.subtract, op1=ALU.mult)
                        last.then_inc(z3_step, 1)
                        dve.wait_ge(z3_step, b + 1)
                        if isinstance(r, int):
                            if b >= 2:
                                dve.wait_ge(stored[s], 16 * (b // 2))
                        else:
                            at_least(dve, stored[s], 16 * (half - 1))
                        for t in range(NT):
                            last = dve.scalar_tensor_tensor(out=result[s][:, t, :], in0=z3_gain[:, t, :],
                                                            scalar=rstd3[s][:, t:t + 1], in1=y_be3[s][:, t, :],
                                                            op0=ALU.mult, op1=ALU.add)
                        last.then_inc(result_ready, 1)
                    if within(r, 1, BATCH):
                        b = r - 1
                        dve.wait_ge(mlp_psum, b + 1)
                        dve.wait_ge(x2_b2_ready, b + 1)
                        dve.tensor_tensor(out=flat(z3[1 - s]), in0=psum[7 - s][:, :], in1=flat(x2_b2[1 - s]),
                                          op=ALU.add).then_inc(z3_ready, 1)
                        dve.wait_ge(z3_ready, b + 1)
                        at_least(dve, mv3_ready, b)
                        for t in range(NT):
                            last = dve.bn_stats(stats3[:, t, :], z3[1 - s][:, t, :])
                        last.then_inc(stats3_ready, 1)
                        dve.wait_ge(stats3_ready, b + 1)
                        at_least(dve, result_ready, b - 1)
                        dve.sem_inc(dve_waited, 1)
                        for t in range(NT):
                            last = dve.bn_aggr(mv3[1 - s][:, t, :], stats3[:, t, :])
                        last.then_inc(mv3_ready, 1)
                rounds(dve, round_, 2, BATCH, BATCH + 2)


_INS = ["x", "adj", "L0_gnn_alpha_train", "L0_gnn_w", "L0_gnn_d", "L0_gnn_fc_in_w", "L0_gnn_fc_in_b",
        "L1_gnn_Wc", "L1_gnn_bc", "L1_gnn_g1", "L1_gnn_be1", "L1_gnn_Wq", "L1_gnn_Wk", "L1_gnn_Wv", "L1_gnn_Wo",
        "L1_gnn_bo", "L1_gnn_g2", "L1_gnn_be2", "L1_gnn_W1", "L1_gnn_b1", "L1_gnn_W2", "L1_gnn_b2", "L1_gnn_g3",
        "L1_gnn_be3"]


def kernel(**inputs):
    import numpy as _np
    import concourse.bacc as _bacc
    from concourse import mybir as _mybir
    from concourse.bass_utils import run_bass_kernel_spmd as _run

    nc = _bacc.Bacc("TRN2", target_bir_lowering=False, num_devices=1)
    arrays, args = {}, []
    for name in _INS:
        a = _np.ascontiguousarray(inputs[name])
        arrays[f"in_{name}_dram"] = a
        args.append(nc.dram_tensor(f"in_{name}_dram", a.shape, _mybir.dt.from_np(a.dtype), kind="ExternalInput").ap())
    args.append(nc.dram_tensor("out_dram", (BATCH, N, D), _mybir.dt.float32, kind="ExternalOutput").ap())
    two_layers(nc, *args)
    return _run(nc, [arrays], core_ids=[0]).results[0]["out_dram"]
```

```python
from contextlib import ExitStack
from math import comb

import concourse.bass as bass
from concourse import mybir

F32 = mybir.dt.float32
F32R = mybir.dt.float32r
BF16 = mybir.dt.bfloat16
ALU = mybir.AluOpType
ACT = mybir.ActivationFunctionType
AX = mybir.AxisListType

BATCH, N, D = 16, 512, 128
P = 128
NT = N // P
STEPS = 8
DT = 1.0 / STEPS
HEADS = 4
HD = D // HEADS
HID = 2 * D
HT = HID // P
EPS = 1e-5
GROUP = 3
MASKED = 1e30
TINY = 1e-15
BC, G1, BE1, BO, G2, BE2, B2, G3, BE3 = range(9)
ROWS = 9
UNITS = NT * HEADS
assert (STEPS + 1) == GROUP * GROUP and BATCH % 2 == 0


def at_least(eng, semaphore, value):
    if isinstance(value, int) and value <= 0:
        return
    eng.wait_ge(semaphore, value)


def rounds(eng, body, first_full, after_full, last, first=0):
    for r in range(first, first_full):
        body(r, r % 2, r // 2)
    with eng.Fori(first_full // 2, after_full // 2) as half:
        body(2 * half, 0, half)
        body(2 * half + 1, 1, half)
    for r in range(after_full, last):
        body(r, r % 2, r // 2)


def within(r, low, high):
    return low <= r <= high if isinstance(r, int) else True


class Shared:
    pass


def two_layers(nc, x, adj, alpha, w, d, fc_w, fc_b, Wc, bc, g1, be1, Wq, Wk, Wv, Wo, bo, g2, be2, W1, b1, W2, b2,
               g3, be3, out):
    x_dram = x.rearrange("b (t p) d -> p b t d", p=P)
    out_dram = out.rearrange("b (t p) d -> p b t d", p=P)

    with ExitStack() as whole:
        def tensor(ctx, name, shape, dt=F32):
            return ctx.enter_context(nc.sbuf_tensor(name, shape, dt))

        def sem(name):
            return whole.enter_context(nc.semaphore(name))

        psum = [whole.enter_context(nc.psum_tensor(f"bank{i}", [P, N], F32)) for i in range(8)]

        waited = (sem("dve_waited"), sem("pool_waited"))

        y = tensor(whole, "y", [P, BATCH * N])
        with ExitStack() as early:
            adjT = tensor(early, "adjT", [P, NT, N])
        L_lo = tensor(whole, "L_lo", [P, NT, N], F32R)
        mask = tensor(whole, "mask", [P, NT, N], BF16)
        ident = tensor(whole, "ident", [P, P])
        ones = tensor(whole, "ones", [P, P])
        exponent = tensor(whole, "exponent", [P, NT])
        two_over_lam = tensor(whole, "two_over_lam", [P, 1])
        one = Shared()
        one.row_in = tensor(whole, "row_in", [1, ROWS, D])
        one.bc_all = tensor(whole, "bc_all", [P, ROWS, D])
        one.Wcs = tensor(whole, "W_c", [P, D])
        one.Wqs = tensor(whole, "W_q", [P, D])
        one.Wks = tensor(whole, "W_k", [P, D])
        one.Wvs = tensor(whole, "W_v", [P, D])
        one.Wos = tensor(whole, "W_o", [P, D])
        one.W1s = tensor(whole, "W1s", [P, HID])
        one.W2s = tensor(whole, "W2s", [P, HT, D])
        one.b1s = tensor(whole, "b1s", [P, HT])
        one.stats = tensor(whole, "stats_a", [P, NT, 6])
        one.mv = tensor(whole, "mv_a", [P, NT, 2])
        one.var_eps = tensor(whole, "ve_a", [P, NT])
        one.rstd = [tensor(whole, f"rstd_a{i}", [P, NT]) for i in range(2)]
        one.minus_one = tensor(whole, "minus_one", [P, NT])
        one.mean_rstd = tensor(whole, "mean_rstd_a", [P, NT])
        one.shift = [tensor(whole, f"shift_a{i}", [P, NT]) for i in range(2)]
        one.h = [tensor(whole, f"h{i}", [P, NT, D]) for i in range(2)]
        one.y, one.Lnorm, one.ident, one.exponent = y, adjT, ident, exponent
        one.dve_waited, one.pool_waited = waited
        one.L_lo = L_lo
        one.b_stats, one.b_mv = tensor(whole, "stats_b", [P, NT, 6]), tensor(whole, "mv_b", [P, NT, 2])
        one.b_var_eps, one.b_rstd = tensor(whole, "ve_b", [P, NT]), tensor(whole, "rstd_b", [P, NT])
        one.v = [tensor(whole, "v_0", [P, NT, D]), None]
        with ExitStack() as early:
            one.S = tensor(early, "S", [P, NT, N])
            one.Sq = [tensor(early, f"Sq{i}", [P, NT, N], F32R) for i in range(2)]
            one.B = tensor(early, "B", [P, GROUP, GROUP, D])
            one.powers = tensor(early, "powers", [P, STEPS + 1, D + 1])
            one.U_rows = tensor(early, "U_rows", [GROUP, N])
            one.w_in, one.fc_in, one.wT, one.dwT = (tensor(early, n, [P, D]) for n in ("w_in", "fc_in", "wT", "dwT"))
        one.q_parts, one.k_parts = (tensor(whole, n, [P, 2, N], F32R) for n in ("q_parts", "k_parts"))
        one.q_stack, one.k_stack = [None, None], [None, None]
        one.q_stack[0], one.k_stack[0] = (tensor(whole, f"{n}_stack0", [P, HEADS, N], F32R) for n in "qk")
        one.x1 = [tensor(whole, "x1_0", [P, NT, D]), None]
        one.x1T = tensor(whole, "x1T", [P, N])
        one.convT = tensor(whole, "convT", [P, N])
        one.z, one.z_std, one.z_gain, one.z_norm = (
            tensor(whole, n, [P, NT, D]) for n in ("z", "z_std", "z_gain", "z_norm"))
        one.bounce = [[nc.dram_tensor(f"bounce_{n}{i}", (2, P, N), F32, kind="Internal").ap() for i in range(2)]
                      for n in "qk"]
        one.rows_loaded = sem("rows_loaded")
        one.weights_loaded = sem("weights_loaded")
        one.mlp_loaded = sem("mlp_loaded")
        one.rows_spread = sem("rows_spread")
        one.rows_copied = sem("rows_copied")
        one.minus_set = sem("minus_set")
        one.stats_ready = sem("a_stats")
        one.mv_ready = sem("a_mv")
        one.pool_step = sem("a_pool")
        one.scales = sem("a_scales")
        one.h_ready = sem("h_ready")
        one.conv_psum, one.conv_ready, one.z_psum, one.z_ready = (
            sem(n) for n in ("conv_psum", "conv_ready", "z_psum", "z_ready"))
        one.b_stats_ready, one.b_mv_ready, one.b_pool = sem("b_stats"), sem("b_mv"), sem("b_pool")
        one.z_std_ready, one.z_gain_ready, one.z_norm_ready, one.x1_ready, one.x1_bo_ready = (
            sem(n) for n in ("z_std_ready", "z_gain_ready", "z_norm_ready", "x1_ready", "x1_bo_ready"))
        one.x1T_psum, one.x1T_ready = sem("x1T_psum"), sem("x1T_ready")
        one.q_psum, one.q_hi_ready, one.q_lo_ready = sem("q_psum"), sem("q_hi_ready"), sem("q_lo_ready")
        one.k_psum, one.k_hi_ready, one.k_lo_ready = sem("k_psum"), sem("k_hi_ready"), sem("k_lo_ready")
        one.v_psum, one.v_copied = sem("v_psum"), sem("v_copied")
        one.q_written, one.k_written = ([sem(f"{n}_written{i}") for i in range(2)] for n in "qk")
        one.stacked = [sem(f"stacked{i}") for i in range(2)]

        layer0(nc, whole, tensor, sem, psum, x_dram, adj, alpha, w, d, fc_w, fc_b,
               (bc, g1, be1, bo, g2, be2, b2, g3, be3), (Wc, Wq, Wk, Wv, Wo), (W1, W2, b1), one,
               y, adjT, mask, ident, ones, exponent, two_over_lam, waited)
        layer1(nc, whole, tensor, sem, psum, one, out_dram, y, mask, ident, exponent, waited)


def inverse_root(pool, b, mv, mv_ready, var_eps, rstd, pool_step, used_sem, used, exponent, pool_waited):
    pool.wait_ge(mv_ready, b + 1)
    at_least(pool, pool_step, 2 * b)
    at_least(pool, used_sem, used)
    pool.sem_inc(pool_waited, 1)
    pool.tensor_scalar(var_eps[:, :], mv[:, :, 1], EPS, None, ALU.add).then_inc(pool_step, 1)
    pool.wait_ge(pool_step, 2 * b + 1)
    pool.tensor_tensor(out=rstd[:, :], in0=var_eps[:, :], in1=exponent[:, :], op=ALU.pow).then_inc(pool_step, 1)


def h_scales(pool, one, b, s):
    inverse_root(pool, b, one.mv, one.mv_ready, one.var_eps, one.rstd[s], one.pool_step, one.h_ready, NT * (b - 1),
                 one.exponent, one.pool_waited)
    pool.wait_ge(one.pool_step, 2 * b + 2)
    pool.tensor_tensor(out=one.mean_rstd[:, :], in0=one.mv[:, :, 0], in1=one.rstd[s][:, :],
                       op=ALU.mult).then_inc(one.scales, 1)
    pool.wait_ge(one.scales, 2 * b + 1)
    pool.tensor_tensor(out=one.shift[s][:, :], in0=one.mean_rstd[:, :], in1=one.minus_one[:, :],
                       op=ALU.mult).then_inc(one.scales, 1)


def normalise(act, one, b, s, t):
    if t == 0:
        act.wait_ge(one.scales, 2 * b + 2)
        at_least(act, one.x1_ready, b - 1)
    act.activation(one.h[s][:, t, :], one.y[:, bass.ds(b * N + t * D, D)], ACT.Relu,
                   scale=one.rstd[s][:, t:t + 1], bias=one.shift[s][:, t:t + 1]).then_inc(one.h_ready, 1)


def all_tiles(one, row):
    return one.bc_all[:, row:row + 1, :].broadcast_to([P, NT, D])


def flat(t):
    return t[:, :, :].rearrange("p t d -> p (t d)")


def products(left, right):
    (left_hi, left_lo), (right_hi, right_lo) = left, right
    return (left_hi, right_hi), (left_hi, right_lo), (left_lo, right_hi)


def conv(pe, one, bank, b, s, k):
    pe.wait_ge(one.h_ready, NT * b + k + 1)
    last = pe.matmul(bank[:, :], one.h[s][:, k, :], one.Lnorm[:, k, :], start=k == 0, stop=k == NT - 1)
    if k == NT - 1:
        last.then_inc(one.conv_psum, 1)


def conv_out(act, one, bank, b):
    act.wait_ge(one.conv_psum, b + 1)
    act.activation(one.convT[:, :], bank[:, :], ACT.Copy).then_inc(one.conv_ready, 1)


def conv_weights(pe, one, bank, b):
    pe.wait_ge(one.conv_ready, b + 1)
    for t in range(NT):
        last = pe.matmul(bank[:, t * D:(t + 1) * D], one.convT[:, t * P:(t + 1) * P], one.Wcs[:, :],
                         start=True, stop=True)
    last.then_inc(one.z_psum, 1)


def z_out(dve, one, bank, b):
    dve.wait_ge(one.z_psum, b + 1)
    at_least(dve, one.z_std_ready, b)
    dve.tensor_tensor(out=one.z[:, :, :], in0=bank[:, :].rearrange("p (t d) -> p t d", d=D),
                      in1=all_tiles(one, BC), op=ALU.add).then_inc(one.z_ready, 1)


def moments(dve, b, source, stats, stats_sem, mv, mv_sem, used_sem, used, dve_waited):
    at_least(dve, mv_sem, b)
    for t in range(NT):
        last = dve.bn_stats(stats[:, t, :], source(t))
    last.then_inc(stats_sem, 1)
    dve.wait_ge(stats_sem, b + 1)
    at_least(dve, used_sem, used)
    dve.sem_inc(dve_waited, 1)
    for t in range(NT):
        last = dve.bn_aggr(mv[:, t, :], stats[:, t, :])
    last.then_inc(mv_sem, 1)


def y_moments(dve, one, b):
    moments(dve, b, lambda t: one.y[:, bass.ds(b * N + t * D, D)], one.stats, one.stats_ready, one.mv, one.mv_ready,
            one.scales, 2 * b, one.dve_waited)


def z_moments(dve, one, b):
    dve.wait_ge(one.z_ready, b + 1)
    moments(dve, b, lambda t: one.z[:, t, :], one.b_stats, one.b_stats_ready, one.b_mv, one.b_mv_ready,
            one.z_std_ready, b, one.dve_waited)


def standardise(dve, out, source, mv, rstd, done):
    for t in range(NT):
        last = dve.tensor_scalar(out[:, t, :], source[:, t, :], mv[:, t, 0:1], rstd[:, t:t + 1],
                                 ALU.subtract, ALU.mult)
    last.then_inc(done, 1)


def z_standard(dve, one, b):
    dve.wait_ge(one.b_pool, 2 * b + 2)
    at_least(dve, one.z_gain_ready, b)
    standardise(dve, one.z_std, one.z, one.b_mv, one.b_rstd, one.z_std_ready)


def z_root(pool, one, b):
    inverse_root(pool, b, one.b_mv, one.b_mv_ready, one.b_var_eps, one.b_rstd, one.b_pool, one.z_std_ready, b,
                 one.exponent, one.pool_waited)


def norm_z(pool, one, b):
    pool.wait_ge(one.z_std_ready, b + 1)
    pool.tensor_tensor(out=one.z_gain[:, :, :], in0=one.z_std[:, :, :], in1=all_tiles(one, G1),
                       op=ALU.mult).then_inc(one.z_gain_ready, 1)
    pool.wait_ge(one.z_gain_ready, b + 1)
    at_least(pool, one.x1_ready, b)
    pool.tensor_tensor(out=one.z_norm[:, :, :], in0=one.z_gain[:, :, :], in1=all_tiles(one, BE1),
                       op=ALU.add).then_inc(one.z_norm_ready, 1)


def residual(dve, one, b, s):
    dve.wait_ge(one.z_norm_ready, b + 1)
    at_least(dve, one.x1T_psum, b - 1)
    at_least(dve, one.x1_bo_ready, b - 1)
    dve.scalar_tensor_tensor(out=flat(one.x1[s]), in0=flat(one.z_norm), scalar=0.0, in1=flat(one.h[s]),
                             op0=ALU.max, op1=ALU.add).then_inc(one.x1_ready, 1)


def x1_transpose(pe, one, bank, b, s):
    pe.wait_ge(one.x1_ready, b + 1)
    for t in range(NT):
        last = pe.transpose(bank[:, t * P:(t + 1) * P], one.x1[s][:, t, :], one.ident[:, :])
    last.then_inc(one.x1T_psum, 1)


def x1T_out(act, one, bank, b):
    act.wait_ge(one.x1T_psum, b + 1)
    at_least(act, one.v_psum, b)
    act.activation(one.x1T[:, :], bank[:, :], ACT.Copy).then_inc(one.x1T_ready, 1)


def k_product(pe, one, bank, b):
    pe.wait_ge(one.x1T_ready, b + 1)
    pe.matmul(bank[:, :], one.Wks[:, :], one.x1T[:, :], start=True, stop=True).then_inc(one.k_psum, 1)


def q_product(pe, one, bank, b):
    pe.matmul(bank[:, :], one.Wqs[:, :], one.x1T[:, :], start=True, stop=True).then_inc(one.q_psum, 1)


def v_product(pe, one, bank, b):
    for t in range(NT):
        last = pe.matmul(bank[:, t * D:(t + 1) * D], one.x1T[:, t * P:(t + 1) * P], one.Wvs[:, :],
                         start=True, stop=True)
    last.then_inc(one.v_psum, 1)


def k_hi_out(act, one, bank, b, s, half):
    act.wait_ge(one.k_psum, b + 1)
    if not (isinstance(b, int) and b == 0):
        act.wait_ge(one.k_written[1 - s], 16 * (half + s))
    act.activation(one.k_parts[:, 0, :], bank[:, :], ACT.Copy).then_inc(one.k_hi_ready, 1)


def q_hi_out(act, one, bank, b, s, half):
    act.wait_ge(one.q_psum, b + 1)
    if not (isinstance(b, int) and b == 0):
        act.wait_ge(one.q_written[1 - s], 16 * (half + s))
    act.activation(one.q_parts[:, 0, :], bank[:, :], ACT.Copy, scale=-float(HD) ** -0.5).then_inc(one.q_hi_ready, 1)


def k_lo_out(dve, one, bank, b):
    dve.wait_ge(one.k_hi_ready, b + 1)
    dve.tensor_tensor(out=one.k_parts[:, 1, :], in0=bank[:, :], in1=one.k_parts[:, 0, :].bitcast(F32),
                      op=ALU.subtract).then_inc(one.k_lo_ready, 1)


def q_lo_out(dve, one, bank, b):
    dve.wait_ge(one.q_hi_ready, b + 1)
    dve.scalar_tensor_tensor(out=one.q_parts[:, 1, :], in0=bank[:, :], scalar=-float(HD) ** -0.5,
                             in1=one.q_parts[:, 0, :].bitcast(F32), op0=ALU.mult,
                             op1=ALU.subtract).then_inc(one.q_lo_ready, 1)


def v_out(act, one, bank, b, s):
    act.wait_ge(one.v_psum, b + 1)
    act.activation(flat(one.v[s]), bank[:, :], ACT.Copy).then_inc(one.v_copied, 1)


def stack(sp, one, b, s, half):
    for n, (tile, ready, parts_of, written) in enumerate((
            (one.k_stack, one.k_lo_ready, one.k_parts, one.k_written),
            (one.q_stack, one.q_lo_ready, one.q_parts, one.q_written))):
        sp.wait_ge(ready, b + 1)
        sp.dma_start(one.bounce[n][s].rearrange("a p n -> p a n"), parts_of[:, :, :].bitcast(F32)
                     ).then_inc(written[s], 16)
        sp.wait_ge(written[s], 16 * (half + 1))
        for j, part in enumerate(((0, 1, 0, 1), (0, 0, 1, 1))[n]):
            sp.dma_start(tile[s][j * HD:(j + 1) * HD, :, :].bitcast(F32),
                         one.bounce[n][s][part, :, :].rearrange("(h d) n -> d h n", h=HEADS)
                         ).then_inc(one.stacked[s], 16)


def layer0(nc, whole, tensor, sem, psum, x_dram, adj, alpha, w, d, fc_w, fc_b, rows, weights, mlp, one,
           y, adjT, mask, ident, ones, exponent, two_over_lam, waited):
    dve_waited, pool_waited = waited
    with ExitStack() as ctx:
        def sb(name, shape, dt=F32):
            return tensor(ctx, name, shape, dt)

        alpha_in = sb("alpha_in", [P, NT])
        w_in, fc_in, wT, dwT = one.w_in, one.fc_in, one.wT, one.dwT
        d_in = sb("d_in", [P, 1])
        b_in = sb("b_in", [P, 1])
        P3T = sb("P3T", [P, NT, N])
        a_exp = sb("a_exp", [P, NT])
        a_one = sb("a_one", [P, NT])
        a_sig = sb("a_sig", [P, NT])
        edge_scale = sb("edge_scale", [P, NT])
        self_scale = sb("self_scale", [P, NT])
        d_clip = sb("d_clip", [P, 1])
        d_dt = sb("d_dt", [P, 1])
        powers = one.powers
        W = powers[:, 1, 0:D]
        B = one.B
        B_parts = [sb(f"B_{part}", [P, GROUP, GROUP, D], F32R) for part in ("hi", "lo")]
        U = sb("U", [P, NT, GROUP])
        beta = sb("beta", [P, STEPS + 1])
        U_rows = one.U_rows
        beta_rows = sb("beta_rows", [GROUP, GROUP * D])
        bias = sb("bias", [P, NT, GROUP, D])
        S, Sq = one.S, one.Sq
        row_sum = sb("row_sum", [P, 1])
        shift = sb("shift", [P, 1])
        diagonal = sb("diagonal", [P, NT, D], BF16)
        trace_part = sb("trace_part", [P, 1])
        trace = sb("trace", [P, 1])
        trace_inv = sb("trace_inv", [P, 1])
        trace_inv2 = sb("trace_inv2", [P, 1])
        v = sb("v", [P, NT])
        Sv = sb("Sv", [P, NT])
        scratch4 = sb("scratch4", [P, NT])
        quotient = sb("quotient", [P, 2])
        quotient_all = sb("quotient_all", [P, 2])
        den_inv = sb("den_inv", [P, 1])
        lam = sb("lam", [P, 1])
        lam_inv = sb("lam_inv", [P, 1])
        x_in = [sb(f"x_in{i}", [P, NT, D]) for i in range(2)]
        stats = sb("stats", [P, NT, 6])
        mv = [sb(f"mv{i}", [P, NT, 2]) for i in range(2)]
        var_eps = [sb(f"var_eps{i}", [P, NT]) for i in range(2)]
        rstd = [sb(f"rstd{i}", [P, NT]) for i in range(2)]
        mean_rstd = [sb(f"mean_rstd{i}", [P, NT]) for i in range(2)]
        shift_ln = [sb(f"shift_ln{i}", [P, NT]) for i in range(2)]
        x0 = sb("x0", [P, NT, D])
        x_bias = sb("x_bias", [P, NT, D])
        x0_parts = [[sb(f"x0_{part}{i}", [P, NT, D], F32R) for part in ("hi", "lo")] for i in range(2)]
        T_parts = [[[sb(f"T{m}_{part}{i}", [P, N], F32R) for part in ("hi", "lo")] for m in range(GROUP)]
                   for i in range(2)]
        C2 = sb("C2", [P, NT, D])
        Y1 = sb("Y1", [P, NT, D])

        with ExitStack() as early:
            A, Pn, PT, P2T = (tensor(early, n, [P, NT, N]) for n in ("A", "Pn", "PT", "P2T"))
        PT_hi, P2T_hi, PT_lo, P2T_lo = (sb(n, [P, NT, N], F32R) for n in ("PT_hi", "P2T_hi", "PT_lo", "P2T_lo"))
        PT_parts, P2T_parts = (PT_hi, PT_lo), (P2T_hi, P2T_lo)

        loaded = sem("adj_loaded")
        small_loaded = sem("small_loaded")
        x_loaded = [sem(f"x_loaded{i}") for i in range(2)]
        consts_set = sem("consts_set")
        alpha_exp = sem("alpha_exp")
        dve_setup = sem("dve_setup")
        ident_ready = sem("ident_ready")
        P_ready = sem("P_ready")
        PT_psum = sem("PT_psum")
        PT_ready = sem("PT_ready")
        adjT_psum = sem("adjT_psum")
        adjT_ready = sem("adjT_ready")
        wT_psum = sem("wT_psum")
        wT_ready = sem("wT_ready")
        weff_psum = sem("weff_psum")
        power_psum = sem("power_psum")
        power_ready = sem("power_ready")
        FW_psum = sem("FW_psum")
        B_step = sem("B_step")
        P2_psum = sem("P2_psum")
        P2_ready = sem("P2_ready")
        P3_psum = sem("P3_psum")
        P3_ready = sem("P3_ready")
        U_psum = sem("U_psum")
        U_ready = sem("U_ready")
        beta_ready = sem("beta_ready")
        rows_psum = sem("rows_psum")
        rows_ready = sem("rows_ready")
        bias_psum = sem("bias_psum")
        bias_ready = sem("bias_ready")
        S_ready = sem("S_ready")
        sum_psum = sem("sum_psum")
        S0_ready = sem("S0_ready")
        trace_part_ready = sem("trace_part_ready")
        trace_psum = sem("trace_psum")
        trace_step = sem("trace_step")
        square_psum = sem("square_psum")
        square_ready = sem("square_ready")
        v_ready = sem("v_ready")
        Sv_psum = sem("Sv_psum")
        Sv_step = sem("Sv_step")
        quotient_psum = sem("quotient_psum")
        lam_step = sem("lam_step")
        stats_ready = sem("stats_ready")
        mv_ready = sem("mv_ready")
        ln_pool = sem("ln_pool")
        x0_ready = sem("x0_ready")
        x_bias_ready = sem("x_bias_ready")
        T_psum = [sem(f"T{m}_psum") for m in range(GROUP)]
        T_hi_ready, T_lo_ready = ([sem(f"T{m}_{part}_ready") for m in range(GROUP)] for part in ("hi", "lo"))
        x0_hi_ready, x0_lo_ready = sem("x0_hi_ready"), sem("x0_lo_ready")
        PT_hi_ready, PT_lo_ready, B_hi_ready, B_lo_ready = (
            sem(n) for n in ("PT_hi_ready", "PT_lo_ready", "B_hi_ready", "B_lo_ready"))
        C_psum = sem("C_psum")
        C2_ready = sem("C2_ready")
        Y1_psum = sem("Y1_psum")
        Y1_ready = sem("Y1_ready")
        Y0_psum = sem("Y0_psum")
        y_ready = sem("y_ready")

        SQ_BANK = psum[7]

        def FW(k):
            return psum[4 + k // NT][:, k % NT * D:(k % NT + 1) * D] if k < STEPS else SQ_BANK[:, D:2 * D]

        def first_squaring(r, s):
            return (2 * r, 0) if isinstance(r, int) and r < 2 else (r + 2, s)

        def squares_again(r):
            return isinstance(r, int) and r < 2

        ident_tiles = ident[:, :].unsqueeze(1).broadcast_to([P, NT, D])
        n_B = sum(STEPS - j for j in range(STEPS))

        def diagonal_of(tile):
            a = tile[:, :, 0:D]
            step = list(map(list, a.ap))
            step[1][0] += D
            return bass.AP(tensor=a.tensor, offset=a.offset, ap=step)

        with nc.Block() as block:

            @block.sync
            def _(sp):
                adj_tiles = adj.rearrange("(t p) m -> p t m", p=P)
                for t in range(NT):
                    sp.dma_start(A[:, t, :], adj_tiles[:, t, :]).then_inc(loaded, 16)
                sp.dma_start(alpha_in[:, :], alpha.rearrange("(t p) -> p t", p=P),
                             allow_slow_non_contiguous=True).then_inc(small_loaded, 16)
                sp.dma_start(w_in[:, :], w).then_inc(small_loaded, 16)
                sp.dma_start(fc_in[:, :], fc_w).then_inc(small_loaded, 16)
                sp.dma_start(d_in[:, :], d.rearrange("(p o) -> p o", o=1)).then_inc(small_loaded, 16)
                sp.dma_start(b_in[:, :], fc_b.rearrange("(p o) -> p o", o=1)).then_inc(small_loaded, 16)

                def load_layer1_weights():
                    for n, row in enumerate(rows):
                        sp.dma_start(one.row_in[:, n, :], row.rearrange("(o d) -> o d", o=1)
                                     ).then_inc(one.rows_loaded, 16)
                    for tile, source in zip((one.Wcs, one.Wqs, one.Wks, one.Wvs, one.Wos), weights):
                        sp.dma_start(tile[:, :], source).then_inc(one.weights_loaded, 16)
                    W1, W2, b1 = mlp
                    sp.dma_start(one.W1s[:, :], W1).then_inc(one.mlp_loaded, 16)
                    sp.dma_start(one.W2s[:, :, :], W2.rearrange("(j p) d -> p j d", p=P)).then_inc(one.mlp_loaded, 16)
                    sp.dma_start(one.b1s[:, :], b1.rearrange("(j p) -> p j", p=P),
                                 allow_slow_non_contiguous=True).then_inc(one.mlp_loaded, 16)

                def load_x(b, s, half):
                    at_least(sp, x0_ready, b - 1)
                    at_least(sp, x_bias_ready, b - 1)
                    sp.dma_start(x_in[s][:, :, :], x_dram[:, bass.ds(b, 1), :, :].rearrange("p b t d -> p (b t) d")
                                 ).then_inc(x_loaded[s], 16)
                    if isinstance(b, int) and b == 1:
                        load_layer1_weights()
                rounds(sp, load_x, 2, BATCH, BATCH)
                stack(sp, one, 0, 0, 0)

            @block.gpsimd
            def _(pool):
                pool.memset(ident[:, :], 0.0).then_inc(consts_set, 1)
                pool.memset(ones[:, :], 1.0).then_inc(consts_set, 1)
                pool.memset(exponent[:, :], -0.5).then_inc(consts_set, 1)
                pool.memset(one.minus_one[:, :], -1.0).then_inc(one.minus_set, 1)
                pool.wait_ge(consts_set, 1)
                pool.affine_select(out=ident[:, :], in_=ident[:, :], compare_op=ALU.not_equal, fill=1.0, base=0,
                                   pattern=[[-1, P]], channel_multiplier=1).then_inc(ident_ready, 1)

                def scales(b, s):
                    pool.wait_ge(mv_ready, b + 1)
                    at_least(pool, x0_ready, b - 1)
                    pool.sem_inc(pool_waited, 1)
                    pool.tensor_scalar(var_eps[s][:, :], mv[s][:, :, 1], EPS, None, ALU.add).then_inc(ln_pool, 1)
                    pool.wait_ge(consts_set, 3)
                    pool.wait_ge(ln_pool, 4 * b + 1)
                    pool.tensor_tensor(out=rstd[s][:, :], in0=var_eps[s][:, :], in1=exponent[:, :],
                                       op=ALU.pow).then_inc(ln_pool, 1)
                    pool.wait_ge(ln_pool, 4 * b + 2)
                    pool.tensor_tensor(out=mean_rstd[s][:, :], in0=mv[s][:, :, 0], in1=rstd[s][:, :],
                                       op=ALU.mult).then_inc(ln_pool, 1)
                    pool.wait_ge(ln_pool, 4 * b + 3)
                    pool.sem_inc(pool_waited, 1)
                    pool.tensor_scalar(shift_ln[s][:, :], mean_rstd[s][:, :], -1.0, None,
                                       ALU.mult).then_inc(ln_pool, 1)

                def round_(r, s, half):
                    if isinstance(r, int) and r == BATCH - 2:
                        pool.wait_ge(one.minus_set, 1)
                        for b in range(2):
                            h_scales(pool, one, b, b)
                    if within(r, 0, BATCH - 2):
                        scales(r + 1, 1 - s)
                    if isinstance(r, int) and r == BATCH - 1:
                        z_root(pool, one, 0)
                        norm_z(pool, one, 0)
                    b = r
                    pool.wait_ge(bias_ready, NT)
                    at_least(pool, y_ready, NT * b)
                    pool.tensor_tensor(out=x_bias[:, :, :], in0=x_in[s][:, :, :], in1=bias[:, :, 0, :],
                                       op=ALU.add).then_inc(x_bias_ready, 1)
                scales(0, 0)
                rounds(pool, round_, 2, BATCH - 2, BATCH)
                z_root(pool, one, 1)
                norm_z(pool, one, 1)
                h_scales(pool, one, 2, 0)

            @block.tensor
            def _(pe):
                pe.wait_ge(ident_ready, 1)
                pe.wait_ge(loaded, 16 * NT)
                for mt in range(NT):
                    for nt in range(NT):
                        last = pe.transpose(psum[mt][:, nt * P:(nt + 1) * P], A[:, nt, mt * P:(mt + 1) * P],
                                            ident[:, :])
                    last.then_inc(adjT_psum, 1)
                pe.wait_ge(small_loaded, 16 * 5)
                pe.transpose(psum[4][:, 0:D], w_in[:, :], ident[:, :]).then_inc(wT_psum, 1)
                pe.wait_ge(wT_ready, 2)
                pe.matmul(psum[5][:, 0:D], wT[:, :], dwT[:, :], start=True, stop=True).then_inc(weff_psum, 1)
                pe.wait_ge(P_ready, 2 * NT)
                for mt in range(NT):
                    pe.wait_ge(adjT_ready, mt + 1)
                    for nt in range(NT):
                        last = pe.transpose(psum[mt][:, nt * P:(nt + 1) * P], Pn[:, nt, mt * P:(mt + 1) * P],
                                            ident[:, :])
                    last.then_inc(PT_psum, 1)
                for k in range(1, STEPS + 1):
                    pe.wait_ge(power_ready, k)
                    pe.matmul(psum[5][:, 0:D + 1], W, powers[:, k - 1, :], start=True,
                              stop=True).then_inc(power_psum, 1)
                pe.wait_ge(PT_ready, NT)
                for mt in range(NT):
                    for k in range(NT):
                        last = pe.matmul(psum[mt][:, :], Pn[:, k, mt * P:(mt + 1) * P], PT[:, k, :],
                                         start=k == 0, stop=k == NT - 1)
                    last.then_inc(P2_psum, 1)
                pe.wait_ge(S_ready, 2)
                pe.matmul(SQ_BANK[:, 0:1], ones[:, :], row_sum[:, :], start=True, stop=True).then_inc(sum_psum, 1)
                pe.wait_ge(power_ready, STEPS + 1)
                for k in range(STEPS + 1):
                    last = pe.matmul(FW(k), fc_in[:, :],
                                     powers[:, k, 0:D], start=True, stop=True)
                last.then_inc(FW_psum, 1)
                pe.wait_ge(P2_ready, NT)

                pe.wait_ge(U_ready, 2)
                for nt in range(NT):
                    for k in range(NT):
                        last = pe.matmul(psum[6][:, nt:nt + 1], PT[:, k, nt * P:(nt + 1) * P], U[:, k, 1:2],
                                         start=k == 0, stop=k == NT - 1)
                last.then_inc(U_psum, 1)
                for mt in range(NT):
                    for k in range(NT):
                        last = pe.matmul(psum[mt][:, :], Pn[:, k, mt * P:(mt + 1) * P], P2T[:, k, :],
                                         start=k == 0, stop=k == NT - 1)
                    last.then_inc(P3_psum, 1)
                pe.wait_ge(P3_ready, NT)

                def bias_rows():
                    pe.wait_ge(one.rows_copied, 3)
                    pe.wait_ge(U_ready, GROUP)
                    pe.wait_ge(beta_ready, STEPS + 1)
                    for nt in range(NT):
                        pe.transpose(psum[1][0:GROUP, nt * P:(nt + 1) * P], U[:, nt, :], ident[:, :])
                    for i in range(GROUP):
                        last = pe.transpose(psum[2][0:GROUP, i * D:(i + 1) * D], beta[:, i * GROUP:(i + 1) * GROUP],
                                            ident[:, :])
                    last.then_inc(rows_psum, 1)

                def bias_part():
                    pe.wait_ge(rows_ready, 2)
                    for nt in range(NT):
                        pe.matmul(psum[nt][:, 0:GROUP * D], U_rows[:, nt * P:(nt + 1) * P], beta_rows[:, :],
                                  start=True, stop=True).then_inc(bias_psum, 1)

                pe.wait_ge(B_step, STEPS + 1 + n_B)
                pe.wait_ge(one.rows_loaded, 16 * ROWS)
                row_flat = one.row_in[:, :, :].rearrange("o r d -> o (r d)")
                for c in range(3):
                    cols = min(N, ROWS * D - c * N)
                    pe.matmul(psum[1 + c][:, 0:cols], ones[0:1, :], row_flat[:, c * N:c * N + cols], start=True,
                              stop=True).then_inc(one.rows_spread, 1)

                def trace_sum(q):
                    pe.wait_ge(trace_part_ready, q + 1)
                    pe.matmul(SQ_BANK[:, 0:1], ones[:, :], trace_part[:, :], start=True,
                              stop=True).then_inc(trace_psum, 1)

                def square(q, s, mt, bank=SQ_BANK):
                    if mt == 0:
                        pe.wait_ge(trace_step, 3 * q + 1)
                    elif bank is SQ_BANK:
                        pe.wait_ge(square_ready, NT * q + mt)
                    for k in range(NT):
                        last = pe.matmul(bank[:, :], Sq[s][:, k, mt * P:(mt + 1) * P], Sq[s][:, k, :],
                                         start=k == 0, stop=k == NT - 1)
                    last.then_inc(square_psum, 1)

                def node_product(bank, s, power_parts):
                    for k in range(NT):
                        for n, (x, p) in enumerate(products(x0_parts[s], power_parts)):
                            last = pe.matmul(bank[:, :], x[:, k, :], p[:, k, :], start=k == 0 and n == 0,
                                             stop=k == NT - 1 and n == 2)
                    return last

                def early(r, at):
                    step = (r - (BATCH - 2), at) if isinstance(r, int) else None
                    if step == (0, 1):
                        pe.wait_ge(v_ready, 1)
                        for nt in range(NT):
                            for k in range(NT):
                                last = pe.matmul(SQ_BANK[:, nt:nt + 1], S[:, k, nt * P:(nt + 1) * P], v[:, k:k + 1],
                                                 start=k == 0, stop=k == NT - 1)
                        last.then_inc(Sv_psum, 1)
                    if step == (0, 2):
                        pe.wait_ge(Sv_step, 3)
                        pe.matmul(SQ_BANK[:, NT:NT + 2], ones[:, :], quotient[:, :], start=True,
                                  stop=True).then_inc(quotient_psum, 1)
                    if step == (1, 0):
                        pe.wait_ge(one.weights_loaded, 16 * 5)
                        pe.wait_ge(lam_step, 6 + NT)
                        for k in range(NT):
                            conv(pe, one, SQ_BANK, 0, 0, k)
                    if step == (1, 1):
                        conv_weights(pe, one, SQ_BANK, 0)
                    if step == (1, 3):
                        pe.wait_ge(one.z_ready, 1)
                        for k in range(NT):
                            conv(pe, one, SQ_BANK, 1, 1, k)
                    if step == (1, 4):
                        conv_weights(pe, one, SQ_BANK, 1)
                        x1_transpose(pe, one, psum[4], 0, 0)
                    if step == (2, 5):
                        k_product(pe, one, psum[5], 0)
                        q_product(pe, one, psum[6], 0)
                    if step == (2, 4):
                        v_product(pe, one, psum[4], 0)

                def round_(r, s, half):
                    enters, leaves, squares = within(r, 0, BATCH - 1), within(r, 1, BATCH), within(r, 0, BATCH - 3)
                    q, qs = first_squaring(r, s)
                    if isinstance(r, int) and r == 1:
                        pe.wait_ge(B_lo_ready, 1)
                        pe.wait_ge(bias_ready, NT)
                    if leaves:
                        for m in range(GROUP):
                            pe.wait_ge(T_lo_ready[m], r)
                        for nt in range(NT):
                            at_least(pe, y_ready, NT * (r - 2) + nt + 1)
                            if nt == 1:
                                early(r, 5)
                            for m in range(GROUP):
                                for n, (t, b) in enumerate(products(T_parts[1 - s][m], B_parts)):
                                    last = pe.matmul(psum[nt][:, 0:GROUP * D], t[:, nt * P:(nt + 1) * P],
                                                     b[:, m, :, :].rearrange("p i d -> p (i d)"),
                                                     start=m == 0 and n == 0, stop=m == GROUP - 1 and n == 2,
                                                     skip_group_check=True)
                            last.then_inc(C_psum, 1)
                    if squares:
                        trace_sum(q)
                    early(r, 0)
                    if enters:
                        pe.wait_ge(x0_ready, r + 1)
                        at_least(pe, T_lo_ready[0], r)
                        for nt in range(NT):
                            last = pe.transpose(psum[4][:, nt * P:(nt + 1) * P], x0[:, nt, :], ident[:, :])
                        last.then_inc(T_psum[0], 1)
                        pe.wait_ge(x0_lo_ready, r + 1)
                        pe.wait_ge(PT_lo_ready, 1)
                        at_least(pe, T_lo_ready[1], r)
                        node_product(psum[5], s, PT_parts).then_inc(T_psum[1], 1)
                    first = isinstance(r, int) and r == 0
                    early(r, 1)
                    if squares:
                        square(q, qs, 0)
                    if leaves:
                        pe.wait_ge(C2_ready, NT * r)
                        for nt in range(NT):
                            for k in range(NT):
                                last = pe.matmul(psum[nt][:, D:2 * D], P3T[:, k, nt * P:(nt + 1) * P], C2[:, k, :],
                                                 start=False, stop=k == NT - 1, skip_group_check=True)
                            last.then_inc(Y1_psum, 1)
                    early(r, 2)
                    if squares:
                        square(q, qs, 1)
                    if first:
                        bias_rows()
                        pe.wait_ge(PT_lo_ready, 2)
                    if enters:
                        at_least(pe, T_lo_ready[2], r)
                        node_product(psum[6], s, P2T_parts).then_inc(T_psum[2], 1)
                    early(r, 3)
                    if squares:
                        square(q, qs, 2)
                    if first:
                        bias_part()
                    if leaves:
                        pe.wait_ge(Y1_ready, NT * r)
                        for nt in range(NT):
                            for k in range(NT):
                                last = pe.matmul(psum[nt][:, 0:D], P3T[:, k, nt * P:(nt + 1) * P], Y1[:, k, :],
                                                 start=False, stop=k == NT - 1, skip_group_check=True)
                            last.then_inc(Y0_psum, 1)
                    early(r, 4)
                    if squares:
                        square(q, qs, 3)
                    if squares_again(r):
                        trace_sum(q + 1)
                        for mt in range(NT):
                            if r == 0:
                                pe.wait_ge(bias_ready, NT)
                            else:
                                pe.wait_ge(y_ready, mt + 1)
                            square(q + 1, 1, mt, psum[mt])
                        pe.wait_ge(square_ready, NT * (q + 2))
                rounds(pe, round_, 2, BATCH - 2, BATCH + 1)

            @block.scalar
            def _(act):
                act.wait_ge(small_loaded, 16 * 5)
                act.activation(a_exp[:, :], alpha_in[:, :], ACT.Exp, scale=-1.0).then_inc(alpha_exp, 1)
                for mt in range(NT):
                    act.wait_ge(adjT_psum, mt + 1)
                    act.activation(adjT[:, mt, :], psum[mt][:, :], ACT.Copy).then_inc(adjT_ready, 1)
                for mt in range(NT):
                    act.wait_ge(PT_psum, mt + 1)
                    act.activation(PT[:, mt, :], psum[mt][:, :], ACT.Copy).then_inc(PT_ready, 1)
                for mt in range(NT):
                    act.wait_ge(P2_psum, mt + 1)
                    act.activation(P2T[:, mt, :], psum[mt][:, :], ACT.Copy).then_inc(P2_ready, 1)
                def enter(b, s):
                    act.wait_ge(ln_pool, 4 * b + 4)
                    at_least(act, T_psum[2], b - 1)
                    at_least(act, x0_lo_ready, b)
                    at_least(act, T_psum[0], b)
                    for t in range(NT):
                        last = act.activation(x0[:, t, :], x_in[s][:, t, :], ACT.Relu,
                                              scale=rstd[s][:, t:t + 1], bias=shift_ln[s][:, t:t + 1])
                    last.then_inc(x0_ready, 1)
                    act.wait_ge(x0_ready, b + 1)
                    act.activation(x0_parts[s][0][:, :, :], x0[:, :, :], ACT.Copy).then_inc(x0_hi_ready, 1)

                act.wait_ge(PT_ready, NT)
                act.wait_ge(S_ready, 3)
                act.activation(PT_parts[0][:, :, :], PT[:, :, :], ACT.Copy).then_inc(PT_hi_ready, 1)
                enter(0, 0)
                for mt in range(NT):
                    act.wait_ge(P3_psum, mt + 1)
                    act.activation(P3T[:, mt, :], psum[mt][:, :], ACT.Copy).then_inc(P3_ready, 1)
                act.wait_ge(P2_ready, NT)
                act.activation(P2T_parts[0][:, :, :], P2T[:, :, :], ACT.Copy).then_inc(PT_hi_ready, 1)

                def T_hi(m, b, s):
                    act.wait_ge(T_psum[m], b + 1)
                    act.activation(T_parts[s][m][0][:, :], psum[4 + m][:, :], ACT.Copy).then_inc(T_hi_ready[m], 1)

                def square_out(q, s, mt, bank=SQ_BANK):
                    act.wait_ge(square_psum, NT * q + mt + 1)
                    if mt == 0:
                        act.wait_ge(trace_step, 3 * q + 3)
                    act.activation(Sq[1 - s][:, mt, :], bank[:, :], ACT.Copy,
                                   scale=trace_inv2[:, 0:1]).then_inc(square_ready, 1)

                def round_(r, s, half):
                    enters, leaves, squares = within(r, 0, BATCH - 1), within(r, 1, BATCH), within(r, 0, BATCH - 3)
                    q, qs = first_squaring(r, s)
                    last_rounds = r - (BATCH - 2) if isinstance(r, int) else None
                    if last_rounds == 2:
                        k_hi_out(act, one, psum[5], 0, 0, 0)
                        q_hi_out(act, one, psum[6], 0, 0, 0)
                    if last_rounds == 1:
                        conv_out(act, one, SQ_BANK, 0)
                    if enters:
                        T_hi(0, r, s)
                        T_hi(1, r, s)
                    if squares:
                        square_out(q, qs, 0)
                    if last_rounds == 0:
                        for t in range(NT):
                            normalise(act, one, 0, 0, t)
                    if squares:
                        square_out(q, qs, 1)
                    if within(r, 0, BATCH - 2):
                        enter(r + 1, 1 - s)
                    if enters:
                        T_hi(2, r, s)
                    if last_rounds == 0:
                        for t in range(NT):
                            normalise(act, one, 1, 1, t)
                    if last_rounds == 1:
                        conv_out(act, one, SQ_BANK, 1)
                        x1T_out(act, one, psum[4], 0)
                    if last_rounds == 2:
                        v_out(act, one, psum[4], 0, 0)
                        for t in range(NT):
                            normalise(act, one, 2, 0, t)
                    if squares:
                        square_out(q, qs, 2)
                        square_out(q, qs, 3)
                    if squares_again(r):
                        for mt in range(NT):
                            square_out(q + 1, 1, mt, psum[mt])
                act.wait_ge(B_step, STEPS + 1 + n_B)
                act.activation(B_parts[0][:, :, :, :], B[:, :, :, :], ACT.Copy).then_inc(B_hi_ready, 1)
                rounds(act, round_, 2, BATCH - 2, BATCH + 1)

            @block.vector
            def _(dve):
                dve.wait_ge(alpha_exp, 1)
                dve.tensor_scalar(a_one[:, :], a_exp[:, :], 1.0, None, ALU.add).then_inc(dve_setup, 1)
                dve.wait_ge(dve_setup, 1)
                dve.reciprocal(a_sig[:, :], a_one[:, :]).then_inc(dve_setup, 1)
                dve.wait_ge(dve_setup, 2)
                dve.tensor_scalar(edge_scale[:, :], a_sig[:, :], 0.5 * DT, None, ALU.mult).then_inc(dve_setup, 1)
                dve.tensor_scalar(self_scale[:, :], a_sig[:, :], -0.5 * DT, 1.0 - DT, ALU.mult,
                                  ALU.add).then_inc(dve_setup, 1)
                dve.wait_ge(dve_setup, 4)
                dve.wait_ge(ident_ready, 1)
                dve.wait_ge(loaded, 16 * NT)
                for t in range(NT):
                    dve.tensor_scalar(Pn[:, t, :], A[:, t, :], edge_scale[:, t:t + 1], None,
                                      ALU.mult).then_inc(P_ready, 1)
                for t in range(NT):
                    block_t = Pn[:, t, t * P:(t + 1) * P]
                    dve.wait_ge(P_ready, NT)
                    dve.scalar_tensor_tensor(out=block_t, in0=ident[:, :], scalar=self_scale[:, t:t + 1],
                                             in1=block_t, op0=ALU.mult, op1=ALU.add).then_inc(P_ready, 1)
                dve.tensor_scalar(d_clip[:, :], d_in[:, :], 0.0, 1.0, ALU.max, ALU.min).then_inc(dve_setup, 1)
                dve.wait_ge(dve_setup, 5)
                dve.tensor_scalar(d_dt[:, :], d_clip[:, :], DT, None, ALU.mult).then_inc(dve_setup, 1)
                dve.wait_ge(dve_setup, 6)
                dve.wait_ge(wT_psum, 1)
                dve.tensor_copy(wT[:, :], psum[4][:, 0:D]).then_inc(wT_ready, 1)
                dve.tensor_scalar(dwT[:, :], psum[4][:, 0:D], d_dt[:, 0:1], None, ALU.mult).then_inc(wT_ready, 1)
                dve.tensor_copy(powers[:, 0, 0:D], ident[:, :])
                dve.tensor_copy(powers[:, 0, D:D + 1], b_in[:, :])
                dve.wait_ge(weff_psum, 1)
                dve.tensor_copy(W, psum[5][:, 0:D]).then_inc(power_ready, 1)
                dve.wait_ge(power_psum, 1)
                dve.tensor_copy(powers[:, 1, D:D + 1], psum[5][:, D:D + 1]).then_inc(power_ready, 1)
                for k in range(2, STEPS + 1):
                    dve.wait_ge(power_psum, k)
                    dve.tensor_copy(powers[:, k, :], psum[5][:, 0:D + 1]).then_inc(power_ready, 1)
                dve.memset(U[:, :, 0:1], 1.0).then_inc(U_ready, 1)
                dve.wait_ge(power_ready, STEPS + 1)
                for j in range(STEPS + 1):
                    dve.tensor_scalar(beta[:, j:j + 1], powers[:, STEPS - j, D:D + 1], float(comb(STEPS, j)), None,
                                      ALU.mult).then_inc(beta_ready, 1)
                dve.wait_ge(adjT_ready, NT)
                dve.tensor_tensor(out=S[:, :, :], in0=A[:, :, :], in1=adjT[:, :, :], op=ALU.add).then_inc(S_ready, 1)
                dve.wait_ge(S_ready, 1)
                dve.tensor_reduce(row_sum[:, :], S[:, :, :].rearrange("p t n -> p (t n)"), AX.X,
                                  ALU.add).then_inc(S_ready, 1)
                dve.tensor_scalar(mask[:, :, :], A[:, :, :], 0.0, MASKED, ALU.is_le, ALU.mult).then_inc(S_ready, 1)
                def x_moments(b, s, half):
                    dve.wait_ge(x_loaded[s], 16 * (half + 1))
                    at_least(dve, mv_ready, b)
                    for t in range(NT):
                        last = dve.bn_stats(stats[:, t, :], x_in[s][:, t, :])
                    last.then_inc(stats_ready, 1)
                    dve.wait_ge(stats_ready, b + 1)
                    at_least(dve, ln_pool, 4 * (b - 1))
                    dve.sem_inc(dve_waited, 1)
                    for t in range(NT):
                        last = dve.bn_aggr(mv[s][:, t, :], stats[:, t, :])
                    last.then_inc(mv_ready, 1)

                x_moments(0, 0, 0)
                dve.wait_ge(P_ready, 2 * NT)
                dve.tensor_reduce(U[:, :, 1], Pn[:, :, :], AX.X, ALU.add).then_inc(U_ready, 1)
                dve.wait_ge(FW_psum, 1)
                at = {}
                count = 0
                for j in range(STEPS + 1):
                    k = STEPS - j
                    count += 1
                    at[j] = count
                    dve.tensor_scalar(B[:, j % GROUP, j // GROUP, :], FW(k),
                                      float(comb(STEPS, j)), None, ALU.mult).then_inc(B_step, 1)
                for i in range(STEPS):
                    for j in range(STEPS - i):
                        dve.wait_ge(B_step, at[j])
                        count += 1
                        at[j] = count
                        Bj = B[:, j % GROUP, j // GROUP, :]
                        dve.scalar_tensor_tensor(out=Bj, in0=powers[:, i, 0:D], scalar=DT * comb(i + j, j), in1=Bj,
                                                 op0=ALU.mult, op1=ALU.add).then_inc(B_step, 1)
                dve.wait_ge(sum_psum, 1)
                dve.tensor_scalar(shift[:, :], SQ_BANK[:, 0:1], 0.5 / N, TINY, ALU.mult,
                                  ALU.add).then_inc(S0_ready, 1)
                dve.tensor_scalar(S[:, :, :], S[:, :, :], 0.5, None, ALU.mult).then_inc(S0_ready, 1)
                dve.wait_ge(S0_ready, 2)
                dve.tensor_copy(Sq[0][:, :, :], S[:, :, :]).then_inc(S0_ready, 1)
                dve.wait_ge(S0_ready, 3)
                for t in range(NT):
                    dve.scalar_tensor_tensor(out=Sq[0][:, t, t * P:(t + 1) * P], in0=ident[:, :],
                                             scalar=shift[:, 0:1], in1=S[:, t, t * P:(t + 1) * P],
                                             op0=ALU.mult, op1=ALU.add).then_inc(S0_ready, 1)
                dve.wait_ge(S0_ready, 3 + NT)
                dve.tensor_tensor_reduce(diagonal[:, :, :], diagonal_of(Sq[0]).bitcast(F32), ident_tiles, 1.0, 0.0,
                                         ALU.mult, ALU.add, trace_part[:, :]).then_inc(trace_part_ready, 1)
                def x0_lo(b, s):
                    dve.wait_ge(x0_hi_ready, b + 1)
                    dve.tensor_tensor(out=x0_parts[s][1][:, :, :], in0=x0[:, :, :],
                                      in1=x0_parts[s][0][:, :, :].bitcast(F32), op=ALU.subtract
                                      ).then_inc(x0_lo_ready, 1)

                def T_lo(m, b, s):
                    dve.wait_ge(T_hi_ready[m], b + 1)
                    dve.tensor_tensor(out=T_parts[s][m][1][:, :], in0=psum[4 + m][:, :],
                                      in1=T_parts[s][m][0][:, :].bitcast(F32), op=ALU.subtract
                                      ).then_inc(T_lo_ready[m], 1)

                def early(r, at):
                    step = (r - (BATCH - 2), at) if isinstance(r, int) else None
                    if step == (0, 0):
                        for b in range(2):
                            y_moments(dve, one, b)
                        dve.tensor_reduce(v[:, :], Sq[0][:, :, :].bitcast(F32), AX.X, ALU.add).then_inc(v_ready, 1)
                    if step == (0, 1):
                        dve.wait_ge(Sv_psum, 1)
                        dve.tensor_copy(Sv[:, :], SQ_BANK[:, 0:NT]).then_inc(Sv_step, 1)
                        dve.wait_ge(Sv_step, 1)
                        dve.tensor_tensor_reduce(scratch4[:, :], v[:, :], Sv[:, :], 1.0, 0.0, ALU.mult, ALU.add,
                                                 quotient[:, 0:1]).then_inc(Sv_step, 1)
                        dve.wait_ge(Sv_step, 2)
                        dve.tensor_tensor_reduce(scratch4[:, :], v[:, :], v[:, :], 1.0, 0.0, ALU.mult, ALU.add,
                                                 quotient[:, 1:2]).then_inc(Sv_step, 1)
                    if step == (0, 2):
                        dve.wait_ge(quotient_psum, 1)
                        dve.tensor_scalar(quotient_all[:, :], SQ_BANK[:, NT:NT + 2], TINY, None,
                                          ALU.max).then_inc(lam_step, 1)
                        dve.wait_ge(lam_step, 1)
                        dve.reciprocal(den_inv[:, :], quotient_all[:, 1:2]).then_inc(lam_step, 1)
                        dve.wait_ge(lam_step, 2)
                        dve.tensor_scalar(lam[:, :], quotient_all[:, 0:1], den_inv[:, 0:1], 1e-8, ALU.mult,
                                          ALU.add).then_inc(lam_step, 1)
                        dve.wait_ge(lam_step, 3)
                        dve.reciprocal(lam_inv[:, :], lam[:, :]).then_inc(lam_step, 1)
                        dve.wait_ge(lam_step, 4)
                        dve.tensor_scalar(two_over_lam[:, :], lam_inv[:, :], 2.0, None, ALU.mult).then_inc(lam_step, 1)
                        dve.wait_ge(lam_step, 5)
                        dve.tensor_scalar(adjT[:, :, :], adjT[:, :, :], two_over_lam[:, 0:1], None,
                                          ALU.mult).then_inc(lam_step, 1)
                        dve.wait_ge(lam_step, 6)
                        for t in range(NT):
                            own = adjT[:, t, t * P:(t + 1) * P]
                            dve.tensor_tensor(out=own, in0=own, in1=ident[:, :], op=ALU.subtract).then_inc(lam_step, 1)
                    if step == (1, 1):
                        z_out(dve, one, SQ_BANK, 0)
                        z_moments(dve, one, 0)
                    if step == (1, 3):
                        z_standard(dve, one, 0)
                    if step == (1, 4):
                        residual(dve, one, 0, 0)
                        z_out(dve, one, SQ_BANK, 1)
                        z_moments(dve, one, 1)
                        z_standard(dve, one, 1)
                    if step == (2, 5):
                        k_lo_out(dve, one, psum[5], 0)
                        q_lo_out(dve, one, psum[6], 0)
                    if step == (2, 4):
                        y_moments(dve, one, 2)

                def trace_out(q):
                    dve.wait_ge(trace_psum, q + 1)
                    dve.tensor_scalar(trace[:, :], SQ_BANK[:, 0:1], TINY, None, ALU.max).then_inc(trace_step, 1)
                    dve.wait_ge(trace_step, 3 * q + 1)
                    dve.reciprocal(trace_inv[:, :], trace[:, :]).then_inc(trace_step, 1)
                    dve.wait_ge(trace_step, 3 * q + 2)
                    at_least(dve, square_ready, NT * q)
                    dve.tensor_tensor(out=trace_inv2[:, :], in0=trace_inv[:, :], in1=trace_inv[:, :],
                                      op=ALU.mult).then_inc(trace_step, 1)

                def trace_parts(q, s):
                    dve.wait_ge(square_ready, NT * (q + 1))
                    dve.tensor_tensor_reduce(diagonal[:, :, :], diagonal_of(Sq[1 - s]).bitcast(F32), ident_tiles, 1.0,
                                             0.0, ALU.mult, ALU.add, trace_part[:, :]).then_inc(trace_part_ready, 1)

                def round_(r, s, half):
                    enters, leaves, squares = within(r, 0, BATCH - 1), within(r, 1, BATCH), within(r, 0, BATCH - 3)
                    q, qs = first_squaring(r, s)
                    early(r, 0)
                    if squares:
                        trace_out(q)
                    if leaves:
                        for nt in range(NT):
                            if nt == 1:
                                early(r, 5)
                            dve.wait_ge(C_psum, NT * (r - 1) + nt + 1)
                            dve.tensor_tensor(out=C2[:, nt, :], in0=psum[nt][:, 2 * D:3 * D], in1=bias[:, nt, 2, :],
                                              op=ALU.add).then_inc(C2_ready, 1)
                    if enters:
                        T_lo(0, r, s)
                        T_lo(1, r, s)
                    early(r, 1)
                    if leaves:
                        for nt in range(NT):
                            dve.wait_ge(Y1_psum, NT * (r - 1) + nt + 1)
                            dve.tensor_tensor(out=Y1[:, nt, :], in0=psum[nt][:, D:2 * D], in1=bias[:, nt, 1, :],
                                              op=ALU.add).then_inc(Y1_ready, 1)
                    if isinstance(r, int) and r == 0:
                        bias_rows_out()
                    if within(r, 0, BATCH - 2):
                        x_moments(r + 1, 1 - s, half + s)
                    early(r, 2)
                    if enters:
                        T_lo(2, r, s)
                    early(r, 3)
                    if within(r, 0, BATCH - 2):
                        x0_lo(r + 1, 1 - s)
                    if isinstance(r, int) and r == 0:
                        bias_and_B_out()
                    if leaves:
                        dve.wait_ge(x_bias_ready, r)
                        for nt in range(NT):
                            dve.wait_ge(Y0_psum, NT * (r - 1) + nt + 1)
                            dve.tensor_tensor(out=y[:, bass.ds((r - 1) * N + nt * D, D)], in0=psum[nt][:, 0:D],
                                              in1=x_bias[:, nt, :], op=ALU.add).then_inc(y_ready, 1)
                    early(r, 4)
                    if squares:
                        trace_parts(q, qs)
                    if squares_again(r):
                        trace_out(q + 1)
                        trace_parts(q + 1, 1)
                def bias_rows_out():
                    dve.wait_ge(rows_psum, 1)
                    dve.tensor_copy(U_rows[:, :], psum[1][0:GROUP, :]).then_inc(rows_ready, 1)
                    dve.tensor_copy(beta_rows[:, :], psum[2][0:GROUP, 0:GROUP * D]).then_inc(rows_ready, 1)

                def bias_and_B_out():
                    dve.wait_ge(B_hi_ready, 1)
                    dve.tensor_tensor(out=B_parts[1][:, :, :, :], in0=B[:, :, :, :],
                                      in1=B_parts[0][:, :, :, :].bitcast(F32), op=ALU.subtract).then_inc(B_lo_ready, 1)
                    for nt in range(NT):
                        dve.wait_ge(bias_psum, nt + 1)
                        dve.tensor_copy(bias[:, nt, :, :].rearrange("p i d -> p (i d)"), psum[nt][:, 0:GROUP * D]
                                        ).then_inc(bias_ready, 1)

                dve.wait_ge(U_psum, 1)
                dve.tensor_copy(U[:, :, 2], psum[6][:, 0:NT]).then_inc(U_ready, 1)
                for n, (whole_power, parts) in enumerate(((PT, PT_parts), (P2T, P2T_parts))):
                    dve.wait_ge(PT_hi_ready, n + 1)
                    dve.wait_ge((P2_psum, P3_psum)[n], NT)
                    dve.tensor_tensor(out=parts[1][:, :, :], in0=whole_power[:, :, :],
                                      in1=parts[0][:, :, :].bitcast(F32), op=ALU.subtract).then_inc(PT_lo_ready, 1)
                    if n == 0:
                        x0_lo(0, 0)
                for c in range(3):
                    cols = min(N, ROWS * D - c * N)
                    dve.wait_ge(one.rows_spread, c + 1)
                    dve.tensor_copy(one.bc_all[:, :, :].rearrange("p r d -> p (r d)")[:, c * N:c * N + cols],
                                    psum[1 + c][:, 0:cols]).then_inc(one.rows_copied, 1)
                rounds(dve, round_, 2, BATCH - 2, BATCH + 1)


AT_X1, AT_X1T, AT_X1T_OUT, AT_K, AT_Q, AT_K_HI, AT_Q_HI, AT_K_LO, AT_Q_LO = 1, 2, 2, 3, 5, 3, 5, 5, 6
AT_V, AT_V_OUT = 14, 14
AT_CONV, AT_CONV_OUT, AT_Z, AT_Z_OUT, AT_Z_MOMENTS, AT_Z_STD = 6, 9, 10, 11, 12, 14
AT_Y_MOMENTS, AT_H = 9, (11, 12, 13, 15)
AT_RINV, AT_SPREAD, AT_SPREAD_OUT, AT_O, AT_PROJ, AT_Z2 = 0, 1, 2, 8, 11, 12
AT_Z2_MOMENTS, AT_Z2_STD = 3, 5
TURN_LAG = 3
VALUES_LAG = 8
DVE_COPIES = (0, 7, 11, 13, 15)
RING = 4
TURNED = 8
STACKS = 4


def copied(by_dve, batch, unit):
    mine = [u for u in range(UNITS) if (u in DVE_COPIES) == by_dve]
    return len(mine) * batch + sum(u <= unit for u in mine)


def layer1(nc, whole, tensor, sem, psum, one, out_dram, y, mask, ident, exponent, waited):
    dve_waited, pool_waited = waited
    x2 = tensor(whole, "x2", [P, BATCH * N])
    bc_all = one.bc_all
    Wos, W1s, W2s, b1s = one.Wos, one.W1s, one.W2s, one.b1s
    x2_now = (one.z, one.z_std)
    x2T = (one.convT, one.x1T)
    gelu = ((flat(one.h[0]), flat(one.h[1])), (flat(one.z_gain), flat(one.z_norm)))
    x2_now_ready, x2T_psum, x2T_ready, hid_psum, gelu_ready, mlp_psum, z3_ready = (
        sem(n) for n in ("x2_now_ready", "x2T_psum", "x2T_ready", "hid_psum", "gelu_ready", "mlp_psum", "z3_ready"))

    def transpose(pe, b, s):
        pe.wait_ge(x2_now_ready, b + 1)
        at_least(pe, x2T_ready, b - 1)
        for t in range(NT):
            last = pe.transpose(psum[s][:, t * P:(t + 1) * P], x2_now[s][:, t, :], ident[:, :])
        last.then_inc(x2T_psum, 1)

    def mlp_products(pe, r, s):
        if within(r, 0, BATCH - 1):
            pe.wait_ge(x2T_ready, r + 1)
            for j in range(HT):
                at_least(pe, gelu_ready, HT * (r - 2) + j + 1)
                pe.matmul(psum[2 + HT * s + j][:, :], W1s[:, j * P:(j + 1) * P], x2T[s][:, :],
                          start=True, stop=True).then_inc(hid_psum, 1)
        if within(r, 0, BATCH - 2):
            transpose(pe, r + 1, 1 - s)
        if within(r, 1, BATCH):
            pe.wait_ge(gelu_ready, HT * r)
            at_least(pe, z3_ready, r - 2)
            for t in range(NT):
                for j in range(HT):
                    last = pe.matmul(psum[7 - s][:, t * D:(t + 1) * D],
                                     gelu[1 - s][j][:, t * P:(t + 1) * P], W2s[:, j, :],
                                     start=j == 0, stop=j == HT - 1)
            last.then_inc(mlp_psum, 1)

    def fetch(act, b, s):
        at_least(act, x2T_psum, b - 1)
        act.activation(flat(x2_now[s]), x2[:, bass.ds(b * N, N)], ACT.Copy).then_inc(x2_now_ready, 1)

    def transposed_out(act, b, s):
        act.wait_ge(x2T_psum, b + 1)
        act.activation(x2T[s][:, :], psum[s][:, :], ACT.Copy).then_inc(x2T_ready, 1)

    def mlp_activations(act, r, s):
        if within(r, 0, BATCH - 1):
            for j in range(HT):
                act.wait_ge(hid_psum, HT * r + j + 1)
                act.activation(gelu[s][j], psum[2 + HT * s + j][:, :], ACT.Gelu,
                               bias=b1s[:, j:j + 1]).then_inc(gelu_ready, 1)
        if within(r, 0, BATCH - 2):
            transposed_out(act, r + 1, 1 - s)
        if within(r, 0, BATCH - 3):
            fetch(act, r + 2, s)

    with ExitStack() as ctx:
        def sb(name, shape, dt=F32):
            return tensor(ctx, name, shape, dt)

        stats_c, mv_c = sb("stats_c", [P, NT, 6]), sb("mv_c", [P, NT, 2])
        ve_c, rstd_c = sb("ve_c", [P, NT]), sb("rstd_c", [P, NT])
        z2_std = sb("z2_std", [P, NT, D])
        one.x1[1], one.v[1] = sb("x1_1", [P, NT, D]), sb("v_1", [P, NT, D])
        x1 = one.x1
        x1_bo = [sb(f"x1_bo{i}", [P, NT, D]) for i in range(2)]
        one.q_stack[1], one.k_stack[1] = (sb(f"{n}_stack1", [P, HEADS, N], F32R) for n in "qk")
        q_stack, k_stack, v = one.q_stack, one.k_stack, one.v
        prob = [sb(f"prob{i}", [P, N]) for i in range(RING)]
        low = sb("low", [P, TURNED])
        probT = [sb(f"probT{i}", [P, NT, P]) for i in range(TURNED)]
        row_sums = [sb(f"row_sums{i}", [P, UNITS]) for i in range(2)]
        sums_inv = sb("sums_inv", [P, UNITS])
        rinv = sb("rinv", [P, UNITS * HD])
        spread = sb("spread", [P, N])
        oT = sb("oT", [P, N])
        z2 = sb("z2", [P, NT, D])
        z2_gain = sb("z2_gain", [P, NT, D])
        L_parts = (sb("L_hi", [P, NT, N], F32R), one.L_lo)
        h_parts = tuple(sb(f"h_{part}", [P, NT, D], F32R) for part in ("hi", "lo"))

        L_hi_ready, L_lo_ready, h_hi_ready, h_lo_ready = (
            sem(n) for n in ("L_hi_ready", "L_lo_ready", "h_hi_ready", "h_lo_ready"))
        z2_std_ready, z2_gain_ready, sums_inv_ready = (
            sem(n) for n in ("z2_std_ready", "z2_gain_ready", "sums_inv_ready"))
        x1_ready, x1_bo_ready, x1T_ready, q_lo_ready, k_lo_ready, v_copied, stacked = (
            one.x1_ready, one.x1_bo_ready, one.x1T_ready, one.q_lo_ready, one.k_lo_ready, one.v_copied, one.stacked)
        scores_psum, masked, exp_done, turned_psum = (
            sem(n) for n in ("scores_psum", "masked", "exp_done", "turned_psum"))
        copied_act, copied_dve = sem("copied_act"), sem("copied_dve")
        o_psum, rinv_ready, spread_psum, spread_ready, oT_ready = (
            sem(n) for n in ("o_psum", "rinv_ready", "spread_psum", "spread_ready", "oT_ready"))
        proj_psum, z2_ready, c_stats, c_mv, c_pool, x2_ready = (
            sem(n) for n in ("proj_psum", "z2_ready", "c_stats", "c_mv", "c_pool", "x2_ready"))

        A_BANK, B_BANK = psum[4], psum[5]
        STACK_DMAS = 2 * STACKS * 16

        def parts(r):
            return within(r, 0, BATCH - 1), within(r, 1, BATCH), within(r, 2, BATCH + 1)

        def copy_wait(eng, batch, unit):
            by_dve = unit in DVE_COPIES
            at_least(eng, copied_dve if by_dve else copied_act, copied(by_dve, batch, unit))

        with nc.Block() as block:

            @block.sync
            def _(sp):
                rounds(sp, lambda b, s, half: stack(sp, one, b, s, half), 2, BATCH, BATCH, first=1)

            @block.gpsimd
            def _(pool):
                def split_h(b, s):
                    pool.wait_ge(one.h_ready, NT * (b + 1))
                    pool.wait_ge(one.conv_psum, b)
                    pool.sem_inc(pool_waited, 1)
                    pool.tensor_copy(h_parts[0][:, :, :], one.h[s][:, :, :]).then_inc(h_hi_ready, 1)
                    pool.wait_ge(h_hi_ready, b - 1)
                    pool.tensor_tensor(out=h_parts[1][:, :, :], in0=one.h[s][:, :, :],
                                       in1=h_parts[0][:, :, :].bitcast(F32), op=ALU.subtract
                                       ).then_inc(h_lo_ready, 1)

                def add_bo(b, s):
                    pool.wait_ge(x1_ready, b + 1)
                    at_least(pool, z2_ready, b - 1)
                    pool.tensor_tensor(out=x1_bo[s][:, :, :], in0=x1[s][:, :, :], in1=all_tiles(one, BO),
                                       op=ALU.add).then_inc(x1_bo_ready, 1)

                def round_(r, s, half):
                    enters, attends, leaves = parts(r)
                    e = r - 3
                    if within(r, 3, BATCH + 2):
                        inverse_root(pool, e, mv_c, c_mv, ve_c, rstd_c, c_pool, z2_std_ready, e, exponent, pool_waited)
                        pool.wait_ge(z2_std_ready, e + 1)
                        pool.tensor_tensor(out=z2_gain[:, :, :], in0=z2_std[:, :, :], in1=all_tiles(one, G2),
                                           op=ALU.mult).then_inc(z2_gain_ready, 1)
                        pool.wait_ge(z2_gain_ready, e + 1)
                        pool.tensor_tensor(out=x2[:, bass.ds(e * N, N)].rearrange("p (t d) -> p t d", d=D),
                                           in0=z2_gain[:, :, :], in1=all_tiles(one, BE2), op=ALU.add
                                           ).then_inc(x2_ready, 1)
                    if within(r, 0, BATCH - 3):
                        h_scales(pool, one, r + 2, s)
                    if enters:
                        add_bo(r, s)
                    if within(r, 0, BATCH - 2):
                        z_root(pool, one, r + 1)
                    if within(r, 0, BATCH - 2):
                        norm_z(pool, one, r + 1)
                    if within(r, 0, BATCH - 3):
                        split_h(r + 2, s)
                add_bo(0, 0)
                split_h(2, 0)
                rounds(pool, round_, 4, BATCH - 2, BATCH + 3, first=1)

            @block.tensor
            def _(pe):
                def scores(a, s, u, half):
                    if u == 0:
                        pe.wait_ge(stacked[s], STACK_DMAS * half)
                    at_least(pe, masked, UNITS * a + u - 1)
                    t, head = divmod(u, HEADS)
                    pe.matmul(psum[u % 2][:, :], q_stack[s][:, head, t * P:(t + 1) * P], k_stack[s][:, head, :],
                              start=True, stop=True).then_inc(scores_psum, 1)

                def turn(batch, u):
                    pe.wait_ge(exp_done, UNITS * batch + u + 1)
                    if isinstance(batch, int) and batch == 0 and u < 2:
                        pass
                    elif u < 2:
                        copy_wait(pe, batch - 1, u - 2 + UNITS)
                    else:
                        copy_wait(pe, batch, u - 2)
                    for mt in range(NT):
                        last = pe.transpose(psum[2 + u % 2][:, mt * P:(mt + 1) * P],
                                            prob[u % RING][:, mt * P:(mt + 1) * P], ident[:, :])
                    last.then_inc(turned_psum, 1)

                def values(batch, s, t, mt):
                    if mt == 0:
                        tile_units = range(HEADS * t, HEADS * (t + 1))
                        for by_dve in (False, True):
                            mine = [u for u in tile_units if (u in DVE_COPIES) == by_dve]
                            if mine:
                                copy_wait(pe, batch, mine[-1])
                        if t == 0:
                            pe.wait_ge(v_copied, batch + 1)
                            at_least(pe, oT_ready, batch - 1)
                            pe.wait_ge(k_lo_ready, min(batch + 2, BATCH) if isinstance(batch, int) else batch + 2)
                    for head in range(HEADS):
                        rows = slice(head * HD, (head + 1) * HD)
                        last = pe.matmul(psum[6 + s][rows, t * P:(t + 1) * P], v[s][:, mt, rows],
                                         probT[(HEADS * t + head) % TURNED][:, mt, :],
                                         start=mt == 0, stop=mt == NT - 1, skip_group_check=True)
                    if mt == NT - 1:
                        last.then_inc(o_psum, 1)

                def round_(r, s, half):
                    enters, attends, leaves = parts(r)
                    a, e = r - 1, r - 2
                    for u in range(UNITS):
                        if u < VALUES_LAG and leaves:
                            values(e, s, (u + UNITS - VALUES_LAG) // HEADS, u % HEADS)
                        if u >= VALUES_LAG and attends:
                            values(a, 1 - s, (u - VALUES_LAG) // HEADS, u % HEADS)
                        if u >= TURN_LAG and attends:
                            turn(a, u - TURN_LAG)
                        if u < TURN_LAG and leaves:
                            turn(e, u - TURN_LAG + UNITS)
                        if u + 1 < UNITS and attends:
                            scores(a, 1 - s, u + 1, half + s)
                        if u + 1 == UNITS and enters:
                            scores(r, s, 0, half + 1)
                        if u == AT_X1T and enters:
                            x1_transpose(pe, one, A_BANK, r, s)
                        if u == AT_SPREAD and leaves:
                            pe.wait_ge(rinv_ready, e + 1)
                            pe.wait_ge(v_copied, min(r, BATCH) if isinstance(r, int) else r)
                            for t in range(NT):
                                last = pe.transpose(B_BANK[:, t * P:(t + 1) * P], rinv[:, t * P:(t + 1) * P],
                                                    ident[:, :])
                            last.then_inc(spread_psum, 1)
                        if u == AT_K and enters:
                            at_least(pe, oT_ready, r - 2)
                            k_product(pe, one, psum[7 - s], r)
                        if u == AT_Q and enters:
                            at_least(pe, v_copied, r)
                            at_least(pe, spread_ready, r - 1)
                            q_product(pe, one, B_BANK, r)
                        if AT_CONV <= u < AT_CONV + NT and within(r, 0, BATCH - 2):
                            if u == AT_CONV:
                                at_least(pe, x1T_ready, r + 1)
                                pe.wait_ge(h_lo_ready, r)
                                pe.wait_ge(L_lo_ready, 1)
                            k = u - AT_CONV
                            for n, (h_part, L_part) in enumerate(products(h_parts, L_parts)):
                                last = pe.matmul(A_BANK[:, :], h_part[:, k, :], L_part[:, k, :],
                                                 start=k == 0 and n == 0, stop=k == NT - 1 and n == 2)
                            if k == NT - 1:
                                last.then_inc(one.conv_psum, 1)
                        if u == AT_PROJ and leaves:
                            pe.wait_ge(oT_ready, e + 1)
                            pe.wait_ge(q_lo_ready,
                                       min(r + 1, BATCH) if isinstance(r, int) else r + 1)
                            for t in range(NT):
                                last = pe.matmul(B_BANK[:, t * D:(t + 1) * D], oT[:, t * P:(t + 1) * P],
                                                 Wos[:, :], start=True, stop=True)
                            last.then_inc(proj_psum, 1)
                        if u == AT_Z and within(r, 0, BATCH - 2):
                            conv_weights(pe, one, A_BANK, r + 1)
                        if u == AT_V and enters:
                            pe.wait_ge(q_lo_ready, r + 1)
                            at_least(pe, z2_ready, r - 1)
                            v_product(pe, one, B_BANK, r)
                scores(0, 0, 0, 1)
                rounds(pe, round_, 2, BATCH - 2, BATCH + 2, first=1)
                pe.wait_ge(masked, UNITS * BATCH)
                pe.wait_ge(one.mlp_loaded, 16 * 3)
                transpose(pe, 0, 0)
                mlp_products(pe, 0, 0)

            @block.scalar
            def _(act):
                def copy_turned(batch, u):
                    act.wait_ge(turned_psum, UNITS * batch + u + 1)
                    act.activation(probT[u % TURNED][:, :, :].rearrange("p t n -> p (t n)"), psum[2 + u % 2][:, :],
                                   ACT.Copy).then_inc(copied_act, 1)

                def round_(r, s, half):
                    enters, attends, leaves = parts(r)
                    a, e = r - 1, r - 2
                    for u in range(UNITS):
                        if attends:
                            if u == 0:
                                at_least(act, rinv_ready, a - 1)
                            act.wait_ge(masked, UNITS * a + u + 1)
                            act.activation(prob[u % RING][:, :], prob[u % RING][:, :], ACT.Exp,
                                           bias=low[:, u % TURNED:u % TURNED + 1], scale=-1.0,
                                           accum_out=row_sums[1 - s][:, u:u + 1]).then_inc(exp_done, 1)
                        x = (u - TURN_LAG) % UNITS
                        if x not in DVE_COPIES:
                            if u < TURN_LAG and leaves:
                                copy_turned(e, x)
                            if u >= TURN_LAG and attends:
                                copy_turned(a, x)
                        if u == AT_X1T_OUT and enters:
                            x1T_out(act, one, A_BANK, r)
                        if u == AT_K_HI and enters:
                            k_hi_out(act, one, psum[7 - s], r, s, half)
                        if u == AT_Q_HI and enters:
                            q_hi_out(act, one, B_BANK, r, s, half)
                        if u in AT_H and within(r, 0, BATCH - 3):
                            normalise(act, one, r + 2, s, AT_H.index(u))
                        if u == AT_V_OUT and enters:
                            v_out(act, one, B_BANK, r, s)
                        if u == AT_SPREAD_OUT and leaves:
                            act.wait_ge(spread_psum, e + 1)
                            at_least(act, oT_ready, e)
                            act.activation(spread[:, :], B_BANK[:, :], ACT.Copy).then_inc(spread_ready, 1)
                        if u == AT_CONV_OUT and within(r, 0, BATCH - 2):
                            conv_out(act, one, A_BANK, r + 1)
                act.activation(L_parts[0][:, :, :], one.Lnorm[:, :, :], ACT.Copy).then_inc(L_hi_ready, 1)
                rounds(act, round_, 2, BATCH - 2, BATCH + 2, first=1)
                act.wait_ge(x2_ready, 3)
                fetch(act, 0, 0)
                fetch(act, 1, 1)
                transposed_out(act, 0, 0)
                mlp_activations(act, 0, 0)

            @block.vector
            def _(dve):
                def copy_turned(batch, u):
                    dve.wait_ge(turned_psum, UNITS * batch + u + 1)
                    dve.tensor_copy(probT[u % TURNED][:, :, :].rearrange("p t n -> p (t n)"),
                                    psum[2 + u % 2][:, :]).then_inc(copied_dve, 1)

                def round_(r, s, half):
                    enters, attends, leaves = parts(r)
                    a, e = r - 1, r - 2
                    finishes = within(r, 3, BATCH + 2)
                    for u in range(UNITS):
                        if attends:
                            dve.wait_ge(scores_psum, UNITS * a + u + 1)
                            at_least(dve, turned_psum, UNITS * a + u + 1 - RING)
                            dve.sem_inc(dve_waited, 1)
                            dve.tensor_tensor_reduce(prob[u % RING][:, :], psum[u % 2][:, :],
                                                     mask[:, u // HEADS, :], 1.0, 3e38, ALU.add, ALU.min,
                                                     low[:, u % TURNED:u % TURNED + 1]).then_inc(masked, 1)
                        x = (u - TURN_LAG) % UNITS
                        if x in DVE_COPIES:
                            if u < TURN_LAG and leaves:
                                copy_turned(e, x)
                            if u >= TURN_LAG and attends:
                                copy_turned(a, x)
                        if u == AT_X1 and enters:
                            residual(dve, one, r, s)
                        if u == AT_Y_MOMENTS and within(r, 0, BATCH - 3):
                            y_moments(dve, one, r + 2)
                        if u == AT_RINV and leaves:
                            dve.wait_ge(exp_done, UNITS * (e + 1))
                            at_least(dve, spread_psum, e)
                            dve.reciprocal(sums_inv[:, :], row_sums[s][:, :]).then_inc(sums_inv_ready, 1)
                            dve.wait_ge(sums_inv_ready, e + 1)
                            dve.tensor_copy(rinv[:, :].rearrange("p (u d) -> p u d", d=HD),
                                            sums_inv[:, :].unsqueeze(2).broadcast_to([P, UNITS, HD])
                                            ).then_inc(rinv_ready, 1)
                        if u == AT_K_LO and enters:
                            k_lo_out(dve, one, psum[7 - s], r)
                        if u == AT_Q_LO and enters:
                            q_lo_out(dve, one, B_BANK, r)
                        if u == AT_O and leaves:
                            dve.wait_ge(o_psum, NT * (e + 1))
                            dve.wait_ge(spread_ready, e + 1)
                            at_least(dve, proj_psum, e)
                            dve.tensor_tensor(out=oT[:, :], in0=psum[6 + s][:, :], in1=spread[:, :],
                                              op=ALU.mult).then_inc(oT_ready, 1)
                        if u == AT_Z_OUT and within(r, 0, BATCH - 2):
                            z_out(dve, one, A_BANK, r + 1)
                        if u == AT_Z2 and leaves:
                            dve.wait_ge(proj_psum, e + 1)
                            dve.wait_ge(x1_bo_ready, e + 1)
                            at_least(dve, z2_std_ready, e)
                            dve.tensor_tensor(out=flat(z2), in0=B_BANK[:, :], in1=flat(x1_bo[s]),
                                              op=ALU.add).then_inc(z2_ready, 1)
                        if u == AT_Z_MOMENTS and within(r, 0, BATCH - 2):
                            z_moments(dve, one, r + 1)
                        if u == AT_Z2_MOMENTS and finishes:
                            f = r - 3
                            dve.wait_ge(z2_ready, f + 1)
                            moments(dve, f, lambda t: z2[:, t, :], stats_c, c_stats, mv_c, c_mv, z2_std_ready, f,
                                    dve_waited)
                        if u == AT_Z_STD and within(r, 0, BATCH - 2):
                            z_standard(dve, one, r + 1)
                        if u == AT_Z2_STD and finishes:
                            dve.wait_ge(c_pool, 2 * f + 2)
                            at_least(dve, z2_gain_ready, f)
                            standardise(dve, z2_std, z2, mv_c, rstd_c, z2_std_ready)
                dve.wait_ge(L_hi_ready, 1)
                dve.tensor_tensor(out=L_parts[1][:, :, :], in0=one.Lnorm[:, :, :],
                                  in1=L_parts[0][:, :, :].bitcast(F32), op=ALU.subtract).then_inc(L_lo_ready, 1)
                rounds(dve, round_, 4, BATCH - 2, BATCH + 3, first=1)

    with ExitStack() as ctx:
        def sb(name, shape, dt=F32):
            return tensor(ctx, name, shape, dt)

        x2_b2 = [sb(f"x2_b2{i}", [P, NT, D]) for i in range(2)]
        y_be3 = [sb(f"y_be3{i}", [P, NT, D]) for i in range(2)]
        z3 = [sb(f"z3_{i}", [P, NT, D]) for i in range(2)]
        z3_gain = [sb(f"z3_gain{i}", [P, NT, D]) for i in range(2)]
        result = [sb(f"result{i}", [P, NT, D]) for i in range(2)]
        stats3 = sb("stats3", [P, NT, 6])
        mv3 = [sb(f"mv3{i}", [P, NT, 2]) for i in range(2)]
        ve3 = sb("ve3", [P, NT])
        rstd3 = [sb(f"rstd3{i}", [P, NT]) for i in range(2)]

        x2_b2_ready, y_be3_ready, stats3_ready, mv3_ready, pool3, z3_step, result_ready = (
            sem(n) for n in ("x2_b2_ready", "y_be3_ready", "stats3_ready", "mv3_ready", "pool3", "z3_step",
                             "result_ready"))
        stored = [sem(f"stored{i}") for i in range(2)]

        with nc.Block() as block:

            @block.sync
            def _(sp):
                def store(b, s, half):
                    sp.wait_ge(result_ready, b + 1)
                    sp.dma_start(out_dram[:, bass.ds(b, 1), :, :].rearrange("p b t d -> p (b t) d"),
                                 result[s][:, :, :]).then_inc(stored[s], 16)
                rounds(sp, store, 2, BATCH, BATCH)
                for s in range(2):
                    sp.wait_ge(stored[s], 16 * (BATCH // 2))

            @block.gpsimd
            def _(pool):
                def tiles(t, b):
                    return t[:, bass.ds(b * N, N)].rearrange("p (t d) -> p t d", d=D)

                def round_(r, s, half):
                    if within(r, 0, BATCH - 1):
                        at_least(pool, z3_ready, r - 1)
                        pool.tensor_tensor(out=x2_b2[s][:, :, :], in0=tiles(x2, r), in1=all_tiles(one, B2),
                                           op=ALU.add).then_inc(x2_b2_ready, 1)
                    if within(r, 1, BATCH):
                        b = r - 1
                        inverse_root(pool, b, mv3[1 - s], mv3_ready, ve3, rstd3[1 - s], pool3, result_ready, b - 1,
                                     exponent, pool_waited)
                        pool.tensor_tensor(out=y_be3[1 - s][:, :, :], in0=tiles(y, b), in1=all_tiles(one, BE3),
                                           op=ALU.add).then_inc(y_be3_ready, 1)
                rounds(pool, round_, 2, BATCH, BATCH + 1)

            @block.tensor
            def _(pe):
                rounds(pe, lambda r, s, half: mlp_products(pe, r, s), 2, BATCH - 2, BATCH + 1, first=1)

            @block.scalar
            def _(act):
                rounds(act, lambda r, s, half: mlp_activations(act, r, s), 2, BATCH - 2, BATCH, first=1)

            @block.vector
            def _(dve):
                def round_(r, s, half):
                    if within(r, 1, BATCH):
                        b = r - 1
                        dve.wait_ge(mlp_psum, b + 1)
                        dve.wait_ge(x2_b2_ready, b + 1)
                        dve.tensor_tensor(out=flat(z3[1 - s]), in0=psum[7 - s][:, :], in1=flat(x2_b2[1 - s]),
                                          op=ALU.add).then_inc(z3_ready, 1)
                        dve.wait_ge(z3_ready, b + 1)
                        at_least(dve, mv3_ready, b)
                        for t in range(NT):
                            last = dve.bn_stats(stats3[:, t, :], z3[1 - s][:, t, :])
                        last.then_inc(stats3_ready, 1)
                        dve.wait_ge(stats3_ready, b + 1)
                        at_least(dve, result_ready, b - 1)
                        dve.sem_inc(dve_waited, 1)
                        for t in range(NT):
                            last = dve.bn_aggr(mv3[1 - s][:, t, :], stats3[:, t, :])
                        last.then_inc(mv3_ready, 1)
                    if within(r, 2, BATCH + 1):
                        b = r - 2
                        at_least(dve, result_ready, b - 1)
                        dve.wait_ge(pool3, 2 * b + 2)
                        dve.wait_ge(y_be3_ready, b + 1)
                        for t in range(NT):
                            last = dve.scalar_tensor_tensor(out=z3_gain[s][:, t, :], in0=z3[s][:, t, :],
                                                            scalar=mv3[s][:, t, 0:1], in1=bc_all[:, G3, :],
                                                            op0=ALU.subtract, op1=ALU.mult)
                        last.then_inc(z3_step, 1)
                        dve.wait_ge(z3_step, b + 1)
                        if isinstance(r, int):
                            if b >= 2:
                                dve.wait_ge(stored[s], 16 * (b // 2))
                        else:
                            at_least(dve, stored[s], 16 * (half - 1))
                        for t in range(NT):
                            last = dve.scalar_tensor_tensor(out=result[s][:, t, :], in0=z3_gain[s][:, t, :],
                                                            scalar=rstd3[s][:, t:t + 1], in1=y_be3[s][:, t, :],
                                                            op0=ALU.mult, op1=ALU.add)
                        last.then_inc(result_ready, 1)
                rounds(dve, round_, 4, BATCH, BATCH + 2)


_INS = ["x", "adj", "L0_gnn_alpha_train", "L0_gnn_w", "L0_gnn_d", "L0_gnn_fc_in_w", "L0_gnn_fc_in_b",
        "L1_gnn_Wc", "L1_gnn_bc", "L1_gnn_g1", "L1_gnn_be1", "L1_gnn_Wq", "L1_gnn_Wk", "L1_gnn_Wv", "L1_gnn_Wo",
        "L1_gnn_bo", "L1_gnn_g2", "L1_gnn_be2", "L1_gnn_W1", "L1_gnn_b1", "L1_gnn_W2", "L1_gnn_b2", "L1_gnn_g3",
        "L1_gnn_be3"]


def kernel(**inputs):
    import numpy as _np
    import concourse.bacc as _bacc
    from concourse import mybir as _mybir
    from concourse.bass_utils import run_bass_kernel_spmd as _run

    nc = _bacc.Bacc("TRN2", target_bir_lowering=False, num_devices=1)
    arrays, args = {}, []
    for name in _INS:
        a = _np.ascontiguousarray(inputs[name])
        arrays[f"in_{name}_dram"] = a
        args.append(nc.dram_tensor(f"in_{name}_dram", a.shape, _mybir.dt.from_np(a.dtype), kind="ExternalInput").ap())
    args.append(nc.dram_tensor("out_dram", (BATCH, N, D), _mybir.dt.float32, kind="ExternalOutput").ap())
    two_layers(nc, *args)
    return _run(nc, [arrays], core_ids=[0]).results[0]["out_dram"]
```
